# Optimizing a Trainium2 kernel written in Bass

```python
import numpy as np
import jax
import jax.numpy as jnp

def _softmax(x, axis=-1):
    return jax.nn.softmax(x, axis=axis)

def _gelu(x):
    return jax.nn.gelu(x, approximate=True)

def _silu(x):
    return jax.nn.silu(x)

def _sigmoid(x):
    return jax.nn.sigmoid(x)

def _layernorm(x, axis=-1, eps=1e-05):
    m = jnp.mean(x, axis=axis, keepdims=True)
    v = jnp.var(x, axis=axis, keepdims=True)
    return (x - m) / jnp.sqrt(v + eps)

def _scatter_add(tgt, idx, src, axis=0):
    return tgt.at[idx].add(src)

def _segment_sum(src, seg, n):
    return jax.ops.segment_sum(src, seg, n)
kernel_name = 'mk_adaln_d2_jaxref_r8_4f40ed'

def setup_inputs(seed: int=0):
    np.random.seed(seed)
    _w = jnp.asarray

    def _L0_attn_setup():
        import jax, jax.numpy as jnp
        import numpy as np
        N_HEAD = 16
        EPS = 1e-06

        def _linear_attention(q, k, v):
            B, H, D = (q.shape[1], q.shape[2], q.shape[3])

            def step(carry, qkv_t):
                S, z = carry
                qt, kt, vt = qkv_t
                S = S + kt[..., :, None] * vt[..., None, :]
                z = z + kt
                num = jnp.einsum('bhi,bhij->bhj', qt, S)
                den = jnp.sum(qt * z, axis=-1, keepdims=True)
                return ((S, z), num / (den + EPS))
            S0 = jnp.zeros((B, H, D, D), q.dtype)
            z0 = jnp.zeros((B, H, D), q.dtype)
            _, y = jax.lax.scan(step, (S0, z0), (q, k, v))
            return y
        key = jax.random.key(seed)
        k1, k2, k3 = jax.random.split(key, 3)
        B, T, C = (2, 256, 128)
        x = jax.random.normal(k1, (B, T, C), dtype=jnp.float32)
        w_attn = jax.random.normal(k2, (C, 3 * C), dtype=jnp.float32) * 0.02
        w_proj = jax.random.normal(k3, (C, C), dtype=jnp.float32) * 0.02
        return {'x': x, 'w_attn': w_attn, 'w_proj': w_proj}
    _L0_attn_in = _L0_attn_setup()

    def _L0_ffn_setup():
        import jax, jax.numpy as jnp
        import numpy as np
        DIM = 128

        def _reference_tuple_inner(x, W_r, W_k, W_v, mu_r, mu_k):
            B, T, C = x.shape
            x_prev = jnp.concatenate([jnp.zeros((B, 1, C), x.dtype), x[:, :-1, :]], axis=1)
            xr = mu_r * x + (1.0 - mu_r) * x_prev
            xk = mu_k * x + (1.0 - mu_k) * x_prev
            r = jax.nn.sigmoid(jnp.einsum('btc,dc->btd', xr, W_r))
            k = jnp.einsum('btc,dc->btd', xk, W_k)
            k_act = jnp.square(jax.nn.relu(k))
            out = r * jnp.einsum('btc,dc->btd', k_act, W_v)
            new_state = x[:, -1, :]
            return (out, new_state)
        key = jax.random.key(seed)
        ks = jax.random.split(key, 6)
        B, T, C = (8, 256, DIM)
        x = jax.random.normal(ks[0], (B, T, C), dtype=jnp.float32)
        s = 1.0 / np.sqrt(C)
        W_r = jax.random.uniform(ks[1], (C, C), jnp.float32, -s, s)
        W_k = jax.random.uniform(ks[2], (C, C), jnp.float32, -s, s)
        W_v = jax.random.uniform(ks[3], (C, C), jnp.float32, -s, s)
        mu_r = jax.random.uniform(ks[4], (C,), jnp.float32)
        mu_k = jax.random.uniform(ks[5], (C,), jnp.float32)
        return {'x': x, 'W_r': W_r, 'W_k': W_k, 'W_v': W_v, 'mu_r': mu_r, 'mu_k': mu_k}
    _L0_ffn_in = _L0_ffn_setup()
    _L0_c = _w((lambda *s: np.random.randn(*s).astype(np.float32) * 0.05)(16, 128))
    _L0_wmod = _w((lambda *s: np.random.randn(*s).astype(np.float32) * 0.05)(128, 6 * 128) * 128 ** (-0.5))

    def _L1_attn_setup():
        import jax, jax.numpy as jnp
        import numpy as np
        EMBED_DIM = 128
        NUM_HEADS = 16
        HEAD_DIM = EMBED_DIM // NUM_HEADS
        SCALING = HEAD_DIM ** (-0.5)
        EPS = 1e-05

        def _rope(seq_len):
            inv_freq = 1.0 / 10000.0 ** (jnp.arange(0, HEAD_DIM, 2, dtype=jnp.float32) / HEAD_DIM)
            freqs = jnp.arange(seq_len, dtype=jnp.float32)[:, None] * inv_freq[None, :]
            emb = jnp.concatenate([freqs, freqs], axis=-1)
            return (jnp.cos(emb), jnp.sin(emb))

        def _rotate(x, cos, sin):
            d = x.shape[-1]
            x1, x2 = (x[..., :d // 2], x[..., d // 2:])
            rotated = jnp.concatenate([-x2, x1], axis=-1)
            return x * cos + rotated * sin
        key = jax.random.key(seed)
        ks = jax.random.split(key, 6)
        B, S, D = (2, 256, EMBED_DIM)
        scale = D ** (-0.5)
        return {'x': jax.random.normal(ks[0], (B, S, D), jnp.float32), 'Wq': jax.random.normal(ks[1], (D, D), jnp.float32) * scale, 'Wk': jax.random.normal(ks[2], (D, D), jnp.float32) * scale, 'Wv': jax.random.normal(ks[3], (D, D), jnp.float32) * scale, 'Wg': jax.random.normal(ks[4], (D, D), jnp.float32) * scale, 'Wo': jax.random.normal(ks[5], (D, D), jnp.float32) * scale, 'gn_w': jnp.ones((D,), jnp.float32), 'gn_b': jnp.zeros((D,), jnp.float32)}
    _L1_attn_in = _L1_attn_setup()

    def _L1_ffn_setup():
        import jax, jax.numpy as jnp
        import numpy as np
        D = 128
        H = 4
        DF = 512
        E = 8
        EPS = 1e-05

        def _layer_norm(x, g, b):
            mu = jnp.mean(x, axis=-1, keepdims=True)
            var = jnp.mean(jnp.square(x - mu), axis=-1, keepdims=True)
            return (x - mu) * jax.lax.rsqrt(var + EPS) * g + b

        def _mha(x, Wqkv, bqkv, Wo, bo):
            S, B, _ = x.shape
            hd = D // H
            qkv = x @ Wqkv.T + bqkv
            q, k, v = jnp.split(qkv, 3, axis=-1)
            to_heads = lambda t: t.reshape(S, B, H, hd).transpose(1, 2, 0, 3)
            q, k, v = (to_heads(q), to_heads(k), to_heads(v))
            scores = jnp.einsum('bhqd,bhkd->bhqk', q, k) * (1.0 / np.sqrt(hd))
            att = jax.nn.softmax(scores, axis=-1)
            o = jnp.einsum('bhqk,bhkd->bhqd', att, v)
            o = o.transpose(2, 0, 1, 3).reshape(S, B, D)
            return o @ Wo.T + bo

        def _moe(x, Wg, W1, b1, W2, b2):
            S, B, _ = x.shape
            xf = x.reshape(S * B, D)
            logits = xf @ Wg.T
            idx = jnp.argmax(logits, axis=-1)
            out = jnp.zeros_like(xf)
            for e in range(E):
                m = (idx == e)[:, None].astype(xf.dtype)
                h = jax.nn.relu(xf @ W1[e] + b1[e])
                out = out + m * (h @ W2[e] + b2[e])
            return out.reshape(S, B, D)
        key = jax.random.key(seed)
        ks = jax.random.split(key, 16)
        S, B = (64, 8)
        s = lambda k, shape, fan: jax.random.normal(k, shape, jnp.float32) * (1.0 / np.sqrt(fan))
        return {'x': jax.random.normal(ks[0], (S, B, D), jnp.float32), 'Wqkv': s(ks[1], (3 * D, D), D), 'bqkv': jnp.zeros((3 * D,), jnp.float32), 'Wo': s(ks[2], (D, D), D), 'bo': jnp.zeros((D,), jnp.float32), 'g1': jnp.ones((D,), jnp.float32), 'be1': jnp.zeros((D,), jnp.float32), 'g2': jnp.ones((D,), jnp.float32), 'be2': jnp.zeros((D,), jnp.float32), 'Wg': s(ks[3], (E, D), D), 'W1': s(ks[4], (E, D, DF), D), 'b1': jnp.zeros((E, DF), jnp.float32), 'W2': s(ks[5], (E, DF, D), DF), 'b2': jnp.zeros((E, D), jnp.float32)}
    _L1_ffn_in = _L1_ffn_setup()
    _L1_c = _w((lambda *s: np.random.randn(*s).astype(np.float32) * 0.05)(16, 128))
    _L1_wmod = _w((lambda *s: np.random.randn(*s).astype(np.float32) * 0.05)(128, 6 * 128) * 128 ** (-0.5))
    _d = {'L0_attn_x': _L0_attn_in['x'], 'L0_attn_w_attn': _L0_attn_in['w_attn'], 'L0_attn_w_proj': _L0_attn_in['w_proj'], 'L0_ffn_W_r': _L0_ffn_in['W_r'], 'L0_ffn_W_k': _L0_ffn_in['W_k'], 'L0_ffn_W_v': _L0_ffn_in['W_v'], 'L0_ffn_mu_r': _L0_ffn_in['mu_r'], 'L0_ffn_mu_k': _L0_ffn_in['mu_k'], 'L0_c': _L0_c, 'L0_wmod': _L0_wmod, 'L1_attn_Wq': _L1_attn_in['Wq'], 'L1_attn_Wk': _L1_attn_in['Wk'], 'L1_attn_Wv': _L1_attn_in['Wv'], 'L1_attn_Wg': _L1_attn_in['Wg'], 'L1_attn_Wo': _L1_attn_in['Wo'], 'L1_attn_gn_w': _L1_attn_in['gn_w'], 'L1_attn_gn_b': _L1_attn_in['gn_b'], 'L1_ffn_Wqkv': _L1_ffn_in['Wqkv'], 'L1_ffn_bqkv': _L1_ffn_in['bqkv'], 'L1_ffn_Wo': _L1_ffn_in['Wo'], 'L1_ffn_bo': _L1_ffn_in['bo'], 'L1_ffn_g1': _L1_ffn_in['g1'], 'L1_ffn_be1': _L1_ffn_in['be1'], 'L1_ffn_g2': _L1_ffn_in['g2'], 'L1_ffn_be2': _L1_ffn_in['be2'], 'L1_ffn_Wg': _L1_ffn_in['Wg'], 'L1_ffn_W1': _L1_ffn_in['W1'], 'L1_ffn_b1': _L1_ffn_in['b1'], 'L1_ffn_W2': _L1_ffn_in['W2'], 'L1_ffn_b2': _L1_ffn_in['b2'], 'L1_c': _L1_c, 'L1_wmod': _L1_wmod}
    _x0 = _d['L0_attn_x']
    _d['L0_attn_x'] = jax.random.normal(jax.random.fold_in(jax.random.key(seed), 1), (16, 512, 128), dtype=_x0.dtype)
    del _x0
    return _d

def reference(L0_attn_x, L0_attn_w_attn, L0_attn_w_proj, L0_ffn_W_r, L0_ffn_W_k, L0_ffn_W_v, L0_ffn_mu_r, L0_ffn_mu_k, L0_c, L0_wmod, L1_attn_Wq, L1_attn_Wk, L1_attn_Wv, L1_attn_Wg, L1_attn_Wo, L1_attn_gn_w, L1_attn_gn_b, L1_ffn_Wqkv, L1_ffn_bqkv, L1_ffn_Wo, L1_ffn_bo, L1_ffn_g1, L1_ffn_be1, L1_ffn_g2, L1_ffn_be2, L1_ffn_Wg, L1_ffn_W1, L1_ffn_b1, L1_ffn_W2, L1_ffn_b2, L1_c, L1_wmod):

    def _L0_attn_ref(x, w_attn, w_proj):
        import jax, jax.numpy as jnp
        import numpy as np
        N_HEAD = 16
        EPS = 1e-06

        def _linear_attention(q, k, v):
            B, H, D = (q.shape[1], q.shape[2], q.shape[3])

            def step(carry, qkv_t):
                S, z = carry
                qt, kt, vt = qkv_t
                S = S + kt[..., :, None] * vt[..., None, :]
                z = z + kt
                num = jnp.einsum('bhi,bhij->bhj', qt, S)
                den = jnp.sum(qt * z, axis=-1, keepdims=True)
                return ((S, z), num / (den + EPS))
            S0 = jnp.zeros((B, H, D, D), q.dtype)
            z0 = jnp.zeros((B, H, D), q.dtype)
            _, y = jax.lax.scan(step, (S0, z0), (q, k, v))
            return y
        B, T, C = x.shape
        H = N_HEAD
        D = C // H
        qkv = x @ w_attn
        q, k, v = jnp.split(qkv, 3, axis=-1)

        def to_tbhd(a):
            return a.reshape(B, T, H, D).transpose(1, 0, 2, 3)
        q = jax.nn.elu(to_tbhd(q)) + 1.0
        k = jax.nn.elu(to_tbhd(k)) + 1.0
        v = to_tbhd(v)
        y = _linear_attention(q, k, v)
        y = y.transpose(1, 0, 2, 3).reshape(B, T, C)
        return y @ w_proj

    def _L0_ffn_ref(x, W_r, W_k, W_v, mu_r, mu_k):
        import jax, jax.numpy as jnp
        import numpy as np
        DIM = 128

        def _reference_tuple_inner(x, W_r, W_k, W_v, mu_r, mu_k):
            B, T, C = x.shape
            x_prev = jnp.concatenate([jnp.zeros((B, 1, C), x.dtype), x[:, :-1, :]], axis=1)
            xr = mu_r * x + (1.0 - mu_r) * x_prev
            xk = mu_k * x + (1.0 - mu_k) * x_prev
            r = jax.nn.sigmoid(jnp.einsum('btc,dc->btd', xr, W_r))
            k = jnp.einsum('btc,dc->btd', xk, W_k)
            k_act = jnp.square(jax.nn.relu(k))
            out = r * jnp.einsum('btc,dc->btd', k_act, W_v)
            new_state = x[:, -1, :]
            return (out, new_state)
        return _reference_tuple_inner(x, W_r, W_k, W_v, mu_r, mu_k)[0]

    def _L1_attn_ref(x, Wq, Wk, Wv, Wg, Wo, gn_w, gn_b):
        import jax, jax.numpy as jnp
        import numpy as np
        EMBED_DIM = 128
        NUM_HEADS = 16
        HEAD_DIM = EMBED_DIM // NUM_HEADS
        SCALING = HEAD_DIM ** (-0.5)
        EPS = 1e-05

        def _rope(seq_len):
            inv_freq = 1.0 / 10000.0 ** (jnp.arange(0, HEAD_DIM, 2, dtype=jnp.float32) / HEAD_DIM)
            freqs = jnp.arange(seq_len, dtype=jnp.float32)[:, None] * inv_freq[None, :]
            emb = jnp.concatenate([freqs, freqs], axis=-1)
            return (jnp.cos(emb), jnp.sin(emb))

        def _rotate(x, cos, sin):
            d = x.shape[-1]
            x1, x2 = (x[..., :d // 2], x[..., d // 2:])
            rotated = jnp.concatenate([-x2, x1], axis=-1)
            return x * cos + rotated * sin
        B, S, D = x.shape
        H, Dh = (NUM_HEADS, HEAD_DIM)

        def split_heads(t):
            return t.reshape(B, S, H, Dh).transpose(0, 2, 1, 3)
        q = split_heads(x @ Wq.T)
        k = split_heads(x @ Wk.T)
        v = split_heads(x @ Wv.T)
        cos, sin = _rope(S)
        q = _rotate(q, cos, sin)
        k = _rotate(k, cos, sin)
        retention = jnp.einsum('bhsd,bhtd->bhst', q, k) * SCALING
        gammas = 1.0 - 2.0 ** (-5.0 - jnp.arange(H, dtype=jnp.float32))
        diff = jnp.arange(S)[:, None] - jnp.arange(S)[None, :]
        causal = diff >= 0
        decay = jnp.where(causal, gammas[:, None, None] ** jnp.maximum(diff, 0).astype(jnp.float32), 0.0)
        retention = retention * decay[None]
        out = jnp.einsum('bhst,bhtd->bhsd', retention, v)
        out = out.transpose(0, 2, 1, 3).reshape(B * S, H, Dh)
        mean = out.mean(axis=-1, keepdims=True)
        var = out.var(axis=-1, keepdims=True)
        out = (out - mean) * jax.lax.rsqrt(var + EPS)
        out = out * gn_w.reshape(H, Dh) + gn_b.reshape(H, Dh)
        out = out.reshape(B, S, D)
        gate = jax.nn.silu(x @ Wg.T)
        return gate * out @ Wo.T

    def _L1_ffn_ref(x, Wqkv, bqkv, Wo, bo, g1, be1, g2, be2, Wg, W1, b1, W2, b2):
        import jax, jax.numpy as jnp
        import numpy as np
        D = 128
        H = 4
        DF = 512
        E = 8
        EPS = 1e-05

        def _layer_norm(x, g, b):
            mu = jnp.mean(x, axis=-1, keepdims=True)
            var = jnp.mean(jnp.square(x - mu), axis=-1, keepdims=True)
            return (x - mu) * jax.lax.rsqrt(var + EPS) * g + b

        def _mha(x, Wqkv, bqkv, Wo, bo):
            S, B, _ = x.shape
            hd = D // H
            qkv = x @ Wqkv.T + bqkv
            q, k, v = jnp.split(qkv, 3, axis=-1)
            to_heads = lambda t: t.reshape(S, B, H, hd).transpose(1, 2, 0, 3)
            q, k, v = (to_heads(q), to_heads(k), to_heads(v))
            scores = jnp.einsum('bhqd,bhkd->bhqk', q, k) * (1.0 / np.sqrt(hd))
            att = jax.nn.softmax(scores, axis=-1)
            o = jnp.einsum('bhqk,bhkd->bhqd', att, v)
            o = o.transpose(2, 0, 1, 3).reshape(S, B, D)
            return o @ Wo.T + bo

        def _moe(x, Wg, W1, b1, W2, b2):
            S, B, _ = x.shape
            xf = x.reshape(S * B, D)
            logits = xf @ Wg.T
            idx = jnp.argmax(logits, axis=-1)
            out = jnp.zeros_like(xf)
            for e in range(E):
                m = (idx == e)[:, None].astype(xf.dtype)
                h = jax.nn.relu(xf @ W1[e] + b1[e])
                out = out + m * (h @ W2[e] + b2[e])
            return out.reshape(S, B, D)
        y = _layer_norm(x + _mha(x, Wqkv, bqkv, Wo, bo), g1, be1)
        z = _layer_norm(y + _moe(y, Wg, W1, b1, W2, b2), g2, be2)
        return z
    x = L0_attn_x
    mod = (_silu(L0_c) @ L0_wmod).reshape(L0_c.shape[0], 6, 1, -1)
    sa, ca, ga, sb, cb, gb = (mod[:, 0], mod[:, 1], mod[:, 2], mod[:, 3], mod[:, 4], mod[:, 5])
    ga = (2 * (ga >= 0) - 1) * jnp.maximum(jnp.abs(ga), 0.25)
    gb = (2 * (gb >= 0) - 1) * jnp.maximum(jnp.abs(gb), 0.25)
    h = _layernorm(x, axis=-1) * (1 + ca) + sa
    x = x + ga * _L0_attn_ref(h, L0_attn_w_attn, L0_attn_w_proj)
    h = _layernorm(x, axis=-1) * (1 + cb) + sb
    x = x + gb * _L0_ffn_ref(h, L0_ffn_W_r, L0_ffn_W_k, L0_ffn_W_v, L0_ffn_mu_r, L0_ffn_mu_k)
    mod = (_silu(L1_c) @ L1_wmod).reshape(L1_c.shape[0], 6, 1, -1)
    sa, ca, ga, sb, cb, gb = (mod[:, 0], mod[:, 1], mod[:, 2], mod[:, 3], mod[:, 4], mod[:, 5])
    ga = (2 * (ga >= 0) - 1) * jnp.maximum(jnp.abs(ga), 0.25)
    gb = (2 * (gb >= 0) - 1) * jnp.maximum(jnp.abs(gb), 0.25)
    h = _layernorm(x, axis=-1) * (1 + ca) + sa
    x = x + ga * _L1_attn_ref(h, L1_attn_Wq, L1_attn_Wk, L1_attn_Wv, L1_attn_Wg, L1_attn_Wo, L1_attn_gn_w, L1_attn_gn_b)
    h = _layernorm(x, axis=-1) * (1 + cb) + sb
    x = x + gb * _L1_ffn_ref(h, L1_ffn_Wqkv, L1_ffn_bqkv, L1_ffn_Wo, L1_ffn_bo, L1_ffn_g1, L1_ffn_be1, L1_ffn_g2, L1_ffn_be2, L1_ffn_Wg, L1_ffn_W1, L1_ffn_b1, L1_ffn_W2, L1_ffn_b2)
    return x

_drawn_inputs = setup_inputs


def setup_inputs(seed=0):
    import zlib

    import numpy as np

    out = dict(_drawn_inputs(seed))
    spreads = {'L1_attn_gn_w': (1.0, 0.2),
     'L1_attn_gn_b': (0.0, 0.339),
     'L1_ffn_bqkv': (0.0, 0.1),
     'L1_ffn_bo': (0.0, 0.1),
     'L1_ffn_g1': (1.0, 0.2),
     'L1_ffn_be1': (0.0, 0.1),
     'L1_ffn_g2': (1.0, 0.2),
     'L1_ffn_be2': (0.0, 0.366),
     'L1_ffn_b1': (0.0, 0.587),
     'L1_ffn_b2': (0.0, 0.414)}
    factors = {'L0_attn_w_attn': 8.0,
     'L0_attn_w_proj': 8.0,
     'L0_ffn_W_r': 4.945,
     'L0_ffn_mu_r': 7.426,
     'L0_ffn_mu_k': 2.705}
    for name, (base, spread) in spreads.items():
        noise = np.random.default_rng([zlib.crc32(name.encode()), seed]).standard_normal(out[name].shape)
        drawn = base * np.exp(spread * noise) if base else spread * noise
        out[name] = jnp.asarray(drawn.astype(out[name].dtype))
    for name, factor in factors.items():
        out[name] = (out[name] * factor).astype(out[name].dtype)
    return out
```

```python
from contextlib import ExitStack

import concourse.bass as bass
from concourse import mybir

F32 = mybir.dt.float32
I32 = mybir.dt.int32
U32 = mybir.dt.uint32
ALU = mybir.AluOpType
ACT = mybir.ActivationFunctionType
AX = mybir.AxisListType

B, T, C = 16, 512, 128
P = 128
TPB = T // P
NT = B * TPB
H, D = 16, 8
EPS = 1e-5
EPS_DEN = 1e-6
GATE_MIN = 0.25
FH, FD = 4, 32
E, DF = 8, 512
FC = DF // P
SLOTS = 72
NEG = -1e30
ds = bass.ds

W_PROJT, W_RT, W_KT, W_Q1, W_K1, W_V1, W_G1, W_FQ, W_FK, W_FV, W_FO = range(11)
SA0, CA0, SB0, CB0, SA1, CA1 = range(6)
MU_R, MU_K, GN_W, GN_B, BQ, BK, BV = range(7)


def wait(e, sem, value):
    if isinstance(value, int) and value <= 0:
        return
    e.wait_ge(sem, value)


def prologue(nc, A, K):
    with ExitStack() as ctx:
        sb = lambda n, s, d=F32: ctx.enter_context(nc.sbuf_tensor(n, s, d))
        sem = lambda n: ctx.enter_context(nc.semaphore(n))
        ps = [ctx.enter_context(nc.psum_tensor(f"p0_{i}", [P, 512], F32)) for i in range(8)]
        craw = sb("craw", [32, P])
        wmod = [sb(f"wmod{l}", [P, 6 * P]) for l in range(2)]
        raw = sb("raw", [P, 12, P])
        raw8 = sb("raw8", [E, P])
        sc = sb("sc", [P, 32])
        sc_rep = sb("sc_rep", [P, 8, 16])
        gates = sb("gates", [P, 3, 16])
        bv_rep = sb("bv_rep", [P, P])
        bo_row = sb("bo_row", [P, P])
        diag = sb("diag", [P, 2, 4, P])
        zeros = sb("zeros", [P, 9 * P])
        ct = [sb(f"ct{i}", [P, P]) for i in range(3)]
        cg = [sb(f"cg{i}", [P, 48]) for i in range(3)]

        s_c, s_w, s_v, s_tab = sem("s_c"), sem("s_w"), sem("s_v"), sem("s_tab")
        silu_done, crep, csT = sem("silu_done"), sem("crep"), sem("csT")
        mod_ps, mod_done, gate_done = sem("mod_ps"), sem("mod_done"), sem("gate_done")
        chain, tab_ps = sem("chain0"), sem("tab_ps")
        wt_ps, wt_done = sem("wt_ps"), sem("wt_done")
        diag_done, wg_ps, wg_done = sem("diag_done"), sem("wg_ps"), sem("wg_done")
        bo_ps, vrep, zset, stats = sem("bo_ps"), sem("vrep"), sem("zset"), sem("stats0")
        ident_in = sem("ident_in")

        col = lambda v: v.rearrange("(p a) -> p a", a=1)
        row = lambda v: v.rearrange("(a n) -> a n", a=1)

        raws = [A["L0_attn_w_proj"], A["L0_ffn_W_r"], A["L0_ffn_W_k"], A["L1_attn_Wq"], A["L1_attn_Wk"],
                A["L1_attn_Wv"], A["L1_attn_Wg"], A["L1_ffn_Wqkv"][0:P, :], A["L1_ffn_Wqkv"][P:2 * P, :],
                A["L1_ffn_Wqkv"][2 * P:3 * P, :], A["L1_ffn_Wo"], A["L0_ffn_W_v"]]

        with nc.Block() as block:
            @block.sync
            def _(sp):
                sp.dma_start(craw[0:16, :], A["L0_c"]).then_inc(s_c, 16)
                sp.dma_start(craw[16:32, :], A["L1_c"]).then_inc(s_c, 16)
                sp.dma_start(K.ident[:, :], A["k_ident"]).then_inc(ident_in, 16)
                for l in range(2):
                    sp.dma_start(wmod[l][:, :], A[f"L{l}_wmod"]).then_inc(s_c, 16)
                for i, w in enumerate(raws):
                    sp.dma_start(raw[:, i, :], w).then_inc(s_w, 16)
                sp.dma_start(raw8[:, :], A["L1_ffn_Wg"]).then_inc(s_w, 16)
                sp.dma_start(K.wo1[:, :], A["L1_attn_Wo"]).then_inc(s_w, 16)
                sp.dma_start(K.cmat[:, :], A["k_centre"]).then_inc(s_w, 16)
                for g in range(4):
                    sp.dma_start(K.X[:, 16 * g:16 * g + 16, :],
                                 A["L0_attn_x"].rearrange("b (t p) f -> p (b t) f", p=P)[:, 16 * g:16 * g + 16, :])\
                      .then_inc(K.x_in[g], 16)
                sp.wait_ge(s_v, 8 * 16)
                sp.wait_ge(s_tab, 12 * 16)
                sp.wait_ge(zset, 1)
                for g in range(8):
                    sp.dma_start(A["ys"].rearrange("(p r) f -> p (r f)", p=P)[:, 9 * P * g:9 * P * g + 9 * P],
                                 zeros[:, :]).then_inc(K.ys_zero, 16)
                sp.wait_ge(K.ys_zero, 8 * 16)

            @block.scalar
            def _(act):
                vecs = [A["L0_ffn_mu_r"], A["L0_ffn_mu_k"], A["L1_attn_gn_w"], A["L1_attn_gn_b"],
                        A["L1_ffn_bqkv"][0:P], A["L1_ffn_bqkv"][P:2 * P], A["L1_ffn_bqkv"][2 * P:3 * P]]
                for i, v in enumerate(vecs):
                    act.dma_start(K.cols[:, i:i + 1], col(v)).then_inc(s_v, 16)
                act.dma_start(bo_row[:, :], row(A["L1_ffn_bo"]).to_broadcast([P, P])).then_inc(s_v, 16)
                act.dma_start(K.wqkv0[:, :], A["L0_attn_w_attn"]).then_inc(s_tab, 16)
                act.dma_start(K.utri[:, :], A["k_utri"]).then_inc(s_tab, 16)
                act.dma_start(K.blk[:, :, :], A["k_blk"].rearrange("p (h j) -> p h j", h=H)).then_inc(s_tab, 16)
                act.dma_start(K.rope_c[:, :, :], A["k_rope_c"].rearrange("(t p) n -> p t n", p=P)).then_inc(s_tab, 16)
                act.dma_start(K.rope_s[:, :, :], A["k_rope_s"].rearrange("(t p) n -> p t n", p=P)).then_inc(s_tab, 16)
                act.dma_start(K.smask[:, :], A["k_smask"]).then_inc(s_tab, 16)
                for i, v in enumerate(("g1", "be1", "g2", "be2")):
                    act.dma_start(K.rows[:, i, :], row(A["L1_ffn_" + v]).to_broadcast([P, P])).then_inc(s_tab, 16)
                act.dma_start(K.w1[:, :, :], A["L1_ffn_W1"].rearrange("e d f -> d e f")).then_inc(s_tab, 16)
                act.dma_start(K.w2[:, :, :, :], A["L1_ffn_W2"].rearrange("e (c p) f -> p e c f", p=P)).then_inc(s_tab, 16)
                act.wait_ge(csT, 1)
                act.activation(sc[:, :], ps[0][:, 0:32], ACT.Silu).then_inc(silu_done, 1)
                for g in range(3):
                    n = min(4, 11 - 4 * g)
                    act.wait_ge(wt_ps, g + 1)
                    act.activation(K.W[:, 4 * g:4 * g + n, :].rearrange("p a b -> p (a b)"), ps[2 + g][:, 0:n * P],
                                   ACT.Copy).then_inc(wt_done, 1)
                act.wait_ge(wt_ps, 4)
                act.activation(K.wg8[:, :], ps[5][:, 0:E], ACT.Copy).then_inc(wt_done, 1)
                for g in range(12):
                    act.wait_ge(wg_ps, g + 1)
                    act.activation(K.wgate[:, g // 4, 4 * (g % 4):4 * (g % 4) + 4, :].rearrange("p a b -> p (a b)"),
                                   ps[6 + g % 2][:, :], ACT.Copy).then_inc(wg_done, 1)

            @block.tensor
            def _(pe):
                pe.wait_ge(s_c, 64)
                pe.wait_ge(ident_in, 16)
                pe.transpose(ps[0][:, 0:32], craw[:, :], K.ident[0:32, 0:32]).then_inc(csT, 1)
                pe.wait_ge(silu_done, 1)
                kinds = [(0, 0), (0, 1), (0, 3), (0, 4), (1, 0), (1, 1), (0, 2), (0, 5), (1, 2)]
                for i, (l, k) in enumerate(kinds):
                    mm = pe.matmul(ps[1][:, 16 * i:16 * i + 16], wmod[l][:, k * P:(k + 1) * P],
                                   sc[:, 16 * l:16 * l + 16], start=True, stop=True)
                mm.then_inc(mod_ps, 1)
                pe.wait_ge(crep, 1)
                pe.matmul(ps[0][:, 0:3 * P], sc_rep[:, :, :].rearrange("p a b -> p (a b)"),
                          wmod[1][:, 3 * P:6 * P], start=True, stop=True).then_inc(tab_ps, 1)
                pe.wait_ge(s_w, 15 * 16)
                for i in range(11):
                    o = ps[2 + i // 4][:, (i % 4) * P:(i % 4 + 1) * P]
                    if i == W_V1:
                        mm = pe.matmul(o, raw[:, i, :], K.cmat[:, :], start=True, stop=True)
                    else:
                        mm = pe.transpose(o, raw[:, i, :], K.ident[:, :])
                    if i % 4 == 3 or i == 10:
                        mm.then_inc(wt_ps, 1)
                pe.transpose(ps[5][:, 0:E], raw8[:, :], K.ident[0:E, 0:E]).then_inc(wt_ps, 1)
                pe.wait_ge(wt_done, 4)
                pe.wait_ge(vrep, 1)
                pe.matmul(ps[5][:, P:2 * P], bv_rep[:, :], K.W[:, W_FO, :], start=True, stop=True).then_inc(bo_ps, 1)
                lhs = [K.W[:, W_PROJT, :], raw[:, 11, :], K.wo1[:, :]]
                for g in range(12):
                    pe.wait_ge(diag_done, g + 1)
                    if g >= 2:
                        pe.wait_ge(wg_done, g - 1)
                    for j in range(4):
                        mm = pe.matmul(ps[6 + g % 2][:, j * P:(j + 1) * P], lhs[g // 4], diag[:, g % 2, j, :],
                                       start=True, stop=True)
                    mm.then_inc(wg_ps, 1)

            @block.gpsimd
            def _(pool):
                pool.memset(zeros[:, :], 0.0).then_inc(zset, 1)
                pool.memset(K.eps[:, :], EPS).then_inc(zset, 1)

            @block.vector
            def _(v):
                count = [0]

                def link(ins):
                    count[0] += 1
                    ins.then_inc(chain, 1)
                    v.wait_ge(chain, count[0])

                def clamp(out, x, tmp):
                    link(v.scalar_tensor_tensor(out=tmp[0], in0=x, scalar=-1.0, in1=x, op0=ALU.mult, op1=ALU.max))
                    link(v.tensor_scalar(tmp[1], x, 0.0, 2.0, ALU.is_ge, ALU.mult))
                    link(v.tensor_scalar(tmp[0], tmp[0], GATE_MIN, None, ALU.max))
                    link(v.scalar_tensor_tensor(out=out, in0=tmp[1], scalar=-1.0, in1=tmp[0],
                                                op0=ALU.add, op1=ALU.mult))

                v.wait_ge(silu_done, 1)
                v.tensor_copy(sc_rep[:, :, :], sc[:, 16:32].unsqueeze(1).to_broadcast([P, 8, 16])).then_inc(crep, 1)
                v.wait_ge(s_v, 8 * 16)
                v.tensor_copy(bv_rep[:, :], K.cols[:, BV:BV + 1].to_broadcast([P, P])).then_inc(vrep, 1)
                v.wait_ge(mod_ps, 1)
                v.tensor_copy(K.mod[:, :, :].rearrange("p k b -> p (k b)"), ps[1][:, 0:96]).then_inc(mod_done, 1)
                link(v.tensor_copy(cg[2][:, :], ps[1][:, 96:144]))
                v.wait_ge(mod_done, 1)
                for k in (CA0, CB0, CA1):
                    link(v.tensor_scalar(K.mod[:, k, :], K.mod[:, k, :], 1.0, None, ALU.add))
                clamp(gates[:, :, :].rearrange("p k b -> p (k b)"), cg[2][:, :], [cg[0][:, :], cg[1][:, :]])
                for g in range(12):
                    if g >= 2:
                        v.wait_ge(wg_ps, g - 1)
                    v.tensor_tensor(diag[:, g % 2, :, :], K.ident[:, :].unsqueeze(1).to_broadcast([P, 4, P]),
                                    gates[:, g // 4, 4 * (g % 4):4 * (g % 4) + 4].unsqueeze(2).to_broadcast([P, 4, P]),
                                    ALU.mult).then_inc(diag_done, 1)
                v.wait_ge(tab_ps, 1)
                link(v.tensor_copy(K.tab[:, 0, :], ps[0][:, 0:P]))
                link(v.tensor_scalar(K.tab[:, 1, :], ps[0][:, P:2 * P], 1.0, None, ALU.add))
                link(v.tensor_copy(ct[2][:, :], ps[0][:, 2 * P:3 * P]))
                clamp(K.tab[:, 2, :], ct[2][:, :], [ct[0][:, :], ct[1][:, :]])
                v.wait_ge(bo_ps, 1)
                link(v.tensor_tensor(K.bo[:, :], ps[5][:, P:2 * P], bo_row[:, :], ALU.add))
                for g in range(4):
                    v.wait_ge(K.x_in[g], 16)
                    with v.Fori(4 * g, 4 * g + 4) as q:
                        for j in range(4):
                            tile_stats(v, K, K.X, 4 * q + j, stats)


def finish_stats_vector(v, K, var_ready, std_ready, rstd_ready):
    mean0, m20, mean1, m21 = (K.bn[:, :, i] for i in (1, 2, 4, 5))
    v.tensor_tensor(K.diff[:, :], mean0, mean1, ALU.subtract).then_inc(var_ready, 1)
    v.tensor_tensor(K.var[:, :], m20, m21, ALU.add).then_inc(var_ready, 1)
    v.wait_ge(var_ready, 2)
    v.scalar_tensor_tensor(out=K.std[:, :], in0=K.diff[:, :], scalar=P / 4.0, in1=K.diff[:, :],
                           op0=ALU.mult, op1=ALU.mult).then_inc(var_ready, 1)
    v.wait_ge(var_ready, 3)
    v.tensor_tensor(K.var[:, :], K.var[:, :], K.std[:, :], ALU.add).then_inc(var_ready, 1)
    v.tensor_tensor(K.diff[:, :], mean0, mean1, ALU.add).then_inc(var_ready, 1)
    v.wait_ge(std_ready, 1)
    v.reciprocal(K.rstd[:, :], K.std[:, :]).then_inc(rstd_ready, 1)
    v.wait_ge(rstd_ready, 1)
    v.wait_ge(var_ready, 5)
    v.scalar_tensor_tensor(out=K.nmr[:, :], in0=K.diff[:, :], scalar=-0.5, in1=K.rstd[:, :],
                           op0=ALU.mult, op1=ALU.mult).then_inc(rstd_ready, 1)


def finish_stats_scalar(act, K, var_ready, std_ready, rstd_ready):
    act.wait_ge(var_ready, 4)
    act.activation(K.std[:, :], K.var[:, :], ACT.Sqrt, bias=K.eps[:, 0:1], scale=1.0 / P).then_inc(std_ready, 1)
    act.wait_ge(rstd_ready, 2)


def tile_stats(v, K, x, n, done):
    v.bn_stats(K.bn[:, ds(n, 1), :].rearrange("p a f -> p (a f)"), x[:, ds(n, 1), :].rearrange("p a f -> p (a f)"))\
     .then_inc(done, 1)


def attention(nc, A, K, layer):
    J = 9 if layer == 0 else 8
    SC = D * J
    heads = [(0, 6), (6, 11), (11, 16)]
    sh, scl = (SA0, CA0) if layer == 0 else (SA1, CA1)
    with ExitStack() as ctx:
        sb = lambda n, s, d=F32: ctx.enter_context(nc.sbuf_tensor(f"a{layer}_{n}", s, d))
        sem = lambda n: ctx.enter_context(nc.semaphore(f"a{layer}_{n}"))
        pb = lambda n: ctx.enter_context(nc.psum_tensor(f"a{layer}_{n}", [P, 512], F32))
        pS = [pb(f"pS{c}") for c in range(3)]
        pR, pT, pQ, pI, pO = pb("pR"), pb("pT"), pb("pQ"), pb("pI"), pb("pO")

        xn = sb("xn", [P, TPB, P])
        hT = sb("hT", [P, TPB * P])
        qk = sb("qk", [P, TPB, 2 * P])
        vv = sb("vv", [P, TPB, H, J])
        kv = sb("kv", [P, 2, H, D, J])
        tt = sb("tt", [P, 2, H, D + 1, J])
        R = sb("R", [P, H, J])
        qT = sb("qT", [P, P])
        nd = sb("nd", [P, 2, H, J])
        rec = sb("rec", [P, H])
        y = sb("y", [P, P])
        yT = sb("yT", [P, P])
        if layer == 0:
            ea = sb("ea", [P, 2, 2 * P])
            eb = sb("eb", [P, 2, 2 * P])
            den = sb("den", [P, H])
            wqkv = K.wqkv0[:, :]
        else:
            ra = sb("ra", [P, 2, 2 * P])
            rb = sb("rb", [P, 2, 2 * P])
            gate = sb("gate", [P, 2 * T])
            sq = sb("sq", [P, P])
            vs = sb("vs", [P, H])
            sd = sb("sd", [P, H])
            yaff = sb("yaff", [P, P])
            wqkv = K.W[:, W_Q1:W_V1 + 1, :].rearrange("p a b -> p (a b)")

        var_ready, std_ready, rstd_ready = sem("var"), sem("std"), sem("rstd")
        xn_ready, xn_T, hT_ready = sem("xn_ready"), sem("xn_T"), sem("hT_ready")
        qkv_ps, v_ready, e_ready, qk_ready = sem("qkv_ps"), sem("v_ready"), sem("e_ready"), sem("qk_ready")
        ones_set, relu_done = sem("ones_set"), sem("relu_done")
        gate_ps, gate_ready, rope_read, rope_b = sem("gate_ps"), sem("gate_ready"), sem("rope_read"), sem("rope_b")
        kv_ready, u_done, t_done, red_done = sem("kv_ready"), sem("u_done"), sem("t_done"), sem("red_done")
        p_done, r_ready, q_T, qT_ready = sem("p_done"), sem("r_ready"), sem("q_T"), sem("qT_ready")
        inter_ps, inter_ready = sem("inter_ps"), sem("inter_ready")
        den_done, rec_done, y_ready, y_T, yT_ready = (sem("den_done"), sem("rec_done"), sem("y_ready"),
                                                      sem("y_T"), sem("yT_ready"))
        aff_done, sq_done, var_done, sd_done = sem("aff_done"), sem("sq_done"), sem("var_done"), sem("sd_done")
        proj_ps, x_done, bn_done, x_out = sem("proj_ps"), sem("x_done"), sem("bn_done"), sem("x_out")

        qk_free = qk_ready if layer == 0 else rope_read

        def tile(t, n):
            return t[:, ds(n, 1), :].rearrange("p a f -> p (a f)")

        def column(t, n):
            return t[:, ds(n, 1)]


        def act_normalise(act, b):
            for t in range(TPB):
                wait(act, xn_T, 4 * b - 3 + t)
                act.activation(xn[:, t, :], tile(K.X, 4 * b + t), ACT.Identity, bias=column(K.nmr, 4 * b + t),
                               scale=column(K.rstd, 4 * b + t)).then_inc(xn_ready, 1)

        def pe_transpose_x(pe, b):
            for t in range(TPB):
                pe.wait_ge(xn_ready, 4 * b + t + 1)
                if t == 0:
                    wait(pe, hT_ready if layer == 0 else gate_ready, b)
                pe.transpose(pT[:, t * P:(t + 1) * P], xn[:, t, :], K.ident[:, :]).then_inc(xn_T, 1)

        def act_modulate(act, b):
            act.wait_ge(xn_T, 4 * b + 4)
            wait(act, qkv_ps, 4 * b)
            if layer == 1:
                wait(act, gate_ps, b)
            act.activation(hT[:, :], pT[:, :], ACT.Identity, bias=column(K.mod[:, sh, :], b),
                           scale=column(K.mod[:, scl, :], b)).then_inc(hT_ready, 1)

        def pe_qkv(pe, b, t):
            m = 4 * b + t
            pe.wait_ge(hT_ready, b + 1)
            wait(pe, v_ready, m)
            wait(pe, qk_free, m)
            pe.matmul(pQ[:, 0:3 * P], hT[:, t * P:(t + 1) * P], wqkv, start=True, stop=True).then_inc(qkv_ps, 1)

        def act_qkv(act, b, t):
            m = 4 * b + t
            act.wait_ge(qkv_ps, m + 1)
            wait(act, kv_ready, m - 3)
            if t < 3:
                wait(act, p_done, 3 * b - 3 + t + 1)
            act.activation(vv[:, t, :, 0:D], pQ[:, 2 * P:3 * P].rearrange("p (h j) -> p h j", h=H),
                           ACT.Copy).then_inc(v_ready, 1)
            if layer == 0:
                wait(act, e_ready, m - 1)
                act.activation(ea[:, t % 2, :], pQ[:, 0:2 * P], ACT.Relu, scale=-1.0).then_inc(relu_done, 1)
                act.wait_ge(relu_done, m + 1)
                wait(act, qk_ready, m - 1)
                act.activation(eb[:, t % 2, :], ea[:, t % 2, :], ACT.Exp, scale=-1.0).then_inc(e_ready, 1)

        def slot_free(e, b, t):
            m = 4 * b + t
            wait(e, kv_ready, m - 3)
            wait(e, t_done, 3 * (m - 3))
            if t < 3:
                wait(e, p_done, 3 * b - 3 + t + 1)
            if t > 0:
                wait(e, q_T, 3 * b - 3 + t)

        def vec_qk(v, b, t):
            m = 4 * b + t
            if layer == 0:
                v.wait_ge(e_ready, m + 1)
                v.wait_ge(v_ready, m + 1)
                slot_free(v, b, t)
                v.scalar_tensor_tensor(out=qk[:, t, :], in0=pQ[:, 0:2 * P], scalar=1.0, in1=eb[:, t % 2, :],
                                       op0=ALU.add, op1=ALU.max).then_inc(qk_ready, 1)
            else:
                v.wait_ge(v_ready, m + 1)
                wait(v, qk_ready, m - 1)
                v.tensor_tensor(ra[:, t % 2, :], pQ[:, 0:2 * P], K.rope_c[:, t, :], ALU.mult).then_inc(rope_b, 1)
                pv = pQ[:, 0:2 * P].rearrange("p (g u i) -> p g u i", u=2, i=D // 2)
                rv = rb[:, t % 2, :].rearrange("p (g u i) -> p g u i", u=2, i=D // 2)
                sv = K.rope_s[:, t, :].rearrange("p (g u i) -> p g u i", u=2, i=D // 2)
                v.tensor_tensor(rv[:, :, 0, :], pv[:, :, 1, :], sv[:, :, 0, :], ALU.mult).then_inc(rope_b, 1)
                v.tensor_tensor(rv[:, :, 1, :], pv[:, :, 0, :], sv[:, :, 1, :], ALU.mult).then_inc(rope_read, 1)

        def pool_rope(pool, b, t):
            m = 4 * b + t
            pool.wait_ge(rope_read, m + 1)
            pool.wait_ge(rope_b, 2 * m + 2)
            slot_free(pool, b, t)
            pool.tensor_tensor(qk[:, t, :], ra[:, t % 2, :], rb[:, t % 2, :], ALU.add).then_inc(qk_ready, 1)

        def pool_kv(pool, n, t):
            pool.wait_ge(qk_ready, n + 1)
            pool.wait_ge(v_ready, n + 1)
            wait(pool, u_done, 3 * (n - 1))
            kk = qk[:, t, P:2 * P].rearrange("p (h i) -> p h i", h=H)
            pool.tensor_tensor(kv[:, t % 2, :, :, :], kk.unsqueeze(3).to_broadcast([P, H, D, J]),
                               vv[:, t, :, :].unsqueeze(2).to_broadcast([P, H, D, J]), ALU.mult).then_inc(kv_ready, 1)

        def pe_states(pe, b, t):
            n = 4 * b + t
            pe.wait_ge(kv_ready, n + 1)
            flat = kv[:, t % 2, :, :, :].rearrange("p h i j -> p (h i j)")
            for c, (h0, h1) in enumerate(heads):
                wait(pe, t_done, 3 * (n - 1) + c + 1)
                pe.matmul(pS[c][:, 0:(h1 - h0) * SC], K.utri[:, :], flat[:, h0 * SC:h1 * SC],
                          start=True, stop=True).then_inc(u_done, 1)

        def pe_inter(pe, b, t):
            pe.wait_ge(qT_ready, 3 * b + t)
            pe.wait_ge(r_ready, 3 * b + t)
            pe.matmul(pI[:, P:P + H * J], qT[:, :], R[:, :, :].rearrange("p h j -> p (h j)"),
                      start=True, stop=True).then_inc(inter_ps, 1)

        def pe_state_sum(pe, b, t):
            wait(pe, r_ready, 3 * b + t)
            pe.wait_ge(v_ready, 4 * b + t + 1)
            pe.matmul(pR[:, 0:H * J], qk[:, t, P:2 * P], vv[:, t, :, :].rearrange("p h j -> p (h j)"),
                      start=(t == 0), stop=True, skip_group_check=True).then_inc(p_done, 1)

        def pe_transpose_q(pe, b, t):
            pe.wait_ge(qk_ready, 4 * b + t + 1)
            wait(pe, inter_ready, 3 * b + t - 1)
            pe.transpose(pI[:, 0:P], qk[:, t, 0:P], K.ident[:, :]).then_inc(q_T, 1)

        def pe_transpose_y(pe, m):
            pe.wait_ge(y_ready, m + 1)
            wait(pe, x_done, m)
            pe.transpose(pO[:, 0:P], y[:, :], K.ident[:, :]).then_inc(y_T, 1)

        def pe_project(pe, b, t):
            m = 4 * b + t
            pe.wait_ge(yT_ready, m + 1)
            pe.matmul(pO[:, P:2 * P], yT[:, :], tile(K.wgate[:, 0 if layer == 0 else 2, :, :], b),
                      start=True, stop=True).then_inc(proj_ps, 1)

        def act_inter(act, b, t):
            n = 4 * b + t
            act.wait_ge(inter_ps, 3 * b + t)
            wait(act, red_done, n - 1)
            act.activation(tt[:, t % 2, :, D, :], pI[:, P:P + H * J].rearrange("p (h j) -> p h j", h=H),
                           ACT.Copy).then_inc(inter_ready, 1)

        def act_qT(act, b, t):
            act.wait_ge(q_T, 3 * b + t)
            wait(act, inter_ps, 3 * b + t - 1)
            act.activation(qT[:, :], pI[:, 0:P], ACT.Copy).then_inc(qT_ready, 1)

        def act_yT(act, m):
            act.wait_ge(y_T, m + 1)
            if layer == 0:
                wait(act, proj_ps, m)
                act.activation(yT[:, :], pO[:, 0:P], ACT.Copy).then_inc(yT_ready, 1)
            else:
                wait(act, yT_ready, m)
                act.activation(yaff[:, :], pO[:, 0:P], ACT.Identity, bias=K.cols[:, GN_B:GN_B + 1],
                               scale=K.cols[:, GN_W:GN_W + 1]).then_inc(aff_done, 1)

        def pool_gate(pool, b, t, half):
            m = 4 * b + t
            pool.wait_ge(aff_done, m + 1)
            pool.wait_ge(gate_ready, b + 1)
            wait(pool, proj_ps, m)
            pool.tensor_tensor(yT[:, :], yaff[:, :], gate[:, half * T + t * P:half * T + (t + 1) * P],
                               ALU.mult).then_inc(yT_ready, 1)

        def vec_products(v, b, t):
            n = 4 * b + t
            q = qk[:, t, 0:P].rearrange("p (h i) -> p h i", h=H)
            wait(v, red_done, n - 1)
            for c, (h0, h1) in enumerate(heads):
                v.wait_ge(u_done, 3 * n + c + 1)
                v.tensor_tensor(tt[:, t % 2, h0:h1, 0:D, :],
                                pS[c][:, 0:(h1 - h0) * SC].rearrange("p (h i j) -> p h i j", i=D, j=J),
                                q[:, h0:h1, :].unsqueeze(3).to_broadcast([P, h1 - h0, D, J]),
                                ALU.mult).then_inc(t_done, 1)

        def vec_state(v, b, t):
            v.wait_ge(p_done, 3 * b + t + 1)
            wait(v, inter_ps, 3 * b + t)
            v.tensor_tensor(R[:, :, :], pR[:, 0:H * J].rearrange("p (h j) -> p h j", h=H), K.blk[:, :, 0:J],
                            ALU.mult).then_inc(r_ready, 1)

        def vec_sum(v, b, t):
            n = 4 * b + t
            v.wait_ge(t_done, 3 * n + 3)
            rows = D
            if t > 0:
                v.wait_ge(inter_ready, 3 * b + t)
                rows = D + 1
            wait(v, y_ready, n - 1)
            v.tensor_reduce(nd[:, t % 2, :, :], tt[:, t % 2, :, 0:rows, :].rearrange("p h i j -> p h j i"),
                            AX.X, ALU.add).then_inc(red_done, 1)

        def vec_norm_1(v, n, t):
            v.wait_ge(red_done, n + 1)
            if layer == 0:
                wait(v, rec_done, n)
                v.tensor_scalar(den[:, :], nd[:, t % 2, :, D], EPS_DEN, None, ALU.add).then_inc(den_done, 1)

        def act_square(act, n, t):
            act.wait_ge(red_done, n + 1)
            wait(act, var_done, n)
            act.activation(sq[:, :], nd[:, t % 2, :, :].rearrange("p h j -> p (h j)"), ACT.Square)\
               .then_inc(sq_done, 1)

        def act_sd(act, n):
            act.wait_ge(var_done, n + 1)
            wait(act, rec_done, n)
            act.activation(sd[:, :], vs[:, :], ACT.Sqrt, bias=K.eps[:, 0:1], scale=1.0 / D).then_inc(sd_done, 1)

        def vec_var(v, n):
            v.wait_ge(sq_done, n + 1)
            wait(v, sd_done, n)
            v.tensor_reduce(vs[:, :], sq[:, :].rearrange("p (h j) -> p h j", h=H), AX.X, ALU.add)\
             .then_inc(var_done, 1)

        def vec_norm_2(v, n, t):
            wait(v, y_ready, n)
            if layer == 0:
                v.wait_ge(den_done, n + 1)
                v.reciprocal(rec[:, :], den[:, :]).then_inc(rec_done, 1)
            else:
                v.wait_ge(sd_done, n + 1)
                v.reciprocal(rec[:, :], sd[:, :]).then_inc(rec_done, 1)

        def vec_y(v, n, t):
            v.wait_ge(rec_done, n + 1)
            wait(v, y_T, n)
            v.tensor_tensor(y[:, :].rearrange("p (h j) -> p h j", h=H), nd[:, t % 2, :, 0:D],
                            rec[:, :].unsqueeze(2).to_broadcast([P, H, D]), ALU.mult).then_inc(y_ready, 1)

        def vec_residual(v, m):
            v.wait_ge(proj_ps, m + 1)
            wait(v, x_done, m)
            x = tile(K.X, m)
            v.tensor_tensor(x, pO[:, P:2 * P], x, ALU.add).then_inc(x_done, 1)


        def act_gate(act, b, half):
            act.wait_ge(gate_ps, b + 1)
            wait(act, yT_ready, 4 * (b - 1))
            act.activation(gate[:, half * T:(half + 1) * T], pT[:, :], ACT.Silu).then_inc(gate_ready, 1)

        def pe_gate(pe, b):
            pe.wait_ge(hT_ready, b + 1)
            pe.matmul(pT[:, :], K.W[:, W_G1, :], hT[:, :], start=True, stop=True).then_inc(gate_ps, 1)

        def pe_batch(pe, b, first, last):
            for t in range(TPB):
                pe_states(pe, b, t)
                if t > 0:
                    pe_inter(pe, b, t)
                if t < 3:
                    pe_state_sum(pe, b, t)
                    pe_transpose_q(pe, b, t + 1)
                tail = not (first and t == 0)
                if tail:
                    pe_transpose_y(pe, 4 * b + t - 1)
                if not last:
                    if t == 0:
                        pe_transpose_x(pe, b + 1)
                    pe_qkv(pe, b + 1, t)
                    if layer == 1 and t == 0:
                        pe_gate(pe, b + 1)
                if tail:
                    pe_project(pe, *((b, t - 1) if t else (b - 1, 3)))

        def act_batch(act, b, half, first, last):
            for t in range(TPB):
                if t > 0:
                    act_inter(act, b, t)
                if t < 3:
                    act_qT(act, b, t + 1)
                if not (first and t == 0):
                    act_yT(act, 4 * b + t - 1)
                if not last:
                    if t == 0:
                        act_normalise(act, b + 1)
                        act_modulate(act, b + 1)
                    act_qkv(act, b + 1, t)
                    if layer == 1 and t == 0:
                        act_gate(act, b + 1, 1 - half)
                if layer == 1:
                    act_square(act, 4 * b + t, t)
                    act_sd(act, 4 * b + t)

        def vec_batch(v, b, first, last):
            for t in range(TPB):
                n = 4 * b + t
                vec_products(v, b, t)
                if t < 3:
                    vec_state(v, b, t)
                vec_sum(v, b, t)
                vec_norm_1(v, n, t)
                if layer == 0:
                    vec_norm_2(v, n, t)
                    vec_y(v, n, t)
                if not last:
                    vec_qk(v, b + 1, t)
                if layer == 1:
                    vec_var(v, n)
                    vec_norm_2(v, n, t)
                    vec_y(v, n, t)
                if not (first and t == 0):
                    vec_residual(v, n - 1)
                    if layer == 0 and not (first and t == 1):
                        tile_stats(v, K, K.X, n - 2, bn_done)

        def pool_batch(pool, b, half, first, last):
            for t in range(TPB):
                n = 4 * b + t
                if not (last and t == 3):
                    pool_kv(pool, n + 1, (t + 1) % 4)
                if layer == 1 and not (first and t == 0):
                    pool_gate(pool, *((b, t - 1, half) if t else (b - 1, 3, 1 - half)))
                if layer == 1 and not last:
                    pool_rope(pool, b + 1, t)

        with nc.Block() as block:
            @block.tensor
            def _(pe):
                pe_transpose_x(pe, 0)
                for t in range(TPB):
                    pe_qkv(pe, 0, t)
                if layer == 1:
                    pe_gate(pe, 0)
                pe_batch(pe, 0, True, False)
                with pe.Fori(1, B - 1) as b:
                    pe_batch(pe, b, False, False)
                pe_batch(pe, B - 1, False, True)
                pe_transpose_y(pe, NT - 1)
                pe_project(pe, B - 1, 3)

            @block.scalar
            def _(act):
                finish_stats_scalar(act, K, var_ready, std_ready, rstd_ready)
                act.wait_ge(ones_set, 1)
                act_normalise(act, 0)
                act_modulate(act, 0)
                for t in range(TPB):
                    act_qkv(act, 0, t)
                if layer == 1:
                    act_gate(act, 0, 0)
                act_batch(act, 0, 0, True, False)
                with act.Fori(0, B // 2 - 1) as i:
                    act_batch(act, 2 * i + 1, 1, False, False)
                    act_batch(act, 2 * i + 2, 0, False, False)
                act_batch(act, B - 1, 1, False, True)
                act_yT(act, NT - 1)

            @block.vector
            def _(v):
                v.memset(vv[:, :, :, :], 1.0).then_inc(ones_set, 1)
                finish_stats_vector(v, K, var_ready, std_ready, rstd_ready)
                for t in range(TPB):
                    vec_qk(v, 0, t)
                vec_batch(v, 0, True, False)
                with v.Fori(1, B - 1) as b:
                    vec_batch(v, b, False, False)
                vec_batch(v, B - 1, False, True)
                vec_residual(v, NT - 1)
                if layer == 0:
                    tile_stats(v, K, K.X, NT - 2, bn_done)
                    v.wait_ge(x_done, NT)
                    tile_stats(v, K, K.X, NT - 1, bn_done)

            @block.gpsimd
            def _(pool):
                if layer == 1:
                    for t in range(TPB):
                        pool_rope(pool, 0, t)
                pool_kv(pool, 0, 0)
                pool_batch(pool, 0, 0, True, False)
                with pool.Fori(0, B // 2 - 1) as i:
                    pool_batch(pool, 2 * i + 1, 1, False, False)
                    pool_batch(pool, 2 * i + 2, 0, False, False)
                pool_batch(pool, B - 1, 1, False, True)
                if layer == 1:
                    pool_gate(pool, B - 1, 3, 1)

            @block.sync
            def _(sp):
                if layer == 1:
                    with sp.Fori(0, B) as b:
                        sp.wait_ge(x_done, 4 * b + 4)
                        sp.dma_start(A["xs"].rearrange("(b t p) f -> b p t f", p=P, t=TPB)[ds(b, 1), :, :, :]
                                     .rearrange("o p t f -> (o p) t f"), K.X[:, ds(4 * b, 4), :]).then_inc(x_out, 16)
                    sp.wait_ge(x_out, 16 * B)


def token_shift_ffn(nc, A, K):
    with ExitStack() as ctx:
        sb = lambda n, s, d=F32: ctx.enter_context(nc.sbuf_tensor(f"f_{n}", s, d))
        sem = lambda n: ctx.enter_context(nc.semaphore(f"f_{n}"))
        pb = lambda n: ctx.enter_context(nc.psum_tensor(f"f_{n}", [P, 512], F32))
        pT, pK, pR, pV = pb("pT"), pb("pK"), pb("pR"), pb("pV")
        xn = sb("xn", [P, TPB, P])
        h = sb("h", [P, T + 1])
        d = sb("d", [P, T])
        xr, xk = sb("xr", [P, T]), sb("xk", [P, T])
        kr, ka, sg, vm = sb("kr", [P, T]), sb("ka", [P, T]), sb("sg", [P, T]), sb("vm", [P, T])
        var_ready, std_ready, rstd_ready = sem("var"), sem("std"), sem("rstd")
        xn_ready, xn_T, h_ready, col_zero = sem("xn_ready"), sem("xn_T"), sem("h_ready"), sem("col_zero")
        d_ready, xr_ready, xk_ready = sem("d_ready"), sem("xr_ready"), sem("xk_ready")
        k_ps, r_ps, v_ps = sem("k_ps"), sem("r_ps"), sem("v_ps")
        kr_ready, ka_ready, sg_ready, vm_ready = sem("kr_ready"), sem("ka_ready"), sem("sg_ready"), sem("vm_ready")
        x_done, bn_done = sem("x_done"), sem("bn_done")

        def act_h(act, b):
            for t in range(TPB):
                wait(act, xn_T, 4 * b - 3 + t)
                act.activation(xn[:, t, :], K.X[:, ds(4 * b + t, 1), :].rearrange("p a f -> p (a f)"), ACT.Identity,
                               bias=K.nmr[:, ds(4 * b + t, 1)], scale=K.rstd[:, ds(4 * b + t, 1)]).then_inc(xn_ready, 1)
            act.wait_ge(xn_T, 4 * b + 4)
            wait(act, xr_ready, b)
            wait(act, xk_ready, b)
            act.activation(h[:, 1:T + 1], pT[:, :], ACT.Identity, bias=K.mod[:, SB0, ds(b, 1)],
                           scale=K.mod[:, CB0, ds(b, 1)]).then_inc(h_ready, 1)

        def pe_h(pe, b):
            for t in range(TPB):
                pe.wait_ge(xn_ready, 4 * b + t + 1)
                if t == 0:
                    wait(pe, h_ready, b)
                pe.transpose(pT[:, t * P:(t + 1) * P], xn[:, t, :], K.ident[:, :]).then_inc(xn_T, 1)

        def pool_diff(pool, b):
            pool.wait_ge(h_ready, b + 1)
            wait(pool, xr_ready, b)
            wait(pool, xk_ready, b)
            pool.tensor_tensor(d[:, :], h[:, 1:T + 1], h[:, 0:T], ALU.subtract).then_inc(d_ready, 1)

        def vec_mix(v, b):
            v.wait_ge(d_ready, b + 1)
            wait(v, k_ps, b)
            v.scalar_tensor_tensor(out=xk[:, :], in0=d[:, :], scalar=K.cols[:, MU_K:MU_K + 1], in1=h[:, 0:T],
                                   op0=ALU.mult, op1=ALU.add).then_inc(xk_ready, 1)
            wait(v, r_ps, b)
            v.scalar_tensor_tensor(out=xr[:, :], in0=d[:, :], scalar=K.cols[:, MU_R:MU_R + 1], in1=h[:, 0:T],
                                   op0=ALU.mult, op1=ALU.add).then_inc(xr_ready, 1)

        def pe_kr(pe, b):
            pe.wait_ge(xk_ready, b + 1)
            wait(pe, kr_ready, b)
            pe.matmul(pK[:, :], K.W[:, W_KT, :], xk[:, :], start=True, stop=True).then_inc(k_ps, 1)
            pe.wait_ge(xr_ready, b + 1)
            wait(pe, sg_ready, b)
            for t in range(TPB):
                mm = pe.matmul(pR[:, t * P:(t + 1) * P], xr[:, t * P:(t + 1) * P], K.W[:, W_RT, :],
                               start=True, stop=True)
            mm.then_inc(r_ps, 1)

        def act_kr(act, b):
            act.wait_ge(k_ps, b + 1)
            wait(act, ka_ready, b)
            act.activation(kr[:, :], pK[:, :], ACT.Relu).then_inc(kr_ready, 1)
            act.wait_ge(kr_ready, b + 1)
            wait(act, v_ps, b)
            act.activation(ka[:, :], kr[:, :], ACT.Square).then_inc(ka_ready, 1)
            act.wait_ge(r_ps, b + 1)
            wait(act, vm_ready, b)
            act.activation(sg[:, :], pR[:, :], ACT.Sigmoid).then_inc(sg_ready, 1)

        def pe_v(pe, b):
            pe.wait_ge(ka_ready, b + 1)
            wait(pe, vm_ready, b)
            for t in range(TPB):
                mm = pe.matmul(pV[:, t * P:(t + 1) * P], ka[:, t * P:(t + 1) * P],
                               K.wgate[:, 1, ds(b, 1), :].rearrange("p a f -> p (a f)"), start=True, stop=True)
            mm.then_inc(v_ps, 1)

        def vec_out(v, b):
            v.wait_ge(v_ps, b + 1)
            v.wait_ge(sg_ready, b + 1)
            wait(v, x_done, b)
            v.tensor_tensor(vm[:, :], pV[:, :], sg[:, :], ALU.mult).then_inc(vm_ready, 1)
            v.wait_ge(vm_ready, b + 1)
            x = K.X[:, ds(4 * b, 4), :].rearrange("p a f -> p (a f)")
            v.tensor_tensor(x, vm[:, :], x, ALU.add).then_inc(x_done, 1)

        def vec_stats(v, b):
            for t in range(TPB):
                tile_stats(v, K, K.X, 4 * b + t, bn_done)

        with nc.Block() as block:
            @block.tensor
            def _(pe):
                def step(b, last=False):
                    pe_kr(pe, b)
                    if not last:
                        pe_h(pe, b + 1)
                    pe_v(pe, b)
                pe_h(pe, 0)
                step(0)
                with pe.Fori(1, B - 1) as b:
                    step(b)
                step(B - 1, last=True)

            @block.scalar
            def _(act):
                def step(b, last=False):
                    act_kr(act, b)
                    if not last:
                        act_h(act, b + 1)
                finish_stats_scalar(act, K, var_ready, std_ready, rstd_ready)
                act_h(act, 0)
                step(0)
                with act.Fori(1, B - 1) as b:
                    step(b)
                step(B - 1, last=True)

            @block.vector
            def _(v):
                def step(b, first=False, last=False):
                    if not last:
                        vec_mix(v, b + 1)
                    vec_out(v, b)
                    if not first:
                        vec_stats(v, b - 1)
                v.memset(h[:, 0:1], 0.0).then_inc(col_zero, 1)
                finish_stats_vector(v, K, var_ready, std_ready, rstd_ready)
                vec_mix(v, 0)
                step(0, first=True)
                with v.Fori(1, B - 1) as b:
                    step(b)
                step(B - 1, last=True)
                v.wait_ge(x_done, B)
                vec_stats(v, B - 1)

            @block.gpsimd
            def _(pool):
                pool.wait_ge(col_zero, 1)
                pool_diff(pool, 0)
                with pool.Fori(1, B) as b:
                    pool_diff(pool, b)


def attend_batches(nc, A, K):
    G = NT // 4
    with ExitStack() as ctx:
        sb = lambda n, s, d=F32: ctx.enter_context(nc.sbuf_tensor(f"m_{n}", s, d))
        sem = lambda n: ctx.enter_context(nc.semaphore(f"m_{n}"))
        pb = lambda n: ctx.enter_context(nc.psum_tensor(f"m_{n}", [P, 512], F32))
        pT, pq, pk, pv, pS, pO, pU = pb("pT"), pb("pq"), pb("pk"), pb("pv"), pb("pS"), pb("pO"), pb("pU")
        xn, h1, h, h3 = (sb(n, [P, 4, P]) for n in ("xn", "h1", "h", "h3"))
        hT, qT = sb("hT", [P, 4 * P]), sb("qT", [P, 4 * P])
        kx = sb("kx", [P, 16, FH, 32])
        v_ = sb("v", [P, 4, P])
        sm, s2, ex, pn = (sb(n, [P, 16, 32]) for n in ("sm", "s2", "ex", "pn"))
        mx, sm_sum, rc = sb("mx", [P, 16]), sb("sum", [P, 16]), sb("rc", [P, 16])
        ax = sb("ax", [P, 16, 4, 32])
        oT = sb("oT", [P, 4 * P])
        x_in = [sem(f"x_in{g}") for g in range(4)]
        stats, var_ready, std_ready, rstd_ready = sem("stats"), sem("var"), sem("std"), sem("rstd")
        xn_ready, h1_ready, h_ready, h3_ready = sem("xn_ready"), sem("h1_ready"), sem("h_ready"), sem("h3_ready")
        h_T, hT_ready, q_ps, k_ps, v_ps = sem("h_T"), sem("hT_ready"), sem("q_ps"), sem("k_ps"), sem("v_ps")
        q_ready, kx_act, kx_vec, v_ready, zeroed = (sem("q_ready"), sem("kx_act"), sem("kx_vec"), sem("v_ready"),
                                                    sem("zeroed"))
        s_ps, sm_ready, mx_ready, s2_ready, ex_ready = (sem("s_ps"), sem("sm_ready"), sem("mx_ready"),
                                                        sem("s2_ready"), sem("ex_ready"))
        sum_ready, rc_ready, pn_ready, ax_ready = sem("sum_ready"), sem("rc_ready"), sem("pn_ready"), sem("ax_ready")
        o_ps, oT_ready, w_ps, u_ready, bn_done = sem("o_ps"), sem("oT_ready"), sem("w_ps"), sem("u_ready"), sem("bn_done")

        flat = lambda t: t[:, :, :].rearrange("p a b -> p (a b)")
        over = lambda row: row.unsqueeze(1).to_broadcast([P, 4, P])

        def act_xn(act, g):
            wait(act, h1_ready, g)
            for t in range(4):
                act.activation(xn[:, t, :], K.X[:, ds(4 * g + t, 1), :].rearrange("p a f -> p (a f)"), ACT.Identity,
                               bias=K.nmr[:, ds(4 * g + t, 1)], scale=K.rstd[:, ds(4 * g + t, 1)]).then_inc(xn_ready, 1)

        def pool_h(pool, g):
            pool.wait_ge(xn_ready, 4 * g + 4)
            wait(pool, h_ready, g)
            pool.tensor_tensor(h1[:, :, :], xn[:, :, :], over(K.tab[:, 1, :]), ALU.mult).then_inc(h1_ready, 1)
            pool.wait_ge(h1_ready, g + 1)
            wait(pool, h_T, g)
            wait(pool, h3_ready, g)
            pool.tensor_tensor(h[:, :, :], h1[:, :, :], over(K.tab[:, 0, :]), ALU.add).then_inc(h_ready, 1)

        def pool_h3(pool, g):
            pool.wait_ge(h_ready, g + 1)
            wait(pool, u_ready, g)
            pool.tensor_tensor(h3[:, :, :], h[:, :, :], over(K.bo[:, :]), ALU.add).then_inc(h3_ready, 1)

        def pool_shift(pool, g):
            pool.wait_ge(mx_ready, g + 1)
            wait(pool, ex_ready, g)
            pool.tensor_tensor(s2[:, :, :], sm[:, :, :], mx[:, :].unsqueeze(2).to_broadcast([P, 16, 32]),
                               ALU.subtract).then_inc(s2_ready, 1)

        def pe_T(pe, g):
            pe.wait_ge(h_ready, g + 1)
            wait(pe, hT_ready, g)
            for t in range(4):
                mm = pe.transpose(pT[:, t * P:(t + 1) * P], h[:, t, :], K.ident[:, :])
            mm.then_inc(h_T, 1)

        def act_hT(act, g):
            act.wait_ge(h_T, g + 1)
            wait(act, v_ps, g)
            act.activation(hT[:, :], pT[:, :], ACT.Copy).then_inc(hT_ready, 1)

        def pe_qk(pe, g):
            pe.wait_ge(hT_ready, g + 1)
            wait(pe, q_ready, g)
            pe.matmul(pq[:, :], K.W[:, W_FQ, :], hT[:, :], start=True, stop=True).then_inc(q_ps, 1)
            wait(pe, kx_act, 2 * g)
            wait(pe, kx_vec, 2 * g)
            pe.matmul(pk[:, :], K.W[:, W_FK, :], hT[:, :], start=True, stop=True).then_inc(k_ps, 1)

        def pe_v(pe, g):
            wait(pe, v_ready, g)
            for t in range(4):
                mm = pe.matmul(pv[:, t * P:(t + 1) * P], hT[:, t * P:(t + 1) * P], K.W[:, W_FV, :],
                               start=True, stop=True)
            mm.then_inc(v_ps, 1)

        def act_q(act, g):
            act.wait_ge(q_ps, g + 1)
            wait(act, s_ps, g)
            act.activation(qT[:, :], pq[:, :], ACT.Identity, bias=K.cols[:, BQ:BQ + 1]).then_inc(q_ready, 1)

        def kx_view(hd):
            rows = slice(32 * hd, 32 * hd + 32)
            return rows, kx[rows, :, hd, :], pk[rows, :].rearrange("p (c s) -> p c s", c=16)

        def act_k(act, g):
            act.wait_ge(k_ps, g + 1)
            for hd in range(2):
                rows, o, i = kx_view(hd)
                act.activation(o, i, ACT.Identity, bias=K.cols[rows, BK:BK + 1]).then_inc(kx_act, 1)

        def vec_k(v, g):
            v.wait_ge(k_ps, g + 1)
            wait(v, s_ps, g)
            for hd in range(2, 4):
                rows, o, i = kx_view(hd)
                v.tensor_scalar(o, i, K.cols[rows, BK:BK + 1], None, ALU.add).then_inc(kx_vec, 1)

        def act_v(act, g):
            act.wait_ge(v_ps, g + 1)
            wait(act, o_ps, g)
            act.activation(flat(v_), pv[:, :], ACT.Copy).then_inc(v_ready, 1)

        def pe_scores(pe, g):
            pe.wait_ge(q_ready, g + 1)
            pe.wait_ge(kx_act, 2 * g + 2)
            pe.wait_ge(kx_vec, 2 * g + 2)
            wait(pe, sm_ready, g)
            for t in range(4):
                for c in range(4):
                    mm = pe.matmul(pS[32 * c:32 * c + 32, t * P:(t + 1) * P], qT[:, t * P + 32 * c:t * P + 32 * c + 32],
                                   kx[:, 4 * t + c, :, :].rearrange("p h s -> p (h s)"), start=True, stop=True,
                                   skip_group_check=True)
            mm.then_inc(s_ps, 1)

        def vec_scores(v, g):
            v.wait_ge(s_ps, g + 1)
            wait(v, s2_ready, g)
            v.scalar_tensor_tensor(out=sm[:, :, :], in0=pS[:, :].rearrange("p (a s) -> p a s", s=32),
                                   scalar=float(FD) ** -0.5, in1=K.smask[:, :].unsqueeze(1).to_broadcast([P, 16, 32]),
                                   op0=ALU.mult, op1=ALU.add).then_inc(sm_ready, 1)
            v.wait_ge(sm_ready, g + 1)
            v.tensor_reduce(mx[:, :], sm[:, :, :], AX.X, ALU.max).then_inc(mx_ready, 1)

        def act_exp(act, g):
            act.wait_ge(s2_ready, g + 1)
            wait(act, pn_ready, g)
            act.activation(flat(ex), flat(s2), ACT.Exp).then_inc(ex_ready, 1)

        def vec_probs(v, g):
            v.wait_ge(ex_ready, g + 1)
            wait(v, rc_ready, g)
            v.tensor_reduce(sm_sum[:, :], ex[:, :, :], AX.X, ALU.add).then_inc(sum_ready, 1)
            v.wait_ge(sum_ready, g + 1)
            wait(v, pn_ready, g)
            v.reciprocal(rc[:, :], sm_sum[:, :]).then_inc(rc_ready, 1)
            v.wait_ge(rc_ready, g + 1)
            wait(v, ax_ready, 4 * g)
            v.tensor_tensor(pn[:, :, :], ex[:, :, :], rc[:, :].unsqueeze(2).to_broadcast([P, 16, 32]),
                            ALU.mult).then_inc(pn_ready, 1)
            v.wait_ge(pn_ready, g + 1)
            wait(v, o_ps, g)
            for c in range(4):
                rows = slice(32 * c, 32 * c + 32)
                v.transpose(ax[rows, :, c, :], pn[rows, :, :]).then_inc(ax_ready, 1)

        def pe_values(pe, g):
            pe.wait_ge(ax_ready, 4 * g + 4)
            pe.wait_ge(v_ready, g + 1)
            wait(pe, oT_ready, g)
            for t in range(4):
                for hd in range(FH):
                    mm = pe.matmul(pO[32 * hd:32 * hd + 32, t * P:(t + 1) * P], v_[:, t, 32 * hd:32 * hd + 32],
                                   ax[:, 4 * t + hd, :, :].rearrange("p c s -> p (c s)"), start=True, stop=True,
                                   skip_group_check=True)
            mm.then_inc(o_ps, 1)

        def act_o(act, g):
            act.wait_ge(o_ps, g + 1)
            wait(act, w_ps, g)
            act.activation(oT[:, :], pO[:, :], ACT.Copy).then_inc(oT_ready, 1)

        def pe_out(pe, g):
            pe.wait_ge(oT_ready, g + 1)
            wait(pe, u_ready, g)
            for t in range(4):
                mm = pe.matmul(pU[:, t * P:(t + 1) * P], oT[:, t * P:(t + 1) * P], K.W[:, W_FO, :],
                               start=True, stop=True)
            mm.then_inc(w_ps, 1)

        def vec_u(v, g):
            v.wait_ge(w_ps, g + 1)
            v.wait_ge(h3_ready, g + 1)
            wait(v, u_ready, g)
            v.tensor_tensor(K.U[:, ds(4 * g, 4), :].rearrange("p a f -> p (a f)"), pU[:, :], flat(h3), ALU.add)\
             .then_inc(u_ready, 1)

        def vec_stats(v, g):
            for t in range(4):
                tile_stats(v, K, K.U, 4 * g + t, bn_done)

        with nc.Block() as block:
            @block.sync
            def _(sp):
                xs = A["xs"].rearrange("(b n t) f -> t b n f", n=NT, t=8)
                for g in range(4):
                    for t in range(8):
                        sp.dma_start(K.X[16 * t:16 * t + 16, 16 * g:16 * g + 16, :], xs[t][:, 16 * g:16 * g + 16, :])\
                          .then_inc(x_in[g], 16)

            @block.tensor
            def _(pe):
                def step(g, last=False):
                    pe_scores(pe, g)
                    if not last:
                        pe_T(pe, g + 1)
                        pe_qk(pe, g + 1)
                    pe_values(pe, g)
                    if not last:
                        pe_v(pe, g + 1)
                    pe_out(pe, g)
                pe.wait_ge(zeroed, 2)
                pe_T(pe, 0)
                pe_qk(pe, 0)
                pe_v(pe, 0)
                step(0)
                with pe.Fori(1, G - 1) as g:
                    step(g)
                step(G - 1, last=True)

            @block.scalar
            def _(act):
                def step(g, more=True, last=False):
                    if not last:
                        act_hT(act, g + 1)
                    act_exp(act, g)
                    if not last:
                        act_q(act, g + 1)
                        act_k(act, g + 1)
                    act_o(act, g)
                    if not last:
                        act_v(act, g + 1)
                    if more:
                        act_xn(act, g + 2)
                finish_stats_scalar(act, K, var_ready, std_ready, rstd_ready)
                act.wait_ge(zeroed, 2)
                act_xn(act, 0)
                act_xn(act, 1)
                act_hT(act, 0)
                act_q(act, 0)
                act_k(act, 0)
                act_v(act, 0)
                step(0)
                with act.Fori(1, G - 2) as g:
                    step(g)
                step(G - 2, more=False)
                step(G - 1, more=False, last=True)

            @block.vector
            def _(v):
                def step(g, first=False, last=False):
                    vec_scores(v, g)
                    if not last:
                        vec_k(v, g + 1)
                    vec_probs(v, g)
                    vec_u(v, g)
                    if not first:
                        vec_stats(v, g - 1)
                for g in range(4):
                    v.wait_ge(x_in[g], 8 * 16)
                    with v.Fori(4 * g, 4 * g + 4) as q:
                        for j in range(4):
                            tile_stats(v, K, K.X, 4 * q + j, stats)
                v.wait_ge(stats, NT)
                finish_stats_vector(v, K, var_ready, std_ready, rstd_ready)
                v.wait_ge(zeroed, 2)
                vec_k(v, 0)
                step(0, first=True)
                with v.Fori(1, G - 1) as g:
                    step(g)
                step(G - 1, last=True)
                v.wait_ge(u_ready, G)
                vec_stats(v, G - 1)

            @block.gpsimd
            def _(pool):
                pool.memset(kx[:, :, :, :], 0.0).then_inc(zeroed, 1)
                pool.memset(ax[:, :, :, :], 0.0).then_inc(zeroed, 1)
                pool_h(pool, 0)
                pool_h3(pool, 0)

                def step(g, last=False):
                    if not last:
                        pool_h(pool, g + 1)
                    pool_shift(pool, g)
                    if not last:
                        pool_h3(pool, g + 1)
                step(0)
                with pool.Fori(1, G - 1) as g:
                    step(g)
                step(G - 1, last=True)


def route(nc, A, K, pos, expert):
    G = NT // 4
    with ExitStack() as ctx:
        sb = lambda n, s, d=F32: ctx.enter_context(nc.sbuf_tensor(f"r_{n}", s, d))
        sem = lambda n: ctx.enter_context(nc.semaphore(f"r_{n}"))
        pb = lambda n: ctx.enter_context(nc.psum_tensor(f"r_{n}", [P, 512], F32))
        pT, pL, pR, pC = [pb("pT0"), pb("pT1")], [pb("pL0"), pb("pL1")], pb("pR"), pb("pC")
        yn, y1, yb = (sb(n, [P, 2, 4, P]) for n in ("yn", "y1", "yb"))
        yT = sb("yT", [P, 2, 4 * P])
        logits = sb("logits", [P, NT, E])
        ustrict, tie, iota, ones = sb("ustrict", [P, P]), sb("tie", [P, E]), sb("iota", [P, SLOTS]), sb("ones", [P, P])
        best, first = sb("best", [P, NT]), sb("first", [P, NT])
        hot, work = sb("hot", [P, NT, E]), sb("work", [P, NT, E])
        total, upto = sb("total", [P, E, NT]), sb("upto", [P, E, NT])
        tiles, ends, base = sb("tiles", [P, E]), sb("ends", [P, E]), sb("base", [P, E])
        after = sb("after", [P, SLOTS, E])
        posf, expf = sb("posf", [P, NT]), sb("expf", [P, SLOTS])
        var_ready, std_ready, rstd_ready = sem("var"), sem("std"), sem("rstd")
        tab_in, yn_ready, y1_ready, yb_ready, y_ready = (sem("tab_in"), sem("yn_ready"), sem("y1_ready"),
                                                         sem("yb_ready"), sem("y_ready"))
        y_T, yT_ready, l_ps, l_ready, chain, hot_ready, c_ps = (sem("y_T"), sem("yT_ready"), sem("l_ps"), sem("l_ready"),
                                                                sem("chain"), sem("hot_ready"), sem("c_ps"))
        over = lambda row: row.unsqueeze(1).to_broadcast([P, 4, P])

        def act_step(act, g, s):
            wait(act, y1_ready, g - 1)
            for t in range(4):
                act.activation(yn[:, s, t, :], K.U[:, ds(4 * g + t, 1), :].rearrange("p a f -> p (a f)"), ACT.Identity,
                               bias=K.nmr[:, ds(4 * g + t, 1)], scale=K.rstd[:, ds(4 * g + t, 1)]).then_inc(yn_ready, 1)

        def act_yT(act, g, s):
            act.wait_ge(y_T, g + 1)
            wait(act, l_ps, g - 1)
            act.activation(yT[:, s, :], pT[s][:, :], ACT.Copy).then_inc(yT_ready, 1)

        def pe_T(pe, g, s):
            pe.wait_ge(yb_ready, g + 1)
            wait(pe, yT_ready, g - 1)
            for t in range(4):
                mm = pe.transpose(pT[s][:, t * P:(t + 1) * P], yb[:, s, t, :], K.ident[:, :])
            mm.then_inc(y_T, 1)

        def pe_logits(pe, g, s):
            pe.wait_ge(yT_ready, g + 1)
            wait(pe, l_ready, g - 1)
            for t in range(4):
                mm = pe.matmul(pL[s][:, t * E:(t + 1) * E], yT[:, s, t * P:(t + 1) * P], K.wg8[:, :],
                               start=True, stop=True)
            mm.then_inc(l_ps, 1)

        def vec_y(v, g, s):
            v.wait_ge(yn_ready, 4 * g + 4)
            wait(v, yb_ready, g - 1)
            wait(v, y_ready, g - 1)
            v.tensor_tensor(y1[:, s, :, :], yn[:, s, :, :], over(K.rows[:, 0, :]), ALU.mult).then_inc(y1_ready, 1)
            v.wait_ge(y1_ready, g + 1)
            wait(v, y_T, g - 1)
            v.tensor_tensor(yb[:, s, :, :], y1[:, s, :, :], over(K.rows[:, 1, :]), ALU.add).then_inc(yb_ready, 1)

        def vec_logits(v, g, s):
            v.wait_ge(l_ps, g + 1)
            v.tensor_copy(logits[:, ds(4 * g, 4), :], pL[s][:, 0:4 * E].rearrange("p (a e) -> p a e", e=E))\
             .then_inc(l_ready, 1)

        def pool_y(pool, g, s):
            pool.wait_ge(y1_ready, g + 1)
            pool.tensor_tensor(K.U[:, ds(4 * g, 4), :], y1[:, s, :, :], over(K.rows[:, 1, :]), ALU.add)\
                .then_inc(y_ready, 1)

        with nc.Block() as block:
            @block.sync
            def _(sp):
                sp.dma_start(ustrict[:, :], A["k_ustrict"]).then_inc(tab_in, 16)
                sp.dma_start(tie[:, :], A["k_tie"]).then_inc(tab_in, 16)
                sp.dma_start(iota[:, :], A["k_iota"]).then_inc(tab_in, 16)
                sp.dma_start(K.b1[:, :, :], A["L1_ffn_b1"].rearrange("(a e) f -> a e f", a=1)
                             .to_broadcast([P, E, DF])).then_inc(tab_in, 16)
                sp.dma_start(K.b2[:, :, :], A["L1_ffn_b2"].rearrange("(a e) f -> a e f", a=1)
                             .to_broadcast([P, E, P])).then_inc(tab_in, 16)
                sp.wait_ge(tab_in, 5 * 16)

            @block.scalar
            def _(act):
                finish_stats_scalar(act, K, var_ready, std_ready, rstd_ready)
                act_step(act, 0, 0)
                def pair(i):
                    act_step(act, 2 * i + 1, 1)
                    act_yT(act, 2 * i, 0)
                    act_step(act, 2 * i + 2, 0)
                    act_yT(act, 2 * i + 1, 1)
                pair(0)
                with act.Fori(1, G // 2 - 1) as i:
                    pair(i)
                act_step(act, G - 1, 1)
                act_yT(act, G - 2, 0)
                act_yT(act, G - 1, 1)

            @block.tensor
            def _(pe):
                pe_T(pe, 0, 0)
                def pair(i):
                    pe_T(pe, 2 * i + 1, 1)
                    pe_logits(pe, 2 * i, 0)
                    pe_T(pe, 2 * i + 2, 0)
                    pe_logits(pe, 2 * i + 1, 1)
                pair(0)
                with pe.Fori(1, G // 2 - 1) as i:
                    pair(i)
                pe_T(pe, G - 1, 1)
                pe_logits(pe, G - 2, 0)
                pe_logits(pe, G - 1, 1)
                pe.wait_ge(hot_ready, 1)
                pe.wait_ge(tab_in, 5 * 16)
                h = hot[:, :, :].rearrange("p n e -> p (n e)")
                pe.matmul(pR[:, :], ustrict[:, :], h, start=True, stop=True).then_inc(c_ps, 1)
                pe.matmul(pC[:, :], ones[:, :], h, start=True, stop=True).then_inc(c_ps, 1)

            @block.gpsimd
            def _(pool):
                with pool.Fori(0, G // 2) as i:
                    for s in range(2):
                        pool_y(pool, 2 * i + s, s)

            @block.vector
            def _(v):
                count = [0]

                def link(ins):
                    count[0] += 1
                    ins.then_inc(chain, 1)
                    v.wait_ge(chain, count[0])

                link(v.memset(ones[:, :], 1.0))
                finish_stats_vector(v, K, var_ready, std_ready, rstd_ready)
                v.wait_ge(rstd_ready, 2)
                vec_y(v, 0, 0)
                with v.Fori(0, G // 2 - 1) as i:
                    vec_y(v, 2 * i + 1, 1)
                    vec_logits(v, 2 * i, 0)
                    vec_y(v, 2 * i + 2, 0)
                    vec_logits(v, 2 * i + 1, 1)
                vec_y(v, G - 1, 1)
                vec_logits(v, G - 2, 0)
                vec_logits(v, G - 1, 1)
                v.wait_ge(l_ready, G)
                v.wait_ge(tab_in, 5 * 16)
                by_e = lambda t: t.unsqueeze(2).to_broadcast([P, NT, E])
                by_n = lambda t: t.unsqueeze(1).to_broadcast([P, NT, E])
                link(v.tensor_reduce(best[:, :], logits[:, :, :], AX.X, ALU.max))
                link(v.tensor_tensor(work[:, :, :], logits[:, :, :], by_e(best[:, :]), ALU.is_ge))
                link(v.tensor_tensor(hot[:, :, :], work[:, :, :], by_n(tie[:, :]), ALU.mult))
                link(v.tensor_reduce(first[:, :], hot[:, :, :], AX.X, ALU.max))
                link(v.tensor_tensor(work[:, :, :], by_n(tie[:, :]), by_e(first[:, :]), ALU.is_equal))
                v.tensor_copy(hot[:, :, :], work[:, :, :]).then_inc(hot_ready, 1)
                v.wait_ge(c_ps, 2)
                link(v.tensor_copy(total[:, :, :], pC[:, :].rearrange("p (n e) -> p e n", e=E)))
                for e in range(E):
                    link(v.tensor_tensor_scan(upto[:, e, :], ones[:, 0:NT], total[:, e, :], 0.0, ALU.mult, ALU.add))
                w = work[:, :, :].rearrange("p n e -> p (n e)").rearrange("p (e n) -> p e n", e=E)
                link(v.tensor_scalar(expf[:, 0:NT], iota[:, 0:NT], float(P), None, ALU.mult))
                link(v.tensor_tensor(w, upto[:, :, NT - 1:NT].to_broadcast([P, E, NT]),
                                     expf[:, 0:NT].unsqueeze(1).to_broadcast([P, E, NT]), ALU.is_gt))
                link(v.tensor_reduce(tiles[:, :], w, AX.X, ALU.add))
                link(v.tensor_tensor_scan(ends[:, :], ones[:, 0:E], tiles[:, :], 0.0, ALU.mult, ALU.add))
                link(v.tensor_tensor(base[:, :], ends[:, :], tiles[:, :], ALU.subtract))
                link(v.tensor_scalar(base[:, :], base[:, :], float(P), None, ALU.mult))
                link(v.tensor_tensor(total[:, :, :], upto[:, :, :], total[:, :, :], ALU.subtract))
                link(v.tensor_tensor(total[:, :, :], total[:, :, :], base[:, :].unsqueeze(2).to_broadcast([P, E, NT]),
                                     ALU.add))
                link(v.tensor_tensor(work[:, :, :], pR[:, :].rearrange("p (n e) -> p n e", e=E),
                                     total[:, :, :].rearrange("p e n -> p n e"), ALU.add))
                link(v.tensor_tensor(work[:, :, :], work[:, :, :], hot[:, :, :], ALU.mult))
                link(v.tensor_reduce(posf[:, :], work[:, :, :], AX.X, ALU.add))
                link(v.tensor_copy(pos[:, :], posf[:, :]))
                link(v.tensor_tensor(after[:, :, :], ends[:, :].unsqueeze(1).to_broadcast([P, SLOTS, E]),
                                     iota[:, :].unsqueeze(2).to_broadcast([P, SLOTS, E]), ALU.is_le))
                link(v.tensor_reduce(expf[:, :], after[:, :, :], AX.X, ALU.add))
                link(v.tensor_scalar(expf[:, :], expf[:, :], float(E - 1), None, ALU.min))
                link(v.tensor_copy(expert[:, :], expf[:, :]))


def experts(nc, A, K, out):
    with ExitStack() as ctx:
        sb = lambda n, s, d=F32: ctx.enter_context(nc.sbuf_tensor(f"e_{n}", s, d))
        sem = lambda n: ctx.enter_context(nc.semaphore(f"e_{n}"))
        pb = lambda n: ctx.enter_context(nc.psum_tensor(f"e_{n}", [P, 512], F32))
        pos, expert = sb("pos", [P, NT], U32), sb("expert", [P, SLOTS], I32)
        K.b1, K.b2 = sb("b1", [P, E, DF]), sb("b2", [P, E, P])
        route(nc, A, K, pos, expert)

        scattered = sem("scattered")
        with nc.Block() as block:
            @block.gpsimd
            def _(pool):
                pool.wait_ge(K.ys_zero, 8 * 16)
                for n in range(NT):
                    pool.indirect_dma_start(out=A["ys"], out_offset=bass.IndirectOffsetOnAxis(ap=pos[:, n:n + 1], axis=0),
                                            in_=K.U[:, n, :], in_offset=None).then_inc(scattered, 16)
                pool.wait_ge(scattered, 16 * NT)

        run_experts(nc, A, K, expert)
        finish(nc, A, K, pos, out)


def run_experts(nc, A, K, expert):
    with ExitStack() as ctx:
        sb = lambda n, s, d=F32: ctx.enter_context(nc.sbuf_tensor(f"x_{n}", s, d))
        sem = lambda n: ctx.enter_context(nc.semaphore(f"x_{n}"))
        pb = lambda n: ctx.enter_context(nc.psum_tensor(f"x_{n}", [P, 512], F32))
        pT, pH, pHT, pZ = ([pb(f"{n}{i}") for i in range(2)] for n in ("pT", "pH", "pHT", "pZ"))
        yl, z = sb("yl", [P, 4, P]), sb("z", [P, 4, P])
        yT, hb, hT = sb("yT", [P, 2, P]), sb("hb", [P, 2, DF]), sb("hT", [P, 2, DF])
        y_in, z_out = [sem(f"y_in{s}") for s in range(4)], [sem(f"z_out{s}") for s in range(4)]
        y_T, yT_ready, h_ps, hb_ready, h_T, hT_ready, z_ps, z_ready = (
            sem(n) for n in ("y_T", "yT_ready", "h_ps", "hb_ready", "h_T", "hT_ready", "z_ps", "z_ready"))
        ys, zs = (A[n].rearrange("(j p) f -> j p f", p=P) for n in ("ys", "zs"))
        rounds = SLOTS // 4

        def pe_T(pe, i, s):
            j = 4 * i + s
            pe.wait_ge(y_in[s], 16 * i + 16)
            wait(pe, yT_ready, j - 1)
            pe.transpose(pT[s % 2][:, 0:P], yl[:, s, :], K.ident[:, :]).then_inc(y_T, 1)

        def act_yT(act, i, s):
            j = 4 * i + s
            act.wait_ge(y_T, j + 1)
            wait(act, h_ps, j - 1)
            act.activation(yT[:, s % 2, :], pT[s % 2][:, 0:P], ACT.Copy).then_inc(yT_ready, 1)

        def pe_h(pe, i, s):
            j = 4 * i + s
            e = pe.value_load(expert[0:1, ds(j, 1)], min_val=0, max_val=E - 1)
            pe.wait_ge(yT_ready, j + 1)
            wait(pe, hb_ready, j - 1)
            pe.matmul(pH[s % 2][:, :], yT[:, s % 2, :], K.w1[:, ds(e, 1), :].rearrange("p a f -> p (a f)"),
                      start=True, stop=True).then_inc(h_ps, 1)
            return e

        def vec_h(v, i, s):
            j = 4 * i + s
            e = v.value_load(expert[0:1, ds(j, 1)], min_val=0, max_val=E - 1)
            v.wait_ge(h_ps, j + 1)
            wait(v, h_T, j - 1)
            v.tensor_tensor(hb[:, s % 2, :], pH[s % 2][:, :], K.b1[:, ds(e, 1), :].rearrange("p a f -> p (a f)"),
                            ALU.add).then_inc(hb_ready, 1)

        def pe_hT(pe, i, s):
            j = 4 * i + s
            pe.wait_ge(hb_ready, j + 1)
            wait(pe, hT_ready, j - 1)
            for c in range(FC):
                mm = pe.transpose(pHT[s % 2][:, c * P:(c + 1) * P], hb[:, s % 2, c * P:(c + 1) * P], K.ident[:, :])
            mm.then_inc(h_T, 1)

        def act_hT(act, i, s):
            j = 4 * i + s
            act.wait_ge(h_T, j + 1)
            wait(act, z_ps, j - 1)
            act.activation(hT[:, s % 2, :], pHT[s % 2][:, :], ACT.Relu).then_inc(hT_ready, 1)

        def pe_z(pe, i, s):
            j = 4 * i + s
            e = pe.value_load(expert[0:1, ds(j, 1)], min_val=0, max_val=E - 1)
            pe.wait_ge(hT_ready, j + 1)
            wait(pe, z_ready, j - 1)
            for c in range(FC):
                mm = pe.matmul(pZ[s % 2][:, 0:P], hT[:, s % 2, c * P:(c + 1) * P],
                               K.w2[:, ds(e, 1), c, :].rearrange("p a f -> p (a f)"), start=(c == 0), stop=(c == FC - 1))
            mm.then_inc(z_ps, 1)

        def vec_z(v, i, s):
            j = 4 * i + s
            e = v.value_load(expert[0:1, ds(j, 1)], min_val=0, max_val=E - 1)
            v.wait_ge(z_ps, j + 1)
            wait(v, z_out[s], 16 * i)
            v.tensor_tensor(z[:, s, :], pZ[s % 2][:, 0:P], K.b2[:, ds(e, 1), :].rearrange("p a f -> p (a f)"),
                            ALU.add).then_inc(z_ready, 1)

        def at(i, s):
            return i + s // 4, s % 4

        with nc.Block() as block:
            @block.sync
            def _(sp):
                def load(i, s):
                    wait(sp, y_T, 4 * i + s - 3)
                    sp.dma_start(yl[:, s, :], ys[ds(4 * i + s, 1), :, :].rearrange("o p f -> (o p) f"))\
                      .then_inc(y_in[s], 16)

                def store(i, s):
                    sp.wait_ge(z_ready, 4 * i + s + 1)
                    sp.dma_start(zs[ds(4 * i + s, 1), :, :].rearrange("o p f -> (o p) f"), z[:, s, :])\
                      .then_inc(z_out[s], 16)
                for s in range(4):
                    load(0, s)
                with sp.Fori(0, rounds - 1) as i:
                    for s in range(4):
                        load(i + 1, s)
                        store(i, s)
                for s in range(4):
                    store(rounds - 1, s)
                for s in range(4):
                    sp.wait_ge(z_out[s], 16 * rounds)

            @block.tensor
            def _(pe):
                def step(i, s, last=False):
                    if not (last and s >= 2):
                        pe_T(pe, *at(i, s + 2))
                    pe_hT(pe, i, s)
                    if not (last and s == 3):
                        pe_h(pe, *at(i, s + 1))
                    pe_z(pe, i, s)
                pe_T(pe, 0, 0)
                pe_T(pe, 0, 1)
                pe_h(pe, 0, 0)
                for s in range(4):
                    step(0, s)
                with pe.Fori(1, rounds - 1) as i:
                    for s in range(4):
                        step(i, s)
                for s in range(4):
                    step(rounds - 1, s, last=True)

            @block.scalar
            def _(act):
                def step(i, s, last=False):
                    if not (last and s >= 2):
                        act_yT(act, *at(i, s + 2))
                    act_hT(act, i, s)
                act_yT(act, 0, 0)
                act_yT(act, 0, 1)
                for s in range(4):
                    step(0, s)
                with act.Fori(1, rounds - 1) as i:
                    for s in range(4):
                        step(i, s)
                for s in range(4):
                    step(rounds - 1, s, last=True)

            @block.vector
            def _(v):
                def step(i, s, last=False):
                    if not (last and s == 3):
                        vec_h(v, *at(i, s + 1))
                    vec_z(v, i, s)
                vec_h(v, 0, 0)
                for s in range(4):
                    step(0, s)
                with v.Fori(1, rounds - 1) as i:
                    for s in range(4):
                        step(i, s)
                for s in range(4):
                    step(rounds - 1, s, last=True)


def finish(nc, A, K, pos, out):
    G = NT // 4
    with ExitStack() as ctx:
        sb = lambda n, s, d=F32: ctx.enter_context(nc.sbuf_tensor(f"o_{n}", s, d))
        sem = lambda n: ctx.enter_context(nc.semaphore(f"o_{n}"))
        zg = sb("zg", [P, NT, P])
        zn, zm = sb("zn", [P, 2, 4, P]), sb("zm", [P, 2, 4, P])
        gw, gb = sb("gw", [P, P]), sb("gb", [P, P])
        back = [sem(f"back{g}") for g in range(4)]
        var_ready, std_ready, rstd_ready = sem("var"), sem("std"), sem("rstd")
        tab_done, sum_done, bn_done, zn_ready, zm_ready, xb_done, out_ready, stored = (
            sem(n) for n in ("tab_done", "sum_done", "bn_done", "zn_ready", "zm_ready", "xb_done", "out_ready", "stored"))
        over = lambda row: row.unsqueeze(1).to_broadcast([P, 4, P])
        four = lambda t, g: t[:, ds(4 * g, 4), :]

        with nc.Block() as block:
            @block.gpsimd
            def _(pool):
                for n in range(NT):
                    pool.indirect_dma_start(out=zg[:, n, :], out_offset=None, in_=A["zs"],
                                            in_offset=bass.IndirectOffsetOnAxis(ap=pos[:, n:n + 1], axis=0))\
                        .then_inc(back[n // 16], 16)
                pool.wait_ge(tab_done, 2)

                def scale(i):
                    for s in range(2):
                        g = 2 * i + s
                        pool.wait_ge(zn_ready, 4 * g + 4)
                        wait(pool, out_ready, 2 * i)
                        pool.tensor_tensor(zm[:, s, :, :], zn[:, s, :, :], over(gw[:, :]), ALU.mult).then_inc(zm_ready, 1)
                scale(0)
                with pool.Fori(1, G // 2) as i:
                    scale(i)

            @block.vector
            def _(v):
                v.tensor_tensor(gw[:, :], K.rows[:, 2, :], K.tab[:, 2, :], ALU.mult).then_inc(tab_done, 1)
                v.tensor_tensor(gb[:, :], K.rows[:, 3, :], K.tab[:, 2, :], ALU.mult).then_inc(tab_done, 1)
                v.wait_ge(tab_done, 2)
                with v.Fori(0, G) as g:
                    v.tensor_tensor(four(K.X, g), four(K.X, g), over(gb[:, :]), ALU.add).then_inc(xb_done, 1)
                for q in range(4):
                    v.wait_ge(back[q], 16 * 16)
                    with v.Fori(4 * q, 4 * q + 4) as g:
                        v.tensor_tensor(four(K.U, g), four(K.U, g), four(zg, g), ALU.add).then_inc(sum_done, 1)
                    v.wait_ge(sum_done, 4 * q + 4)
                    with v.Fori(4 * q, 4 * q + 4) as g:
                        for j in range(4):
                            tile_stats(v, K, K.U, 4 * g + j, bn_done)
                v.wait_ge(bn_done, NT)
                finish_stats_vector(v, K, var_ready, std_ready, rstd_ready)
                v.wait_ge(xb_done, G)
                with v.Fori(0, G // 2) as i:
                    for s in range(2):
                        g = 2 * i + s
                        v.wait_ge(zm_ready, g + 1)
                        v.tensor_tensor(four(K.X, g), four(K.X, g), zm[:, s, :, :], ALU.add).then_inc(out_ready, 1)

            @block.scalar
            def _(act):
                finish_stats_scalar(act, K, var_ready, std_ready, rstd_ready)

                def normalise(g, s):
                    wait(act, zm_ready, g - 1)
                    for t in range(4):
                        act.activation(zn[:, s, t, :], K.U[:, ds(4 * g + t, 1), :].rearrange("p a f -> p (a f)"),
                                       ACT.Identity, bias=K.nmr[:, ds(4 * g + t, 1)],
                                       scale=K.rstd[:, ds(4 * g + t, 1)]).then_inc(zn_ready, 1)
                normalise(0, 0)
                normalise(1, 1)
                with act.Fori(1, G // 2) as i:
                    normalise(2 * i, 0)
                    normalise(2 * i + 1, 1)

            @block.sync
            def _(sp):
                xo = out.rearrange("b (n t) f -> t b n f", t=8)
                for q in range(4):
                    sp.wait_ge(out_ready, 4 * q + 4)
                    for t in range(8):
                        sp.dma_start(xo[t][:, 16 * q:16 * q + 16, :], K.X[16 * t:16 * t + 16, 16 * q:16 * q + 16, :])\
                          .then_inc(stored, 16)
                sp.wait_ge(stored, 32 * 16)




def constants():
    import numpy as np
    k = {}
    i = np.arange(P)
    k["k_ident"] = np.eye(P, dtype=np.float32)
    k["k_utri"] = (i[:, None] <= i[None, :]).astype(np.float32)
    k["k_ustrict"] = (i[:, None] < i[None, :]).astype(np.float32)
    k["k_centre"] = (np.eye(P) - (i[:, None] // D == i[None, :] // D) / D).astype(np.float32)
    k["k_blk"] = np.repeat((i[:, None] // D == np.arange(H)[None, :]).astype(np.float32), 9, axis=1)
    inv = (np.float32(1.0) / np.float32(10000.0) ** (np.arange(0, D, 2, dtype=np.float32) / np.float32(D))).astype(np.float32)
    freqs = (np.arange(T, dtype=np.float32)[:, None] * inv[None, :]).astype(np.float32)
    emb = np.concatenate([freqs, freqs], axis=-1)
    cos, sin = np.cos(emb).astype(np.float64), np.sin(emb).astype(np.float64)
    sin[:, :D // 2] *= -1.0
    gam = 1.0 - 2.0 ** (-5.0 - np.arange(H))
    t = np.arange(T)[:, None, None]
    up = gam[None, :, None] ** t * D ** -0.5
    down = gam[None, :, None] ** (-t)
    for name, f in (("k_rope_c", cos), ("k_rope_s", sin)):
        q = (f[:, None, :] * up).reshape(T, P)
        kk = (f[:, None, :] * down).reshape(T, P)
        k[name] = np.concatenate([q, kk], axis=1).astype(np.float32)
    g = (i[:, None] % 32) // 16 != (np.arange(32)[None, :] // 16)
    k["k_smask"] = np.where(g, NEG, 0.0).astype(np.float32)
    k["k_tie"] = np.tile((E - np.arange(E, dtype=np.float32))[None, :], (P, 1))
    k["k_iota"] = np.tile(np.arange(SLOTS, dtype=np.float32)[None, :], (P, 1))
    return k


_INS = ['L0_attn_x', 'L0_attn_w_attn', 'L0_attn_w_proj', 'L0_ffn_W_r', 'L0_ffn_W_k', 'L0_ffn_W_v', 'L0_ffn_mu_r',
        'L0_ffn_mu_k', 'L0_c', 'L0_wmod', 'L1_attn_Wq', 'L1_attn_Wk', 'L1_attn_Wv', 'L1_attn_Wg', 'L1_attn_Wo',
        'L1_attn_gn_w', 'L1_attn_gn_b', 'L1_ffn_Wqkv', 'L1_ffn_bqkv', 'L1_ffn_Wo', 'L1_ffn_bo', 'L1_ffn_g1',
        'L1_ffn_be1', 'L1_ffn_g2', 'L1_ffn_be2', 'L1_ffn_Wg', 'L1_ffn_W1', 'L1_ffn_b1', 'L1_ffn_W2', 'L1_ffn_b2',
        'L1_c', 'L1_wmod']


class Kept:
    pass


def build(nc, A, out):
    K = Kept()
    with ExitStack() as ctx:
        sb = lambda n, s, d=F32: ctx.enter_context(nc.sbuf_tensor(n, s, d))
        sem = lambda n: ctx.enter_context(nc.semaphore(n))
        K.X = sb("X", [P, NT, P])
        K.bn, K.diff, K.var, K.std = sb("bn", [P, NT, 6]), sb("diff", [P, NT]), sb("var", [P, NT]), sb("std", [P, NT])
        K.rstd, K.nmr, K.eps = sb("rstd", [P, NT]), sb("nmr", [P, NT]), sb("eps", [P, 1])
        K.ident, K.utri = sb("ident", [P, P]), sb("utri", [P, P])
        K.W = sb("W", [P, 11, P])
        K.wg8, K.cols, K.mod, K.tab = sb("wg8", [P, E]), sb("cols", [P, 7]), sb("mod", [P, 6, B]), sb("tab", [P, 3, P])
        K.bo, K.rows, K.smask = sb("bo", [P, P]), sb("rows", [P, 4, P]), sb("smask", [P, 32])
        K.w1, K.w2 = sb("w1", [P, E, DF]), sb("w2", [P, E, FC, P])
        K.x_in = [sem(f"x_in{g}") for g in range(4)]
        K.ys_zero = sem("ys_zero")
        with ExitStack() as early:
            sb2 = lambda n, s, d=F32: early.enter_context(nc.sbuf_tensor(n, s, d))
            K.wgate = sb2("wgate", [P, 3, B, P])
            K.wqkv0, K.wo1, K.cmat = sb2("wqkv0", [P, 3 * P]), sb2("wo1", [P, P]), sb2("cmat", [P, P])
            K.blk = sb2("blk", [P, H, 9])
            K.rope_c, K.rope_s = sb2("rope_c", [P, TPB, 2 * P]), sb2("rope_s", [P, TPB, 2 * P])
            prologue(nc, A, K)
            attention(nc, A, K, 0)
            token_shift_ffn(nc, A, K)
            attention(nc, A, K, 1)
        clear_semaphores(nc)
        K.U = sb("U", [P, NT, P])
        attend_batches(nc, A, K)
        clear_semaphores(nc)
        experts(nc, A, K, out)


def clear_semaphores(nc):
    released = sorted(nc.released_uncleared_semaphores)
    with nc.Block() as block:
        @block.gpsimd
        def _(pool):
            start = 0
            for i in range(1, len(released) + 1):
                if i == len(released) or released[i] != released[i - 1] + 1:
                    pool.sem_clear(range(released[start], released[i - 1] + 1))
                    start = i


def kernel(**inputs):
    import numpy as np
    import concourse.bacc as _bacc
    from concourse.bass_utils import run_bass_kernel_spmd as _run

    nc = _bacc.Bacc("TRN2", target_bir_lowering=False, num_devices=1)
    arrays, A = {}, {}
    for name in _INS:
        a = np.ascontiguousarray(inputs[name])
        arrays[f"in_{name}_dram"] = a
        A[name] = nc.dram_tensor(f"in_{name}_dram", a.shape, mybir.dt.from_np(a.dtype), kind="ExternalInput").ap()
    for name, a in constants().items():
        arrays[f"in_{name}_dram"] = a
        A[name] = nc.dram_tensor(f"in_{name}_dram", a.shape, mybir.dt.from_np(a.dtype), kind="ExternalInput").ap()
    A["xs"] = nc.dram_tensor("xs", (B * T, C), F32, kind="Internal").ap()
    A["ys"] = nc.dram_tensor("ys", (SLOTS * P, C), F32, kind="Internal").ap()
    A["zs"] = nc.dram_tensor("zs", (SLOTS * P, C), F32, kind="Internal").ap()
    out = nc.dram_tensor("out_0_dram", (B, T, C), F32, kind="ExternalOutput").ap()
    build(nc, A, out)
    r = _run(nc, [arrays], core_ids=[0])
    return r.results[0]["out_0_dram"]
```

```python
from contextlib import ExitStack

import concourse.bass as bass
from concourse import mybir

F32 = mybir.dt.float32
I32 = mybir.dt.int32
U32 = mybir.dt.uint32
ALU = mybir.AluOpType
ACT = mybir.ActivationFunctionType
AX = mybir.AxisListType

B, T, C = 16, 512, 128
P = 128
TPB = T // P
NT = B * TPB
H, D = 16, 8
EPS = 1e-5
EPS_DEN = 1e-6
GATE_MIN = 0.25
FH, FD = 4, 32
E, DF = 8, 512
FC = DF // P
SLOTS = 72
NEG = -1e30
ds = bass.ds

W_PROJT, W_RT, W_KT, W_Q1, W_K1, W_V1, W_G1, W_FQ, W_FK, W_FV, W_FO = range(11)
SA0, CA0, SB0, CB0, SA1, CA1 = range(6)
MU_R, MU_K, GN_W, GN_B, BQ, BK, BV = range(7)


def wait(e, sem, value):
    if isinstance(value, int) and value <= 0:
        return
    e.wait_ge(sem, value)


def prologue(nc, A, K):
    with ExitStack() as ctx:
        sb = lambda n, s, d=F32: ctx.enter_context(nc.sbuf_tensor(n, s, d))
        sem = lambda n: ctx.enter_context(nc.semaphore(n))
        ps = [ctx.enter_context(nc.psum_tensor(f"p0_{i}", [P, 512], F32)) for i in range(8)]
        craw = sb("craw", [32, P])
        wmod = [sb(f"wmod{l}", [P, 6 * P]) for l in range(2)]
        raw = sb("raw", [P, 12, P])
        raw8 = sb("raw8", [E, P])
        sc = sb("sc", [P, 32])
        sc_rep = sb("sc_rep", [P, 8, 16])
        gates = sb("gates", [P, 3, 16])
        bv_rep = sb("bv_rep", [P, P])
        bo_row = sb("bo_row", [P, P])
        diag = sb("diag", [P, 2, 4, P])
        zeros = sb("zeros", [P, 9 * P])
        ct = [sb(f"ct{i}", [P, P]) for i in range(3)]
        cg = [sb(f"cg{i}", [P, 48]) for i in range(3)]

        s_c, s_w, s_v, s_tab = sem("s_c"), sem("s_w"), sem("s_v"), sem("s_tab")
        silu_done, crep, csT = sem("silu_done"), sem("crep"), sem("csT")
        mod_ps, mod_done, gate_done = sem("mod_ps"), sem("mod_done"), sem("gate_done")
        chain, tab_ps = sem("chain0"), sem("tab_ps")
        wt_ps, wt_done = sem("wt_ps"), sem("wt_done")
        diag_done, wg_ps, wg_done = sem("diag_done"), sem("wg_ps"), sem("wg_done")
        bo_ps, vrep, zset, stats = sem("bo_ps"), sem("vrep"), sem("zset"), sem("stats0")
        ident_in = sem("ident_in")

        col = lambda v: v.rearrange("(p a) -> p a", a=1)
        row = lambda v: v.rearrange("(a n) -> a n", a=1)

        raws = [A["L0_attn_w_proj"], A["L0_ffn_W_r"], A["L0_ffn_W_k"], A["L1_attn_Wq"], A["L1_attn_Wk"],
                A["L1_attn_Wv"], A["L1_attn_Wg"], A["L1_ffn_Wqkv"][0:P, :], A["L1_ffn_Wqkv"][P:2 * P, :],
                A["L1_ffn_Wqkv"][2 * P:3 * P, :], A["L1_ffn_Wo"], A["L0_ffn_W_v"]]

        with nc.Block() as block:
            @block.sync
            def _(sp):
                sp.dma_start(craw[0:16, :], A["L0_c"]).then_inc(s_c, 16)
                sp.dma_start(craw[16:32, :], A["L1_c"]).then_inc(s_c, 16)
                sp.dma_start(K.ident[:, :], A["k_ident"]).then_inc(ident_in, 16)
                for l in range(2):
                    sp.dma_start(wmod[l][:, :], A[f"L{l}_wmod"]).then_inc(s_c, 16)
                for i, w in enumerate(raws):
                    sp.dma_start(raw[:, i, :], w).then_inc(s_w, 16)
                sp.dma_start(raw8[:, :], A["L1_ffn_Wg"]).then_inc(s_w, 16)
                sp.dma_start(K.wo1[:, :], A["L1_attn_Wo"]).then_inc(s_w, 16)
                sp.dma_start(K.cmat[:, :], A["k_centre"]).then_inc(s_w, 16)
                for g in range(4):
                    sp.dma_start(K.X[:, 16 * g:16 * g + 16, :],
                                 A["L0_attn_x"].rearrange("b (t p) f -> p (b t) f", p=P)[:, 16 * g:16 * g + 16, :])\
                      .then_inc(K.x_in[g], 16)
                sp.wait_ge(s_v, 8 * 16)
                sp.wait_ge(s_tab, 12 * 16)
                sp.wait_ge(zset, 1)
                for g in range(8):
                    sp.dma_start(A["ys"].rearrange("(p r) f -> p (r f)", p=P)[:, 9 * P * g:9 * P * g + 9 * P],
                                 zeros[:, :]).then_inc(K.ys_zero, 16)
                sp.wait_ge(K.ys_zero, 8 * 16)

            @block.scalar
            def _(act):
                vecs = [A["L0_ffn_mu_r"], A["L0_ffn_mu_k"], A["L1_attn_gn_w"], A["L1_attn_gn_b"],
                        A["L1_ffn_bqkv"][0:P], A["L1_ffn_bqkv"][P:2 * P], A["L1_ffn_bqkv"][2 * P:3 * P]]
                for i, v in enumerate(vecs):
                    act.dma_start(K.cols[:, i:i + 1], col(v)).then_inc(s_v, 16)
                act.dma_start(bo_row[:, :], row(A["L1_ffn_bo"]).to_broadcast([P, P])).then_inc(s_v, 16)
                act.dma_start(K.wqkv0[:, :], A["L0_attn_w_attn"]).then_inc(s_tab, 16)
                act.dma_start(K.utri[:, :], A["k_utri"]).then_inc(s_tab, 16)
                act.dma_start(K.blk[:, :, :], A["k_blk"].rearrange("p (h j) -> p h j", h=H)).then_inc(s_tab, 16)
                act.dma_start(K.rope_c[:, :, :], A["k_rope_c"].rearrange("(t p) n -> p t n", p=P)).then_inc(s_tab, 16)
                act.dma_start(K.rope_s[:, :, :], A["k_rope_s"].rearrange("(t p) n -> p t n", p=P)).then_inc(s_tab, 16)
                act.dma_start(K.smask[:, :], A["k_smask"]).then_inc(s_tab, 16)
                for i, v in enumerate(("g1", "be1", "g2", "be2")):
                    act.dma_start(K.rows[:, i, :], row(A["L1_ffn_" + v]).to_broadcast([P, P])).then_inc(s_tab, 16)
                act.dma_start(K.w1[:, :, :], A["L1_ffn_W1"].rearrange("e d f -> d e f")).then_inc(s_tab, 16)
                act.dma_start(K.w2[:, :, :, :], A["L1_ffn_W2"].rearrange("e (c p) f -> p e c f", p=P)).then_inc(s_tab, 16)
                act.wait_ge(csT, 1)
                act.activation(sc[:, :], ps[0][:, 0:32], ACT.Silu).then_inc(silu_done, 1)
                for g in range(3):
                    n = min(4, 11 - 4 * g)
                    act.wait_ge(wt_ps, g + 1)
                    act.activation(K.W[:, 4 * g:4 * g + n, :].rearrange("p a b -> p (a b)"), ps[2 + g][:, 0:n * P],
                                   ACT.Copy).then_inc(wt_done, 1)
                act.wait_ge(wt_ps, 4)
                act.activation(K.wg8[:, :], ps[5][:, 0:E], ACT.Copy).then_inc(wt_done, 1)
                for g in range(12):
                    act.wait_ge(wg_ps, g + 1)
                    act.activation(K.wgate[:, g // 4, 4 * (g % 4):4 * (g % 4) + 4, :].rearrange("p a b -> p (a b)"),
                                   ps[6 + g % 2][:, :], ACT.Copy).then_inc(wg_done, 1)

            @block.tensor
            def _(pe):
                pe.wait_ge(s_c, 64)
                pe.wait_ge(ident_in, 16)
                pe.transpose(ps[0][:, 0:32], craw[:, :], K.ident[0:32, 0:32]).then_inc(csT, 1)
                pe.wait_ge(silu_done, 1)
                kinds = [(0, 0), (0, 1), (0, 3), (0, 4), (1, 0), (1, 1), (0, 2), (0, 5), (1, 2)]
                for i, (l, k) in enumerate(kinds):
                    mm = pe.matmul(ps[1][:, 16 * i:16 * i + 16], wmod[l][:, k * P:(k + 1) * P],
                                   sc[:, 16 * l:16 * l + 16], start=True, stop=True)
                mm.then_inc(mod_ps, 1)
                pe.wait_ge(crep, 1)
                pe.matmul(ps[0][:, 0:3 * P], sc_rep[:, :, :].rearrange("p a b -> p (a b)"),
                          wmod[1][:, 3 * P:6 * P], start=True, stop=True).then_inc(tab_ps, 1)
                pe.wait_ge(s_w, 15 * 16)
                for i in range(11):
                    o = ps[2 + i // 4][:, (i % 4) * P:(i % 4 + 1) * P]
                    if i == W_V1:
                        mm = pe.matmul(o, raw[:, i, :], K.cmat[:, :], start=True, stop=True)
                    else:
                        mm = pe.transpose(o, raw[:, i, :], K.ident[:, :])
                    if i % 4 == 3 or i == 10:
                        mm.then_inc(wt_ps, 1)
                pe.transpose(ps[5][:, 0:E], raw8[:, :], K.ident[0:E, 0:E]).then_inc(wt_ps, 1)
                pe.wait_ge(wt_done, 4)
                pe.wait_ge(vrep, 1)
                pe.matmul(ps[5][:, P:2 * P], bv_rep[:, :], K.W[:, W_FO, :], start=True, stop=True).then_inc(bo_ps, 1)
                lhs = [K.W[:, W_PROJT, :], raw[:, 11, :], K.wo1[:, :]]
                for g in range(12):
                    pe.wait_ge(diag_done, g + 1)
                    if g >= 2:
                        pe.wait_ge(wg_done, g - 1)
                    for j in range(4):
                        mm = pe.matmul(ps[6 + g % 2][:, j * P:(j + 1) * P], lhs[g // 4], diag[:, g % 2, j, :],
                                       start=True, stop=True)
                    mm.then_inc(wg_ps, 1)

            @block.gpsimd
            def _(pool):
                pool.memset(zeros[:, :], 0.0).then_inc(zset, 1)
                pool.memset(K.eps[:, :], EPS).then_inc(zset, 1)

            @block.vector
            def _(v):
                count = [0]

                def link(ins):
                    count[0] += 1
                    ins.then_inc(chain, 1)
                    v.wait_ge(chain, count[0])

                def clamp(out, x, tmp):
                    link(v.scalar_tensor_tensor(out=tmp[0], in0=x, scalar=-1.0, in1=x, op0=ALU.mult, op1=ALU.max))
                    link(v.tensor_scalar(tmp[1], x, 0.0, 2.0, ALU.is_ge, ALU.mult))
                    link(v.tensor_scalar(tmp[0], tmp[0], GATE_MIN, None, ALU.max))
                    link(v.scalar_tensor_tensor(out=out, in0=tmp[1], scalar=-1.0, in1=tmp[0],
                                                op0=ALU.add, op1=ALU.mult))

                v.wait_ge(silu_done, 1)
                v.tensor_copy(sc_rep[:, :, :], sc[:, 16:32].unsqueeze(1).to_broadcast([P, 8, 16])).then_inc(crep, 1)
                v.wait_ge(s_v, 8 * 16)
                v.tensor_copy(bv_rep[:, :], K.cols[:, BV:BV + 1].to_broadcast([P, P])).then_inc(vrep, 1)
                v.wait_ge(mod_ps, 1)
                v.tensor_copy(K.mod[:, :, :].rearrange("p k b -> p (k b)"), ps[1][:, 0:96]).then_inc(mod_done, 1)
                link(v.tensor_copy(cg[2][:, :], ps[1][:, 96:144]))
                v.wait_ge(mod_done, 1)
                for k in (CA0, CB0, CA1):
                    link(v.tensor_scalar(K.mod[:, k, :], K.mod[:, k, :], 1.0, None, ALU.add))
                clamp(gates[:, :, :].rearrange("p k b -> p (k b)"), cg[2][:, :], [cg[0][:, :], cg[1][:, :]])
                for g in range(12):
                    if g >= 2:
                        v.wait_ge(wg_ps, g - 1)
                    v.tensor_tensor(diag[:, g % 2, :, :], K.ident[:, :].unsqueeze(1).to_broadcast([P, 4, P]),
                                    gates[:, g // 4, 4 * (g % 4):4 * (g % 4) + 4].unsqueeze(2).to_broadcast([P, 4, P]),
                                    ALU.mult).then_inc(diag_done, 1)
                v.wait_ge(tab_ps, 1)
                link(v.tensor_copy(K.tab[:, 0, :], ps[0][:, 0:P]))
                link(v.tensor_scalar(K.tab[:, 1, :], ps[0][:, P:2 * P], 1.0, None, ALU.add))
                link(v.tensor_copy(ct[2][:, :], ps[0][:, 2 * P:3 * P]))
                clamp(K.tab[:, 2, :], ct[2][:, :], [ct[0][:, :], ct[1][:, :]])
                v.wait_ge(bo_ps, 1)
                link(v.tensor_tensor(K.bo[:, :], ps[5][:, P:2 * P], bo_row[:, :], ALU.add))
                for g in range(4):
                    v.wait_ge(K.x_in[g], 16)
                    with v.Fori(4 * g, 4 * g + 4) as q:
                        for j in range(4):
                            tile_stats(v, K, K.X, 4 * q + j, stats)


def finish_stats_vector(v, K, var_ready, std_ready, rstd_ready, part=0, parts=1):
    n = slice(part * NT // parts, (part + 1) * NT // parts)
    mean0, m20, mean1, m21 = (K.bn[:, n, i] for i in (1, 2, 4, 5))
    v.tensor_tensor(K.diff[:, n], mean0, mean1, ALU.subtract).then_inc(var_ready, 1)
    v.tensor_tensor(K.var[:, n], m20, m21, ALU.add).then_inc(var_ready, 1)
    v.wait_ge(var_ready, 5 * part + 2)
    v.scalar_tensor_tensor(out=K.std[:, n], in0=K.diff[:, n], scalar=P / 4.0, in1=K.diff[:, n],
                           op0=ALU.mult, op1=ALU.mult).then_inc(var_ready, 1)
    v.wait_ge(var_ready, 5 * part + 3)
    v.tensor_tensor(K.var[:, n], K.var[:, n], K.std[:, n], ALU.add).then_inc(var_ready, 1)
    v.tensor_tensor(K.diff[:, n], mean0, mean1, ALU.add).then_inc(var_ready, 1)
    v.wait_ge(std_ready, part + 1)
    v.reciprocal(K.rstd[:, n], K.std[:, n]).then_inc(rstd_ready, 1)
    v.wait_ge(rstd_ready, 2 * part + 1)
    v.wait_ge(var_ready, 5 * part + 5)
    v.scalar_tensor_tensor(out=K.nmr[:, n], in0=K.diff[:, n], scalar=-0.5, in1=K.rstd[:, n],
                           op0=ALU.mult, op1=ALU.mult).then_inc(rstd_ready, 1)


def finish_stats_scalar(act, K, var_ready, std_ready, rstd_ready, part=0, parts=1):
    n = slice(part * NT // parts, (part + 1) * NT // parts)
    act.wait_ge(var_ready, 5 * part + 4)
    act.activation(K.std[:, n], K.var[:, n], ACT.Sqrt, bias=K.eps[:, 0:1], scale=1.0 / P).then_inc(std_ready, 1)
    act.wait_ge(rstd_ready, 2 * part + 2)


def tile_stats(v, K, x, n, done):
    v.bn_stats(K.bn[:, ds(n, 1), :].rearrange("p a f -> p (a f)"), x[:, ds(n, 1), :].rearrange("p a f -> p (a f)"))\
     .then_inc(done, 1)


def attention(nc, A, K, layer):
    J = 9 if layer == 0 else 8
    SC = D * J
    heads = [(0, 6), (6, 11), (11, 16)]
    banks_halved = 3 if layer == 0 else 2
    HH = heads[banks_halved - 1][1]
    sh, scl = (SA0, CA0) if layer == 0 else (SA1, CA1)
    with ExitStack() as ctx:
        sb = lambda n, s, d=F32: ctx.enter_context(nc.sbuf_tensor(f"a{layer}_{n}", s, d))
        sem = lambda n: ctx.enter_context(nc.semaphore(f"a{layer}_{n}"))
        pb = lambda n: ctx.enter_context(nc.psum_tensor(f"a{layer}_{n}", [P, 512], F32))
        pS = [pb(f"pS{c}") for c in range(3)]
        pR, pT, pQ, pI, pO = pb("pR"), pb("pT"), pb("pQ"), pb("pI"), pb("pO")

        xn = sb("xn", [P, TPB, P])
        hT = sb("hT", [P, TPB * P])
        qk = sb("qk", [P, TPB, 2 * P])
        vv = sb("vv", [P, TPB, H, J])
        kv = sb("kv", [P, 2, H, D, J])
        tt = sb("tt", [P, 2, H, D + 1, J])
        R = sb("R", [P, H, J])
        qT = sb("qT", [P, P])
        nd = sb("nd", [P, 2, H, J])
        rec = sb("rec", [P, H])
        y = sb("y", [P, P])
        yT = sb("yT", [P, P])
        if layer == 0:
            ea = sb("ea", [P, 2, 2 * P])
            eb = sb("eb", [P, 2, 2 * P])
            den = sb("den", [P, H])
            wqkv = K.wqkv0[:, :]
        else:
            ra = sb("ra", [P, 2, 2 * P])
            rb = sb("rb", [P, 2, 2 * P])
            gate = sb("gate", [P, 2 * T])
            sq = sb("sq", [P, P])
            vs = sb("vs", [P, H])
            sd = sb("sd", [P, H])
            yaff = sb("yaff", [P, P])
            wqkv = K.W[:, W_Q1:W_V1 + 1, :].rearrange("p a b -> p (a b)")

        var_ready, std_ready, rstd_ready = sem("var"), sem("std"), sem("rstd")
        half_done = sem("half_done")
        xn_ready, xn_T, hT_ready = sem("xn_ready"), sem("xn_T"), sem("hT_ready")
        qkv_ps, v_ready, e_ready, qk_ready = sem("qkv_ps"), sem("v_ready"), sem("e_ready"), sem("qk_ready")
        ones_set, relu_done = sem("ones_set"), sem("relu_done")
        gate_ps, gate_ready, rope_read, rope_b = sem("gate_ps"), sem("gate_ready"), sem("rope_read"), sem("rope_b")
        kv_ready, u_done, t_done, red_done = sem("kv_ready"), sem("u_done"), sem("t_done"), sem("red_done")
        p_done, r_ready, q_T, qT_ready = sem("p_done"), sem("r_ready"), sem("q_T"), sem("qT_ready")
        inter_ps, inter_ready = sem("inter_ps"), sem("inter_ready")
        den_done, rec_done, y_ready, y_T, yT_ready = (sem("den_done"), sem("rec_done"), sem("y_ready"),
                                                      sem("y_T"), sem("yT_ready"))
        aff_done, sq_done, var_done, sd_done = sem("aff_done"), sem("sq_done"), sem("var_done"), sem("sd_done")
        proj_ps, x_done, bn_done, x_out = sem("proj_ps"), sem("x_done"), sem("bn_done"), sem("x_out")

        YT = P + H * J
        yT_read = yT_ready if layer == 0 else aff_done
        qk_free = qk_ready if layer == 0 else rope_read

        def tile(t, n):
            return t[:, ds(n, 1), :].rearrange("p a f -> p (a f)")

        def column(t, n):
            return t[:, ds(n, 1)]

        def near(b, t, d):
            if isinstance(b, int) and not 0 <= 4 * b + t + d < NT:
                return None
            return b + (t + d) // 4, (t + d) % 4


        def act_normalise(act, b, t):
            wait(act, xn_T, 4 * b - 3 + t)
            act.activation(xn[:, t, :], tile(K.X, 4 * b + t), ACT.Identity, bias=column(K.nmr, 4 * b + t),
                           scale=column(K.rstd, 4 * b + t)).then_inc(xn_ready, 1)

        def pe_transpose_x(pe, b):
            for t in range(TPB):
                pe.wait_ge(xn_ready, 4 * b + t + 1)
                if t == 0:
                    wait(pe, hT_ready if layer == 0 else gate_ready, b)
                pe.transpose(pT[:, t * P:(t + 1) * P], xn[:, t, :], K.ident[:, :]).then_inc(xn_T, 1)

        def act_modulate(act, b):
            act.wait_ge(xn_T, 4 * b + 4)
            wait(act, qkv_ps, 4 * b)
            if layer == 1:
                wait(act, gate_ps, b)
            act.activation(hT[:, :], pT[:, :], ACT.Identity, bias=column(K.mod[:, sh, :], b),
                           scale=column(K.mod[:, scl, :], b)).then_inc(hT_ready, 1)

        def pe_qkv(pe, b, t):
            m = 4 * b + t
            pe.wait_ge(hT_ready, b + 1)
            wait(pe, v_ready, m)
            wait(pe, qk_free, m)
            pe.matmul(pQ[:, 0:3 * P], hT[:, t * P:(t + 1) * P], wqkv, start=True, stop=True).then_inc(qkv_ps, 1)

        def act_qkv(act, b, t):
            m = 4 * b + t
            act.wait_ge(qkv_ps, m + 1)
            wait(act, kv_ready, m - 3)
            if t < 3:
                wait(act, p_done, 3 * b - 3 + t + 1)
            act.activation(vv[:, t, :, 0:D], pQ[:, 2 * P:3 * P].rearrange("p (h j) -> p h j", h=H),
                           ACT.Copy).then_inc(v_ready, 1)
            if layer == 0:
                wait(act, e_ready, m - 1)
                act.activation(ea[:, t % 2, :], pQ[:, 0:2 * P], ACT.Relu, scale=-1.0).then_inc(relu_done, 1)
                act.wait_ge(relu_done, m + 1)
                wait(act, qk_ready, m - 1)
                act.activation(eb[:, t % 2, :], ea[:, t % 2, :], ACT.Exp, scale=-1.0).then_inc(e_ready, 1)

        def slot_free(e, b, t):
            m = 4 * b + t
            wait(e, kv_ready, m - 3)
            wait(e, t_done, 3 * (m - 3))
            if t < 3:
                wait(e, p_done, 3 * b - 3 + t + 1)
            if t > 0:
                wait(e, q_T, 3 * b - 3 + t)

        def vec_qk(v, b, t):
            m = 4 * b + t
            if layer == 0:
                v.wait_ge(e_ready, m + 1)
                v.wait_ge(v_ready, m + 1)
                slot_free(v, b, t)
                v.scalar_tensor_tensor(out=qk[:, t, :], in0=pQ[:, 0:2 * P], scalar=1.0, in1=eb[:, t % 2, :],
                                       op0=ALU.add, op1=ALU.max).then_inc(qk_ready, 1)
            else:
                v.wait_ge(v_ready, m + 1)
                wait(v, qk_ready, m - 1)
                v.tensor_tensor(ra[:, t % 2, :], pQ[:, 0:2 * P], K.rope_c[:, t, :], ALU.mult).then_inc(rope_b, 1)
                pv = pQ[:, 0:2 * P].rearrange("p (g u i) -> p g u i", u=2, i=D // 2)
                rv = rb[:, t % 2, :].rearrange("p (g u i) -> p g u i", u=2, i=D // 2)
                sv = K.rope_s[:, t, :].rearrange("p (g u i) -> p g u i", u=2, i=D // 2)
                v.tensor_tensor(rv[:, :, 0, :], pv[:, :, 1, :], sv[:, :, 0, :], ALU.mult).then_inc(rope_b, 1)
                v.tensor_tensor(rv[:, :, 1, :], pv[:, :, 0, :], sv[:, :, 1, :], ALU.mult).then_inc(rope_read, 1)

        def pool_rope(pool, b, t):
            m = 4 * b + t
            pool.wait_ge(rope_read, m + 1)
            pool.wait_ge(rope_b, 2 * m + 2)
            slot_free(pool, b, t)
            pool.tensor_tensor(qk[:, t, :], ra[:, t % 2, :], rb[:, t % 2, :], ALU.add).then_inc(qk_ready, 1)

        def pool_kv(pool, n, t):
            pool.wait_ge(qk_ready, n + 1)
            pool.wait_ge(v_ready, n + 1)
            wait(pool, u_done, 3 * (n - 1))
            kk = qk[:, t, P:2 * P].rearrange("p (h i) -> p h i", h=H)
            pool.tensor_tensor(kv[:, t % 2, :, :, :], kk.unsqueeze(3).to_broadcast([P, H, D, J]),
                               vv[:, t, :, :].unsqueeze(2).to_broadcast([P, H, D, J]), ALU.mult).then_inc(kv_ready, 1)

        def pe_states(pe, b, t):
            n = 4 * b + t
            pe.wait_ge(kv_ready, n + 1)
            flat = kv[:, t % 2, :, :, :].rearrange("p h i j -> p (h i j)")
            for c, (h0, h1) in enumerate(heads):
                wait(pe, t_done, 3 * (n - 1) + c + 1)
                pe.matmul(pS[c][:, 0:(h1 - h0) * SC], K.utri[:, :], flat[:, h0 * SC:h1 * SC],
                          start=True, stop=True).then_inc(u_done, 1)

        def pe_inter(pe, b, t):
            pe.wait_ge(qT_ready, 3 * b + t)
            pe.wait_ge(r_ready, 3 * b + t)
            wait(pe, yT_read, 4 * b + t - 2)
            pe.matmul(pI[:, P:P + H * J], qT[:, :], R[:, :, :].rearrange("p h j -> p (h j)"),
                      start=True, stop=True).then_inc(inter_ps, 1)

        def pe_state_sum(pe, b, t):
            wait(pe, r_ready, 3 * b + t)
            pe.wait_ge(v_ready, 4 * b + t + 1)
            pe.matmul(pR[:, 0:H * J], qk[:, t, P:2 * P], vv[:, t, :, :].rearrange("p h j -> p (h j)"),
                      start=(t == 0), stop=True, skip_group_check=True).then_inc(p_done, 1)

        def pe_transpose_q(pe, b, t):
            pe.wait_ge(qk_ready, 4 * b + t + 1)
            wait(pe, inter_ready, 3 * b + t - 1)
            pe.transpose(pI[:, 0:P], qk[:, t, 0:P], K.ident[:, :]).then_inc(q_T, 1)

        def pe_transpose_y(pe, b, t):
            m = 4 * b + t
            pe.wait_ge(y_ready, m + 1)
            if t != 2 and near(b, t, 2):
                pe.wait_ge(inter_ready, 3 * b + (2, 3, None, 4)[t])
            else:
                wait(pe, yT_read, m)
            pe.transpose(pI[:, YT:YT + P], y[:, :], K.ident[:, :]).then_inc(y_T, 1)

        def pe_project(pe, b, t):
            m = 4 * b + t
            pe.wait_ge(yT_ready, m + 1)
            wait(pe, x_done, m)
            pe.matmul(pO[:, 0:P], yT[:, :], tile(K.wgate[:, 0 if layer == 0 else 2, :, :], b),
                      start=True, stop=True).then_inc(proj_ps, 1)

        def act_inter(act, b, t):
            n = 4 * b + t
            act.wait_ge(inter_ps, 3 * b + t)
            wait(act, red_done, n - 1)
            act.activation(tt[:, t % 2, :, D, :], pI[:, P:P + H * J].rearrange("p (h j) -> p h j", h=H),
                           ACT.Copy).then_inc(inter_ready, 1)

        def act_qT(act, b, t):
            act.wait_ge(q_T, 3 * b + t)
            wait(act, inter_ps, 3 * b + t - 1)
            act.activation(qT[:, :], pI[:, 0:P], ACT.Copy).then_inc(qT_ready, 1)

        def act_yT(act, b, t):
            m = 4 * b + t
            act.wait_ge(y_T, m + 1)
            if layer == 0:
                wait(act, proj_ps, m)
                act.activation(yT[:, :], pI[:, YT:YT + P], ACT.Copy).then_inc(yT_ready, 1)
            else:
                wait(act, yT_ready, m)
                act.activation(yaff[:, :], pI[:, YT:YT + P], ACT.Identity, bias=K.cols[:, GN_B:GN_B + 1],
                               scale=K.cols[:, GN_W:GN_W + 1]).then_inc(aff_done, 1)

        def pool_gate(pool, b, t, half):
            m = 4 * b + t
            pool.wait_ge(aff_done, m + 1)
            pool.wait_ge(gate_ready, b + 1)
            wait(pool, proj_ps, m)
            pool.tensor_tensor(yT[:, :], yaff[:, :], gate[:, half * T + t * P:half * T + (t + 1) * P],
                               ALU.mult).then_inc(yT_ready, 1)

        def vec_products(v, b, t):
            n = 4 * b + t
            q = qk[:, t, 0:P].rearrange("p (h i) -> p h i", h=H)
            wait(v, red_done, n - 1)
            for c, (h0, h1) in enumerate(heads):
                v.wait_ge(u_done, 3 * n + c + 1)
                v.tensor_tensor(tt[:, t % 2, h0:h1, 0:D, :],
                                pS[c][:, 0:(h1 - h0) * SC].rearrange("p (h i j) -> p h i j", i=D, j=J),
                                q[:, h0:h1, :].unsqueeze(3).to_broadcast([P, h1 - h0, D, J]),
                                ALU.mult).then_inc(t_done, 1)

        def vec_state(v, b, t):
            v.wait_ge(p_done, 3 * b + t + 1)
            wait(v, inter_ps, 3 * b + t)
            v.tensor_tensor(R[:, :, :], pR[:, 0:H * J].rearrange("p (h j) -> p h j", h=H), K.blk[:, :, 0:J],
                            ALU.mult).then_inc(r_ready, 1)

        def pool_halve(pool, b, t):
            n = 4 * b + t
            pool.wait_ge(t_done, 3 * n + banks_halved)
            pool.tensor_tensor(tt[:, t % 2, 0:HH, D // 2:D, :], tt[:, t % 2, 0:HH, D // 2:D, :],
                               tt[:, t % 2, 0:HH, 0:D // 2, :], ALU.add).then_inc(half_done, 1)

        def vec_sum(v, b, t):
            n = 4 * b + t
            v.wait_ge(half_done, n + 1)
            v.wait_ge(t_done, 3 * n + 3)
            rows = D
            if t > 0:
                v.wait_ge(inter_ready, 3 * b + t)
                rows = D + 1
            wait(v, y_ready, n - 1)
            for h0, h1, first in ((0, HH, D // 2), (HH, H, 0)):
                if h0 < h1:
                    red = v.tensor_reduce(nd[:, t % 2, h0:h1, :], tt[:, t % 2, h0:h1, first:rows, :]
                                          .rearrange("p h i j -> p h j i"), AX.X, ALU.add)
            red.then_inc(red_done, 1)

        def vec_den(v, n, t):
            v.wait_ge(red_done, n + 1)
            wait(v, rec_done, n)
            v.tensor_scalar(den[:, :], nd[:, t % 2, :, D], EPS_DEN, None, ALU.add).then_inc(den_done, 1)

        def act_square(act, b, t):
            n = 4 * b + t
            act.wait_ge(red_done, n + 1)
            wait(act, var_done, n)
            act.activation(sq[:, :], nd[:, t % 2, :, :].rearrange("p h j -> p (h j)"), ACT.Square)\
               .then_inc(sq_done, 1)

        def act_sd(act, b, t):
            n = 4 * b + t
            act.wait_ge(var_done, n + 1)
            wait(act, rec_done, n)
            act.activation(sd[:, :], vs[:, :], ACT.Sqrt, bias=K.eps[:, 0:1], scale=1.0 / D).then_inc(sd_done, 1)

        def vec_var(v, n):
            v.wait_ge(sq_done, n + 1)
            wait(v, sd_done, n)
            v.tensor_reduce(vs[:, :], sq[:, :].rearrange("p (h j) -> p h j", h=H), AX.X, ALU.add)\
             .then_inc(var_done, 1)

        def vec_rec(v, n):
            wait(v, y_ready, n)
            if layer == 0:
                v.wait_ge(den_done, n + 1)
                v.reciprocal(rec[:, :], den[:, :]).then_inc(rec_done, 1)
            else:
                v.wait_ge(sd_done, n + 1)
                v.reciprocal(rec[:, :], sd[:, :]).then_inc(rec_done, 1)

        def vec_y(v, n, t):
            v.wait_ge(rec_done, n + 1)
            wait(v, y_T, n)
            v.tensor_tensor(y[:, :].rearrange("p (h j) -> p h j", h=H), nd[:, t % 2, :, 0:D],
                            rec[:, :].unsqueeze(2).to_broadcast([P, H, D]), ALU.mult).then_inc(y_ready, 1)

        def vec_residual(v, b, t):
            m = 4 * b + t
            v.wait_ge(proj_ps, m + 1)
            wait(v, x_done, m)
            x = tile(K.X, m)
            v.tensor_tensor(x, pO[:, 0:P], x, ALU.add).then_inc(x_done, 1)


        def act_gate(act, b, half):
            act.wait_ge(gate_ps, b + 1)
            wait(act, yT_ready, 4 * (b - 1))
            act.activation(gate[:, half * T:(half + 1) * T], pT[:, :], ACT.Silu).then_inc(gate_ready, 1)

        def pe_gate(pe, b):
            pe.wait_ge(hT_ready, b + 1)
            pe.matmul(pT[:, :], K.W[:, W_G1, :], hT[:, :], start=True, stop=True).then_inc(gate_ps, 1)

        def pe_batch(pe, b, last=False):
            for t in range(TPB):
                pe_states(pe, b, t)
                if t > 0:
                    pe_inter(pe, b, t)
                if t < 3:
                    pe_state_sum(pe, b, t)
                if not last:
                    pe_qkv(pe, b + 1, t)
                if near(b, t, -3):
                    pe_project(pe, *near(b, t, -3))
                if not last:
                    if layer == 1 and t == 1:
                        pe_gate(pe, b + 1)
                if near(b, t, -2):
                    pe_transpose_y(pe, *near(b, t, -2))
                if t < 3:
                    pe_transpose_q(pe, b, t + 1)
                if t == 3 and not last and not (isinstance(b, int) and b == B - 2):
                    pe_transpose_x(pe, b + 2)

        def act_batch(act, b, half, last=False, more=True):
            for t in range(TPB):
                if t == 0 and not last:
                    act_modulate(act, b + 1)
                if t > 0:
                    act_inter(act, b, t)
                if more:
                    act_normalise(act, b + 2, t)
                if not last:
                    act_qkv(act, b + 1, t)
                if layer == 1 and near(b, t, -1):
                    act_square(act, *near(b, t, -1))
                if t < 3:
                    act_qT(act, b, t + 1)
                if near(b, t, -2):
                    act_yT(act, *near(b, t, -2))
                if layer == 5 and t == 3 and more:
                    act_modulate(act, b + 2)
                if layer == 1:
                    if near(b, t, -1):
                        act_sd(act, *near(b, t, -1))
                    if t == 2 and not last:
                        act_gate(act, b + 1, 1 - half)

        def vec_batch(v, b, last=False):
            for t in range(TPB):
                before, out, done = near(b, t, -1), near(b, t, -3), near(b, t, -4)
                vec_products(v, b, t)
                if before:
                    vec_sum(v, *before)
                if layer == 0:
                    if t < 3:
                        vec_state(v, b, t)
                    if before:
                        vec_den(v, 4 * before[0] + before[1], before[1])
                if not last:
                    vec_qk(v, b + 1, t)
                if before:
                    if layer == 1:
                        vec_var(v, 4 * before[0] + before[1])
                    else:
                        vec_rec(v, 4 * before[0] + before[1])
                if layer == 1 and t < 3:
                    vec_state(v, b, t)
                if out:
                    vec_residual(v, *out)
                if before:
                    if layer == 1:
                        vec_rec(v, 4 * before[0] + before[1])
                    vec_y(v, 4 * before[0] + before[1], before[1])
                if layer == 0 and done:
                    tile_stats(v, K, K.X, 4 * done[0] + done[1], bn_done)

        def pool_batch(pool, b, half, last=False):
            for t in range(TPB):
                if not (last and t == 3):
                    pool_kv(pool, 4 * b + t + 1, (t + 1) % 4)
                if layer == 1:
                    if near(b, t, -3):
                        pool_gate(pool, *near(b, t, -3), half if t == 3 else 1 - half)
                    if near(b, t, 3):
                        pool_rope(pool, *near(b, t, 3))
                pool_halve(pool, b, t)

        with nc.Block() as block:
            @block.tensor
            def _(pe):
                pe_transpose_x(pe, 0)
                for t in range(TPB):
                    pe_qkv(pe, 0, t)
                if layer == 1:
                    pe_gate(pe, 0)
                pe_transpose_x(pe, 1)
                pe_batch(pe, 0)
                with pe.Fori(1, B - 2) as b:
                    pe_batch(pe, b)
                pe_batch(pe, B - 2)
                pe_batch(pe, B - 1, last=True)
                pe_project(pe, B - 1, 1)
                pe_transpose_y(pe, B - 1, 2)
                pe_project(pe, B - 1, 2)
                pe_transpose_y(pe, B - 1, 3)
                pe_project(pe, B - 1, 3)

            @block.scalar
            def _(act):
                finish_stats_scalar(act, K, var_ready, std_ready, rstd_ready)
                act.wait_ge(ones_set, 1)
                for t in range(TPB):
                    act_normalise(act, 0, t)
                act_modulate(act, 0)
                for t in range(TPB):
                    act_qkv(act, 0, t)
                if layer == 1:
                    act_gate(act, 0, 0)
                for t in range(TPB):
                    act_normalise(act, 1, t)
                act_batch(act, 0, 0)
                with act.Fori(0, B // 2 - 2) as i:
                    act_batch(act, 2 * i + 1, 1)
                    act_batch(act, 2 * i + 2, 0)
                act_batch(act, B - 3, 1)
                act_batch(act, B - 2, 0, more=False)
                act_batch(act, B - 1, 1, last=True, more=False)
                if layer == 1:
                    act_square(act, B - 1, 3)
                act_yT(act, B - 1, 2)
                if layer == 1:
                    act_sd(act, B - 1, 3)
                act_yT(act, B - 1, 3)

            @block.vector
            def _(v):
                v.memset(vv[:, :, :, :], 1.0).then_inc(ones_set, 1)
                finish_stats_vector(v, K, var_ready, std_ready, rstd_ready)
                for t in range(TPB):
                    vec_qk(v, 0, t)
                vec_batch(v, 0)
                with v.Fori(1, B - 1) as b:
                    vec_batch(v, b)
                vec_batch(v, B - 1, last=True)
                vec_sum(v, B - 1, 3)
                if layer == 0:
                    vec_den(v, NT - 1, 3)
                else:
                    vec_var(v, NT - 1)
                vec_rec(v, NT - 1)
                vec_y(v, NT - 1, 3)
                for t in (1, 2, 3):
                    vec_residual(v, B - 1, t)
                v.wait_ge(x_done, NT)
                if layer == 0:
                    for n in range(NT - 4, NT):
                        tile_stats(v, K, K.X, n, bn_done)

            @block.gpsimd
            def _(pool):
                if layer == 1:
                    for t in range(3):
                        pool_rope(pool, 0, t)
                pool_kv(pool, 0, 0)
                pool_batch(pool, 0, 0)
                with pool.Fori(0, B // 2 - 1) as i:
                    pool_batch(pool, 2 * i + 1, 1)
                    pool_batch(pool, 2 * i + 2, 0)
                pool_batch(pool, B - 1, 1, last=True)
                if layer == 1:
                    for t in (1, 2, 3):
                        pool_gate(pool, B - 1, t, 1)

            @block.sync
            def _(sp):
                if layer == 1:
                    with sp.Fori(0, B) as b:
                        sp.wait_ge(x_done, 4 * b + 4)
                        sp.dma_start(A["xs"].rearrange("(b t p) f -> b p t f", p=P, t=TPB)[ds(b, 1), :, :, :]
                                     .rearrange("o p t f -> (o p) t f"), K.X[:, ds(4 * b, 4), :]).then_inc(x_out, 16)
                    sp.wait_ge(x_out, 16 * B)


def token_shift_ffn(nc, A, K):
    with ExitStack() as ctx:
        sb = lambda n, s, d=F32: ctx.enter_context(nc.sbuf_tensor(f"f_{n}", s, d))
        sem = lambda n: ctx.enter_context(nc.semaphore(f"f_{n}"))
        pb = lambda n: [ctx.enter_context(nc.psum_tensor(f"f_{n}{i}", [P, 512], F32)) for i in range(2)]
        pT, pK, pR, pV = pb("pT"), pb("pK"), pb("pR"), pb("pV")
        xn = sb("xn", [P, TPB, P])
        h = sb("h", [P, 2, T + 1])
        d, xr, xk, kr, ka, sg, vm = (sb(n, [P, 2, T]) for n in ("d", "xr", "xk", "kr", "ka", "sg", "vm"))
        var_ready, std_ready, rstd_ready = sem("var"), sem("std"), sem("rstd")
        xn_ready, xn_T, h_ready, col_zero = sem("xn_ready"), sem("xn_T"), sem("h_ready"), sem("col_zero")
        d_ready, xr_ready, xk_ready = sem("d_ready"), sem("xr_ready"), sem("xk_ready")
        k_ps, r_ps, v_ps = sem("k_ps"), sem("r_ps"), sem("v_ps")
        kr_ready, ka_ready, sg_ready, vm_ready = sem("kr_ready"), sem("ka_ready"), sem("sg_ready"), sem("vm_ready")
        x_done, bn_done = sem("x_done"), sem("bn_done")

        def act_normalise(act, b):
            for t in range(TPB):
                wait(act, xn_T, 4 * b - 3 + t)
                act.activation(xn[:, t, :], K.X[:, ds(4 * b + t, 1), :].rearrange("p a f -> p (a f)"), ACT.Identity,
                               bias=K.nmr[:, ds(4 * b + t, 1)], scale=K.rstd[:, ds(4 * b + t, 1)]).then_inc(xn_ready, 1)

        def act_h(act, b, p):
            act.wait_ge(xn_T, 4 * b + 4)
            wait(act, xr_ready, b - 1)
            act.activation(h[:, p, 1:T + 1], pT[p][:, :], ACT.Identity, bias=K.mod[:, SB0, ds(b, 1)],
                           scale=K.mod[:, CB0, ds(b, 1)]).then_inc(h_ready, 1)

        def pe_h(pe, b, p):
            for t in range(TPB):
                pe.wait_ge(xn_ready, 4 * b + t + 1)
                if t == 0:
                    wait(pe, h_ready, b - 1)
                pe.transpose(pT[p][:, t * P:(t + 1) * P], xn[:, t, :], K.ident[:, :]).then_inc(xn_T, 1)

        def pool_diff(pool, b, p):
            pool.wait_ge(h_ready, b + 1)
            wait(pool, xr_ready, b - 1)
            pool.tensor_tensor(d[:, p, :], h[:, p, 1:T + 1], h[:, p, 0:T], ALU.subtract).then_inc(d_ready, 1)

        def vec_mix(v, b, p):
            v.wait_ge(d_ready, b + 1)
            wait(v, k_ps, b - 1)
            v.scalar_tensor_tensor(out=xk[:, p, :], in0=d[:, p, :], scalar=K.cols[:, MU_K:MU_K + 1],
                                   in1=h[:, p, 0:T], op0=ALU.mult, op1=ALU.add).then_inc(xk_ready, 1)
            wait(v, r_ps, b - 1)
            v.scalar_tensor_tensor(out=xr[:, p, :], in0=d[:, p, :], scalar=K.cols[:, MU_R:MU_R + 1],
                                   in1=h[:, p, 0:T], op0=ALU.mult, op1=ALU.add).then_inc(xr_ready, 1)

        def pe_kr(pe, b, p):
            pe.wait_ge(xk_ready, b + 1)
            wait(pe, kr_ready, b - 1)
            pe.matmul(pK[p][:, :], K.W[:, W_KT, :], xk[:, p, :], start=True, stop=True).then_inc(k_ps, 1)
            pe.wait_ge(xr_ready, b + 1)
            wait(pe, sg_ready, b - 1)
            for t in range(TPB):
                mm = pe.matmul(pR[p][:, t * P:(t + 1) * P], xr[:, p, t * P:(t + 1) * P], K.W[:, W_RT, :],
                               start=True, stop=True)
            mm.then_inc(r_ps, 1)

        def act_kr(act, b, p):
            act.wait_ge(k_ps, b + 1)
            wait(act, ka_ready, b - 1)
            act.activation(kr[:, p, :], pK[p][:, :], ACT.Relu).then_inc(kr_ready, 1)

        def act_square(act, b, p):
            act.wait_ge(kr_ready, b + 1)
            wait(act, v_ps, b - 1)
            act.activation(ka[:, p, :], kr[:, p, :], ACT.Square).then_inc(ka_ready, 1)

        def act_sigmoid(act, b, p):
            act.wait_ge(r_ps, b + 1)
            wait(act, vm_ready, b - 1)
            act.activation(sg[:, p, :], pR[p][:, :], ACT.Sigmoid).then_inc(sg_ready, 1)

        def pe_v(pe, b, p):
            pe.wait_ge(ka_ready, b + 1)
            wait(pe, vm_ready, b - 1)
            for t in range(TPB):
                mm = pe.matmul(pV[p][:, t * P:(t + 1) * P], ka[:, p, t * P:(t + 1) * P],
                               K.wgate[:, 1, ds(b, 1), :].rearrange("p a f -> p (a f)"), start=True, stop=True)
            mm.then_inc(v_ps, 1)

        def vec_gate(v, b, p):
            v.wait_ge(v_ps, b + 1)
            v.wait_ge(sg_ready, b + 1)
            wait(v, x_done, b)
            v.tensor_tensor(vm[:, p, :], pV[p][:, :], sg[:, p, :], ALU.mult).then_inc(vm_ready, 1)

        def vec_stats(v, b):
            for t in range(TPB):
                tile_stats(v, K, K.X, 4 * b + t, bn_done)

        def vec_residual(v, b, p):
            v.wait_ge(vm_ready, b + 1)
            x = K.X[:, ds(4 * b, 4), :].rearrange("p a f -> p (a f)")
            v.tensor_tensor(x, vm[:, p, :], x, ALU.add).then_inc(x_done, 1)

        def there(b):
            return not isinstance(b, int) or 0 <= b < B

        def pe_step(pe, s, p):
            if there(s - 1):
                pe_v(pe, s - 1, 1 - p)
            if there(s):
                pe_kr(pe, s, p)
            if there(s + 2):
                pe_h(pe, s + 2, p)

        def act_step(act, s, p):
            if there(s):
                act_kr(act, s, p)
                act_square(act, s, p)
                act_sigmoid(act, s, p)
            if there(s + 2):
                act_h(act, s + 2, p)
            if there(s + 3):
                act_normalise(act, s + 3)

        def vec_step(v, s, p):
            if there(s + 1):
                vec_mix(v, s + 1, 1 - p)
            if there(s - 1):
                vec_gate(v, s - 1, 1 - p)
            if there(s - 2):
                vec_stats(v, s - 2)
            if there(s - 1):
                vec_residual(v, s - 1, 1 - p)

        def pool_step(pool, s, p):
            if there(s + 1):
                pool_diff(pool, s + 1, 1 - p)

        def run(e, step):
            for s in (0, 1):
                step(e, s, s % 2)
            with e.Fori(1, B // 2 - 2) as i:
                step(e, 2 * i, 0)
                step(e, 2 * i + 1, 1)
            for s in range(B - 4, B + 1):
                step(e, s, s % 2)

        with nc.Block() as block:
            @block.tensor
            def _(pe):
                pe_h(pe, 0, 0)
                pe_h(pe, 1, 1)
                run(pe, pe_step)

            @block.scalar
            def _(act):
                finish_stats_scalar(act, K, var_ready, std_ready, rstd_ready)
                act_normalise(act, 0)
                act_h(act, 0, 0)
                act_normalise(act, 1)
                act_h(act, 1, 1)
                act_normalise(act, 2)
                run(act, act_step)

            @block.vector
            def _(v):
                v.memset(h[:, :, 0:1], 0.0).then_inc(col_zero, 1)
                finish_stats_vector(v, K, var_ready, std_ready, rstd_ready)
                vec_mix(v, 0, 0)
                run(v, vec_step)
                v.wait_ge(x_done, B)
                vec_stats(v, B - 1)

            @block.gpsimd
            def _(pool):
                pool.wait_ge(col_zero, 1)
                pool_diff(pool, 0, 0)
                run(pool, pool_step)


def attend_batches(nc, A, K):
    G = NT // 4
    with ExitStack() as ctx:
        sb = lambda n, s, d=F32: ctx.enter_context(nc.sbuf_tensor(f"m_{n}", s, d))
        sem = lambda n: ctx.enter_context(nc.semaphore(f"m_{n}"))
        pb = lambda n: ctx.enter_context(nc.psum_tensor(f"m_{n}", [P, 512], F32))
        pT, pq, pk, pv, pS, pO, pU = pb("pT"), pb("pq"), pb("pk"), pb("pv"), pb("pS"), pb("pO"), pb("pU")
        xn, h1, h = (sb(n, [P, 4, P]) for n in ("xn", "h1", "h"))
        hT, qT = sb("hT", [P, 4 * P]), sb("qT", [P, 4 * P])
        kx = sb("kx", [P, 16, FH, 32])
        v_ = sb("v", [P, 2, 4, P])
        sm, s2, ex, pn = (sb(n, [P, 16, 32]) for n in ("sm", "s2", "ex", "pn"))
        mx, sm_sum, rc = sb("mx", [P, 16]), sb("sum", [P, 16]), sb("rc", [P, 16])
        ax = sb("ax", [P, 16, 4, 32])
        oT = sb("oT", [P, 4 * P])
        x_in = [sem(f"x_in{g}") for g in range(4)]
        stats, var_ready, std_ready, rstd_ready = sem("stats"), sem("var"), sem("std"), sem("rstd")
        xn_ready, h1_ready, h_ready, h3_ready = sem("xn_ready"), sem("h1_ready"), sem("h_ready"), sem("h3_ready")
        h_T, hT_ready, q_ps, k_ps, v_ps = sem("h_T"), sem("hT_ready"), sem("q_ps"), sem("k_ps"), sem("v_ps")
        q_ready, kx_ready, v_ready, zeroed = sem("q_ready"), sem("kx_ready"), sem("v_ready"), sem("zeroed")
        s_ps, sm_ready, mx_ready, s2_ready, ex_ready = (sem("s_ps"), sem("sm_ready"), sem("mx_ready"),
                                                        sem("s2_ready"), sem("ex_ready"))
        sum_ready, rc_ready, pn_ready, ax_ready = sem("sum_ready"), sem("rc_ready"), sem("pn_ready"), sem("ax_ready")
        o_ps, oT_ready, w_ps, u_ready, bn_done = sem("o_ps"), sem("oT_ready"), sem("w_ps"), sem("u_ready"), sem("bn_done")

        flat = lambda t: t[:, :, :].rearrange("p a b -> p (a b)")
        over = lambda row: row.unsqueeze(1).to_broadcast([P, 4, P])

        def act_xn(act, g):
            wait(act, h1_ready, g)
            for t in range(4):
                act.activation(xn[:, t, :], K.X[:, ds(4 * g + t, 1), :].rearrange("p a f -> p (a f)"), ACT.Identity,
                               bias=K.nmr[:, ds(4 * g + t, 1)], scale=K.rstd[:, ds(4 * g + t, 1)]).then_inc(xn_ready, 1)

        def pool_h(pool, g):
            pool.wait_ge(xn_ready, 4 * g + 4)
            wait(pool, h_ready, g)
            pool.tensor_tensor(h1[:, :, :], xn[:, :, :], over(K.tab[:, 1, :]), ALU.mult).then_inc(h1_ready, 1)
            pool.wait_ge(h1_ready, g + 1)
            wait(pool, h_T, g)
            wait(pool, h3_ready, g)
            pool.tensor_tensor(h[:, :, :], h1[:, :, :], over(K.tab[:, 0, :]), ALU.add).then_inc(h_ready, 1)

        def pool_h3(pool, g):
            pool.wait_ge(h_ready, g + 1)
            pool.tensor_tensor(K.U[:, ds(4 * g, 4), :], h[:, :, :], over(K.bo[:, :]), ALU.add).then_inc(h3_ready, 1)

        def pool_shift(pool, g):
            pool.wait_ge(mx_ready, g + 1)
            wait(pool, ex_ready, g)
            pool.tensor_tensor(s2[:, :, :], sm[:, :, :], mx[:, :].unsqueeze(2).to_broadcast([P, 16, 32]),
                               ALU.subtract).then_inc(s2_ready, 1)

        def pe_T(pe, g):
            pe.wait_ge(h_ready, g + 1)
            wait(pe, hT_ready, g)
            for t in range(4):
                mm = pe.transpose(pT[:, t * P:(t + 1) * P], h[:, t, :], K.ident[:, :])
            mm.then_inc(h_T, 1)

        def act_hT(act, g):
            act.wait_ge(h_T, g + 1)
            wait(act, v_ps, g)
            act.activation(hT[:, :], pT[:, :], ACT.Copy).then_inc(hT_ready, 1)

        def pe_qk(pe, g):
            pe.wait_ge(hT_ready, g + 1)
            wait(pe, q_ready, g)
            pe.matmul(pq[:, :], K.W[:, W_FQ, :], hT[:, :], start=True, stop=True).then_inc(q_ps, 1)
            wait(pe, kx_ready, 4 * g)
            pe.matmul(pk[:, :], K.W[:, W_FK, :], hT[:, :], start=True, stop=True).then_inc(k_ps, 1)

        def pe_v(pe, g):
            wait(pe, v_ready, g)
            for t in range(4):
                mm = pe.matmul(pv[:, t * P:(t + 1) * P], hT[:, t * P:(t + 1) * P], K.W[:, W_FV, :],
                               start=True, stop=True)
            mm.then_inc(v_ps, 1)

        def act_q(act, g):
            act.wait_ge(q_ps, g + 1)
            wait(act, s_ps, g)
            act.activation(qT[:, :], pq[:, :], ACT.Identity, bias=K.cols[:, BQ:BQ + 1]).then_inc(q_ready, 1)

        def kx_view(hd):
            rows = slice(32 * hd, 32 * hd + 32)
            return rows, kx[rows, :, hd, :], pk[rows, :].rearrange("p (c s) -> p c s", c=16)

        def act_k(act, g):
            act.wait_ge(k_ps, g + 1)
            for hd in range(FH):
                rows, o, i = kx_view(hd)
                act.activation(o, i, ACT.Identity, bias=K.cols[rows, BK:BK + 1]).then_inc(kx_ready, 1)

        def act_v(act, g, p):
            act.wait_ge(v_ps, g + 1)
            wait(act, o_ps, g - 1)
            act.activation(flat(v_[:, p, :, :]), pv[:, :], ACT.Copy).then_inc(v_ready, 1)

        def pe_scores(pe, g):
            pe.wait_ge(q_ready, g + 1)
            pe.wait_ge(kx_ready, 4 * g + 4)
            wait(pe, sm_ready, g)
            for t in range(4):
                for c in range(4):
                    mm = pe.matmul(pS[32 * c:32 * c + 32, t * P:(t + 1) * P], qT[:, t * P + 32 * c:t * P + 32 * c + 32],
                                   kx[:, 4 * t + c, :, :].rearrange("p h s -> p (h s)"), start=True, stop=True,
                                   skip_group_check=True)
            mm.then_inc(s_ps, 1)

        def vec_scores(v, g):
            v.wait_ge(s_ps, g + 1)
            wait(v, s2_ready, g)
            v.scalar_tensor_tensor(out=sm[:, :, :], in0=pS[:, :].rearrange("p (a s) -> p a s", s=32),
                                   scalar=float(FD) ** -0.5, in1=K.smask[:, :].unsqueeze(1).to_broadcast([P, 16, 32]),
                                   op0=ALU.mult, op1=ALU.add).then_inc(sm_ready, 1)

        def vec_max(v, g):
            v.wait_ge(sm_ready, g + 1)
            v.tensor_reduce(mx[:, :], sm[:, :, :], AX.X, ALU.max).then_inc(mx_ready, 1)

        def act_exp(act, g):
            act.wait_ge(s2_ready, g + 1)
            wait(act, pn_ready, g)
            act.activation(flat(ex), flat(s2), ACT.Exp).then_inc(ex_ready, 1)

        def vec_total(v, g):
            v.wait_ge(ex_ready, g + 1)
            wait(v, rc_ready, g)
            v.tensor_reduce(sm_sum[:, :], ex[:, :, :], AX.X, ALU.add).then_inc(sum_ready, 1)

        def vec_reciprocal(v, g):
            v.wait_ge(sum_ready, g + 1)
            wait(v, pn_ready, g)
            v.reciprocal(rc[:, :], sm_sum[:, :]).then_inc(rc_ready, 1)

        def vec_probs(v, g):
            v.wait_ge(rc_ready, g + 1)
            wait(v, ax_ready, 4 * g)
            v.tensor_tensor(pn[:, :, :], ex[:, :, :], rc[:, :].unsqueeze(2).to_broadcast([P, 16, 32]),
                            ALU.mult).then_inc(pn_ready, 1)

        def vec_transpose(v, g):
            v.wait_ge(pn_ready, g + 1)
            wait(v, o_ps, g)
            for c in range(4):
                rows = slice(32 * c, 32 * c + 32)
                v.transpose(ax[rows, :, c, :], pn[rows, :, :]).then_inc(ax_ready, 1)

        def pe_values(pe, g, p):
            pe.wait_ge(ax_ready, 4 * g + 4)
            pe.wait_ge(v_ready, g + 1)
            wait(pe, oT_ready, g)
            for t in range(4):
                for hd in range(FH):
                    mm = pe.matmul(pO[32 * hd:32 * hd + 32, t * P:(t + 1) * P], v_[:, p, t, 32 * hd:32 * hd + 32],
                                   ax[:, 4 * t + hd, :, :].rearrange("p c s -> p (c s)"), start=True, stop=True,
                                   skip_group_check=True)
            mm.then_inc(o_ps, 1)

        def act_o(act, g):
            act.wait_ge(o_ps, g + 1)
            wait(act, w_ps, g)
            act.activation(oT[:, :], pO[:, :], ACT.Copy).then_inc(oT_ready, 1)

        def pe_out(pe, g):
            pe.wait_ge(oT_ready, g + 1)
            wait(pe, u_ready, g)
            for t in range(4):
                mm = pe.matmul(pU[:, t * P:(t + 1) * P], oT[:, t * P:(t + 1) * P], K.W[:, W_FO, :],
                               start=True, stop=True)
            mm.then_inc(w_ps, 1)

        def vec_u(v, g):
            v.wait_ge(w_ps, g + 1)
            v.wait_ge(h3_ready, g + 1)
            wait(v, u_ready, g)
            u = K.U[:, ds(4 * g, 4), :].rearrange("p a f -> p (a f)")
            v.tensor_tensor(u, pU[:, :], u, ALU.add).then_inc(u_ready, 1)

        def vec_stats(v, g):
            for t in range(4):
                tile_stats(v, K, K.U, 4 * g + t, bn_done)

        def there(g):
            return not isinstance(g, int) or 0 <= g < G

        def pe_step(pe, s, p):
            if there(s):
                pe_scores(pe, s)
            if there(s - 2):
                pe_out(pe, s - 2)
            if there(s + 1):
                pe_T(pe, s + 1)
                pe_qk(pe, s + 1)
                pe_v(pe, s + 1)
            if there(s - 1):
                pe_values(pe, s - 1, 1 - p)

        def act_step(act, s, p):
            if there(s - 2):
                act_o(act, s - 2)
            if there(s):
                act_v(act, s, p)
            if there(s + 2):
                act_xn(act, s + 2)
            if there(s + 1):
                act_hT(act, s + 1)
                act_q(act, s + 1)
            if there(s):
                act_exp(act, s)
            if there(s + 1):
                act_k(act, s + 1)

        def vec_step(v, s, p):
            if there(s - 1):
                vec_total(v, s - 1)
            if there(s):
                vec_scores(v, s)
            if there(s - 1):
                vec_reciprocal(v, s - 1)
            if there(s):
                vec_max(v, s)
            if there(s - 1):
                vec_probs(v, s - 1)
                vec_transpose(v, s - 1)
            if there(s - 2):
                vec_u(v, s - 2)
            if there(s - 3):
                vec_stats(v, s - 3)

        def pool_step(pool, s, p):
            if there(s + 2):
                pool_h(pool, s + 2)
            if there(s):
                pool_shift(pool, s)
            if there(s + 2):
                pool_h3(pool, s + 2)

        def run(e, step, before_first=None):
            for s in (-2, -1):
                step(e, s, s % 2)
            if before_first:
                before_first()
            for s in range(4):
                step(e, s, s % 2)
            with e.Fori(2, G // 2 - 1) as i:
                step(e, 2 * i, 0)
                step(e, 2 * i + 1, 1)
            for s in range(G - 2, G + 2):
                step(e, s, s % 2)

        with nc.Block() as block:
            @block.sync
            def _(sp):
                xs = A["xs"].rearrange("(b n t) f -> t b n f", n=NT, t=8)
                for g in range(4):
                    for t in range(8):
                        sp.dma_start(K.X[16 * t:16 * t + 16, 16 * g:16 * g + 16, :], xs[t][:, 16 * g:16 * g + 16, :])\
                          .then_inc(x_in[g], 16)

            @block.tensor
            def _(pe):
                pe.wait_ge(zeroed, 2)
                run(pe, pe_step)

            @block.scalar
            def _(act):
                stats_scalar = lambda q: finish_stats_scalar(act, K, var_ready, std_ready, rstd_ready, q, 4)
                act.wait_ge(zeroed, 2)
                stats_scalar(0)
                run(act, act_step, before_first=lambda: [stats_scalar(q) for q in (1, 2, 3)])

            @block.vector
            def _(v):
                for q in range(4):
                    v.wait_ge(x_in[q], 8 * 16)
                    with v.Fori(4 * q, 4 * q + 4) as g:
                        for j in range(4):
                            tile_stats(v, K, K.X, 4 * g + j, stats)
                    v.wait_ge(stats, 16 * q + 16)
                    finish_stats_vector(v, K, var_ready, std_ready, rstd_ready, q, 4)
                run(v, vec_step)
                v.wait_ge(u_ready, G)
                vec_stats(v, G - 1)

            @block.gpsimd
            def _(pool):
                pool.memset(kx[:, :, :, :], 0.0).then_inc(zeroed, 1)
                pool.memset(ax[:, :, :, :], 0.0).then_inc(zeroed, 1)
                run(pool, pool_step)


def route(nc, A, K, pos, expert):
    G = NT // 4
    with ExitStack() as ctx:
        sb = lambda n, s, d=F32: ctx.enter_context(nc.sbuf_tensor(f"r_{n}", s, d))
        sem = lambda n: ctx.enter_context(nc.semaphore(f"r_{n}"))
        pb = lambda n: ctx.enter_context(nc.psum_tensor(f"r_{n}", [P, 512], F32))
        pT, pL, pR, pC = [pb("pT0"), pb("pT1")], [pb("pL0"), pb("pL1")], pb("pR"), pb("pC")
        yn, y1, yb = (sb(n, [P, 2, 4, P]) for n in ("yn", "y1", "yb"))
        yT = sb("yT", [P, 2, 4 * P])
        logits = sb("logits", [P, NT, E])
        ustrict, tie, iota, ones = sb("ustrict", [P, P]), sb("tie", [P, E]), sb("iota", [P, SLOTS]), sb("ones", [P, P])
        best, first = sb("best", [P, NT]), sb("first", [P, NT])
        hot, work = sb("hot", [P, NT, E]), sb("work", [P, NT, E])
        total, upto = sb("total", [P, E, NT]), sb("upto", [P, E, NT])
        tiles, ends, base = sb("tiles", [P, E]), sb("ends", [P, E]), sb("base", [P, E])
        after = sb("after", [P, SLOTS, E])
        posf, expf = sb("posf", [P, NT]), sb("expf", [P, SLOTS])
        var_ready, std_ready, rstd_ready = sem("var"), sem("std"), sem("rstd")
        tab_in, yn_ready, y1_ready, yb_ready, y_ready = (sem("tab_in"), sem("yn_ready"), sem("y1_ready"),
                                                         sem("yb_ready"), sem("y_ready"))
        y_T, yT_ready, l_ps, l_ready, chain, hot_ready, c_ps = (sem("y_T"), sem("yT_ready"), sem("l_ps"), sem("l_ready"),
                                                                sem("chain"), sem("hot_ready"), sem("c_ps"))
        over = lambda row: row.unsqueeze(1).to_broadcast([P, 4, P])

        def act_step(act, g, s):
            wait(act, y1_ready, g - 1)
            for t in range(4):
                act.activation(yn[:, s, t, :], K.U[:, ds(4 * g + t, 1), :].rearrange("p a f -> p (a f)"), ACT.Identity,
                               bias=K.nmr[:, ds(4 * g + t, 1)], scale=K.rstd[:, ds(4 * g + t, 1)]).then_inc(yn_ready, 1)

        def act_yT(act, g, s):
            act.wait_ge(y_T, g + 1)
            wait(act, l_ps, g - 1)
            act.activation(yT[:, s, :], pT[s][:, :], ACT.Copy).then_inc(yT_ready, 1)

        def pe_T(pe, g, s):
            pe.wait_ge(yb_ready, g + 1)
            wait(pe, yT_ready, g - 1)
            for t in range(4):
                mm = pe.transpose(pT[s][:, t * P:(t + 1) * P], yb[:, s, t, :], K.ident[:, :])
            mm.then_inc(y_T, 1)

        def pe_logits(pe, g, s):
            pe.wait_ge(yT_ready, g + 1)
            wait(pe, l_ready, g - 1)
            for t in range(4):
                mm = pe.matmul(pL[s][:, t * E:(t + 1) * E], yT[:, s, t * P:(t + 1) * P], K.wg8[:, :],
                               start=True, stop=True)
            mm.then_inc(l_ps, 1)

        def vec_y(v, g, s):
            v.wait_ge(yn_ready, 4 * g + 4)
            wait(v, yb_ready, g - 1)
            wait(v, y_ready, g - 1)
            v.tensor_tensor(y1[:, s, :, :], yn[:, s, :, :], over(K.rows[:, 0, :]), ALU.mult).then_inc(y1_ready, 1)
            v.wait_ge(y1_ready, g + 1)
            wait(v, y_T, g - 1)
            v.tensor_tensor(yb[:, s, :, :], y1[:, s, :, :], over(K.rows[:, 1, :]), ALU.add).then_inc(yb_ready, 1)

        def vec_logits(v, g, s):
            v.wait_ge(l_ps, g + 1)
            v.tensor_copy(logits[:, ds(4 * g, 4), :], pL[s][:, 0:4 * E].rearrange("p (a e) -> p a e", e=E))\
             .then_inc(l_ready, 1)

        def pool_y(pool, g, s):
            pool.wait_ge(y1_ready, g + 1)
            pool.tensor_tensor(K.U[:, ds(4 * g, 4), :], y1[:, s, :, :], over(K.rows[:, 1, :]), ALU.add)\
                .then_inc(y_ready, 1)

        with nc.Block() as block:
            @block.sync
            def _(sp):
                sp.dma_start(ustrict[:, :], A["k_ustrict"]).then_inc(tab_in, 16)
                sp.dma_start(tie[:, :], A["k_tie"]).then_inc(tab_in, 16)
                sp.dma_start(iota[:, :], A["k_iota"]).then_inc(tab_in, 16)
                sp.dma_start(K.b1[:, :, :], A["L1_ffn_b1"].rearrange("(a e) f -> a e f", a=1)
                             .to_broadcast([P, E, DF])).then_inc(tab_in, 16)
                sp.dma_start(K.b2[:, :, :], A["L1_ffn_b2"].rearrange("(a e) f -> a e f", a=1)
                             .to_broadcast([P, E, P])).then_inc(tab_in, 16)
                sp.wait_ge(tab_in, 5 * 16)

            @block.scalar
            def _(act):
                finish_stats_scalar(act, K, var_ready, std_ready, rstd_ready)
                act_step(act, 0, 0)
                def pair(i):
                    act_step(act, 2 * i + 1, 1)
                    act_yT(act, 2 * i, 0)
                    act_step(act, 2 * i + 2, 0)
                    act_yT(act, 2 * i + 1, 1)
                pair(0)
                with act.Fori(1, G // 2 - 1) as i:
                    pair(i)
                act_step(act, G - 1, 1)
                act_yT(act, G - 2, 0)
                act_yT(act, G - 1, 1)

            @block.tensor
            def _(pe):
                pe_T(pe, 0, 0)
                def pair(i):
                    pe_T(pe, 2 * i + 1, 1)
                    pe_logits(pe, 2 * i, 0)
                    pe_T(pe, 2 * i + 2, 0)
                    pe_logits(pe, 2 * i + 1, 1)
                pair(0)
                with pe.Fori(1, G // 2 - 1) as i:
                    pair(i)
                pe_T(pe, G - 1, 1)
                pe_logits(pe, G - 2, 0)
                pe_logits(pe, G - 1, 1)
                pe.wait_ge(hot_ready, 1)
                pe.wait_ge(tab_in, 5 * 16)
                h = hot[:, :, :].rearrange("p n e -> p (n e)")
                pe.matmul(pR[:, :], ustrict[:, :], h, start=True, stop=True).then_inc(c_ps, 1)
                pe.matmul(pC[:, :], ones[:, :], h, start=True, stop=True).then_inc(c_ps, 1)

            @block.gpsimd
            def _(pool):
                with pool.Fori(0, G // 2) as i:
                    for s in range(2):
                        pool_y(pool, 2 * i + s, s)

            @block.vector
            def _(v):
                count = [0]

                def link(ins):
                    count[0] += 1
                    ins.then_inc(chain, 1)
                    v.wait_ge(chain, count[0])

                link(v.memset(ones[:, :], 1.0))
                finish_stats_vector(v, K, var_ready, std_ready, rstd_ready)
                v.wait_ge(rstd_ready, 2)
                vec_y(v, 0, 0)
                with v.Fori(0, G // 2 - 1) as i:
                    vec_y(v, 2 * i + 1, 1)
                    vec_logits(v, 2 * i, 0)
                    vec_y(v, 2 * i + 2, 0)
                    vec_logits(v, 2 * i + 1, 1)
                vec_y(v, G - 1, 1)
                vec_logits(v, G - 2, 0)
                vec_logits(v, G - 1, 1)
                v.wait_ge(l_ready, G)
                v.wait_ge(tab_in, 5 * 16)
                by_e = lambda t: t.unsqueeze(2).to_broadcast([P, NT, E])
                by_n = lambda t: t.unsqueeze(1).to_broadcast([P, NT, E])
                link(v.tensor_reduce(best[:, :], logits[:, :, :], AX.X, ALU.max))
                link(v.tensor_tensor(work[:, :, :], logits[:, :, :], by_e(best[:, :]), ALU.is_ge))
                link(v.tensor_tensor(hot[:, :, :], work[:, :, :], by_n(tie[:, :]), ALU.mult))
                link(v.tensor_reduce(first[:, :], hot[:, :, :], AX.X, ALU.max))
                link(v.tensor_tensor(work[:, :, :], by_n(tie[:, :]), by_e(first[:, :]), ALU.is_equal))
                v.tensor_copy(hot[:, :, :], work[:, :, :]).then_inc(hot_ready, 1)
                v.wait_ge(c_ps, 2)
                link(v.tensor_copy(total[:, :, :], pC[:, :].rearrange("p (n e) -> p e n", e=E)))
                for e in range(E):
                    link(v.tensor_tensor_scan(upto[:, e, :], ones[:, 0:NT], total[:, e, :], 0.0, ALU.mult, ALU.add))
                w = work[:, :, :].rearrange("p n e -> p (n e)").rearrange("p (e n) -> p e n", e=E)
                link(v.tensor_scalar(expf[:, 0:NT], iota[:, 0:NT], float(P), None, ALU.mult))
                link(v.tensor_tensor(w, upto[:, :, NT - 1:NT].to_broadcast([P, E, NT]),
                                     expf[:, 0:NT].unsqueeze(1).to_broadcast([P, E, NT]), ALU.is_gt))
                link(v.tensor_reduce(tiles[:, :], w, AX.X, ALU.add))
                link(v.tensor_tensor_scan(ends[:, :], ones[:, 0:E], tiles[:, :], 0.0, ALU.mult, ALU.add))
                link(v.tensor_tensor(base[:, :], ends[:, :], tiles[:, :], ALU.subtract))
                link(v.tensor_scalar(base[:, :], base[:, :], float(P), None, ALU.mult))
                link(v.tensor_tensor(total[:, :, :], upto[:, :, :], total[:, :, :], ALU.subtract))
                link(v.tensor_tensor(total[:, :, :], total[:, :, :], base[:, :].unsqueeze(2).to_broadcast([P, E, NT]),
                                     ALU.add))
                link(v.tensor_tensor(work[:, :, :], pR[:, :].rearrange("p (n e) -> p n e", e=E),
                                     total[:, :, :].rearrange("p e n -> p n e"), ALU.add))
                link(v.tensor_tensor(work[:, :, :], work[:, :, :], hot[:, :, :], ALU.mult))
                link(v.tensor_reduce(posf[:, :], work[:, :, :], AX.X, ALU.add))
                link(v.tensor_copy(pos[:, :], posf[:, :]))
                link(v.tensor_tensor(after[:, :, :], ends[:, :].unsqueeze(1).to_broadcast([P, SLOTS, E]),
                                     iota[:, :].unsqueeze(2).to_broadcast([P, SLOTS, E]), ALU.is_le))
                link(v.tensor_reduce(expf[:, :], after[:, :, :], AX.X, ALU.add))
                link(v.tensor_scalar(expf[:, :], expf[:, :], float(E - 1), None, ALU.min))
                link(v.tensor_copy(expert[:, :], expf[:, :]))


def experts(nc, A, K, out):
    with ExitStack() as ctx:
        sb = lambda n, s, d=F32: ctx.enter_context(nc.sbuf_tensor(f"e_{n}", s, d))
        sem = lambda n: ctx.enter_context(nc.semaphore(f"e_{n}"))
        pb = lambda n: ctx.enter_context(nc.psum_tensor(f"e_{n}", [P, 512], F32))
        pos, expert = sb("pos", [P, NT], U32), sb("expert", [P, SLOTS], I32)
        K.b1, K.b2 = sb("b1", [P, E, DF]), sb("b2", [P, E, P])
        route(nc, A, K, pos, expert)

        scattered = sem("scattered")
        with nc.Block() as block:
            @block.gpsimd
            def _(pool):
                pool.wait_ge(K.ys_zero, 8 * 16)
                for n in range(NT):
                    pool.indirect_dma_start(out=A["ys"], out_offset=bass.IndirectOffsetOnAxis(ap=pos[:, n:n + 1], axis=0),
                                            in_=K.U[:, n, :], in_offset=None).then_inc(scattered, 16)
                pool.wait_ge(scattered, 16 * NT)

        run_experts(nc, A, K, expert)
        finish(nc, A, K, pos, out)


def run_experts(nc, A, K, expert):
    with ExitStack() as ctx:
        sb = lambda n, s, d=F32: ctx.enter_context(nc.sbuf_tensor(f"x_{n}", s, d))
        sem = lambda n: ctx.enter_context(nc.semaphore(f"x_{n}"))
        pb = lambda n: ctx.enter_context(nc.psum_tensor(f"x_{n}", [P, 512], F32))
        pT, pH, pHT, pZ = ([pb(f"{n}{i}") for i in range(2)] for n in ("pT", "pH", "pHT", "pZ"))
        yl, z = sb("yl", [P, 4, P]), sb("z", [P, 4, P])
        yT, hb, hT = sb("yT", [P, 2, P]), sb("hb", [P, 2, DF]), sb("hT", [P, 2, DF])
        y_in, z_out = [sem(f"y_in{s}") for s in range(4)], [sem(f"z_out{s}") for s in range(4)]
        y_T, yT_ready, h_ps, hb_ready, h_T, hT_ready, z_ps, z_ready = (
            sem(n) for n in ("y_T", "yT_ready", "h_ps", "hb_ready", "h_T", "hT_ready", "z_ps", "z_ready"))
        ys, zs = (A[n].rearrange("(j p) f -> j p f", p=P) for n in ("ys", "zs"))
        rounds = SLOTS // 4

        def pe_T(pe, i, s):
            j = 4 * i + s
            pe.wait_ge(y_in[s], 16 * i + 16)
            wait(pe, yT_ready, j - 1)
            pe.transpose(pT[s % 2][:, 0:P], yl[:, s, :], K.ident[:, :]).then_inc(y_T, 1)

        def act_yT(act, i, s):
            j = 4 * i + s
            act.wait_ge(y_T, j + 1)
            wait(act, h_ps, j - 1)
            act.activation(yT[:, s % 2, :], pT[s % 2][:, 0:P], ACT.Copy).then_inc(yT_ready, 1)

        def pe_h(pe, i, s):
            j = 4 * i + s
            e = pe.value_load(expert[0:1, ds(j, 1)], min_val=0, max_val=E - 1)
            pe.wait_ge(yT_ready, j + 1)
            wait(pe, hb_ready, j - 1)
            pe.matmul(pH[s % 2][:, :], yT[:, s % 2, :], K.w1[:, ds(e, 1), :].rearrange("p a f -> p (a f)"),
                      start=True, stop=True).then_inc(h_ps, 1)
            return e

        def vec_h(v, i, s):
            j = 4 * i + s
            e = v.value_load(expert[0:1, ds(j, 1)], min_val=0, max_val=E - 1)
            v.wait_ge(h_ps, j + 1)
            wait(v, h_T, j - 1)
            v.tensor_tensor(hb[:, s % 2, :], pH[s % 2][:, :], K.b1[:, ds(e, 1), :].rearrange("p a f -> p (a f)"),
                            ALU.add).then_inc(hb_ready, 1)

        def pe_hT(pe, i, s):
            j = 4 * i + s
            pe.wait_ge(hb_ready, j + 1)
            wait(pe, hT_ready, j - 1)
            for c in range(FC):
                mm = pe.transpose(pHT[s % 2][:, c * P:(c + 1) * P], hb[:, s % 2, c * P:(c + 1) * P], K.ident[:, :])
            mm.then_inc(h_T, 1)

        def act_hT(act, i, s):
            j = 4 * i + s
            act.wait_ge(h_T, j + 1)
            wait(act, z_ps, j - 1)
            act.activation(hT[:, s % 2, :], pHT[s % 2][:, :], ACT.Relu).then_inc(hT_ready, 1)

        def pe_z(pe, i, s):
            j = 4 * i + s
            e = pe.value_load(expert[0:1, ds(j, 1)], min_val=0, max_val=E - 1)
            pe.wait_ge(hT_ready, j + 1)
            wait(pe, z_ready, j - 1)
            for c in range(FC):
                mm = pe.matmul(pZ[s % 2][:, 0:P], hT[:, s % 2, c * P:(c + 1) * P],
                               K.w2[:, ds(e, 1), c, :].rearrange("p a f -> p (a f)"), start=(c == 0), stop=(c == FC - 1))
            mm.then_inc(z_ps, 1)

        def vec_z(v, i, s):
            j = 4 * i + s
            e = v.value_load(expert[0:1, ds(j, 1)], min_val=0, max_val=E - 1)
            v.wait_ge(z_ps, j + 1)
            wait(v, z_out[s], 16 * i)
            v.tensor_tensor(z[:, s, :], pZ[s % 2][:, 0:P], K.b2[:, ds(e, 1), :].rearrange("p a f -> p (a f)"),
                            ALU.add).then_inc(z_ready, 1)

        def at(i, s):
            return i + s // 4, s % 4

        with nc.Block() as block:
            @block.sync
            def _(sp):
                def load(i, s):
                    wait(sp, y_T, 4 * i + s - 3)
                    sp.dma_start(yl[:, s, :], ys[ds(4 * i + s, 1), :, :].rearrange("o p f -> (o p) f"))\
                      .then_inc(y_in[s], 16)

                def store(i, s):
                    sp.wait_ge(z_ready, 4 * i + s + 1)
                    sp.dma_start(zs[ds(4 * i + s, 1), :, :].rearrange("o p f -> (o p) f"), z[:, s, :])\
                      .then_inc(z_out[s], 16)
                for s in range(4):
                    load(0, s)
                with sp.Fori(0, rounds - 1) as i:
                    for s in range(4):
                        load(i + 1, s)
                        store(i, s)
                for s in range(4):
                    store(rounds - 1, s)
                for s in range(4):
                    sp.wait_ge(z_out[s], 16 * rounds)

            @block.tensor
            def _(pe):
                def step(i, s, last=False):
                    if not (last and s >= 2):
                        pe_T(pe, *at(i, s + 2))
                    pe_hT(pe, i, s)
                    if not (last and s == 3):
                        pe_h(pe, *at(i, s + 1))
                    pe_z(pe, i, s)
                pe_T(pe, 0, 0)
                pe_T(pe, 0, 1)
                pe_h(pe, 0, 0)
                for s in range(4):
                    step(0, s)
                with pe.Fori(1, rounds - 1) as i:
                    for s in range(4):
                        step(i, s)
                for s in range(4):
                    step(rounds - 1, s, last=True)

            @block.scalar
            def _(act):
                def step(i, s, last=False):
                    if not (last and s >= 2):
                        act_yT(act, *at(i, s + 2))
                    act_hT(act, i, s)
                act_yT(act, 0, 0)
                act_yT(act, 0, 1)
                for s in range(4):
                    step(0, s)
                with act.Fori(1, rounds - 1) as i:
                    for s in range(4):
                        step(i, s)
                for s in range(4):
                    step(rounds - 1, s, last=True)

            @block.vector
            def _(v):
                def step(i, s, last=False):
                    if not (last and s == 3):
                        vec_h(v, *at(i, s + 1))
                    vec_z(v, i, s)
                vec_h(v, 0, 0)
                for s in range(4):
                    step(0, s)
                with v.Fori(1, rounds - 1) as i:
                    for s in range(4):
                        step(i, s)
                for s in range(4):
                    step(rounds - 1, s, last=True)


def finish(nc, A, K, pos, out):
    G = NT // 4
    with ExitStack() as ctx:
        sb = lambda n, s, d=F32: ctx.enter_context(nc.sbuf_tensor(f"o_{n}", s, d))
        sem = lambda n: ctx.enter_context(nc.semaphore(f"o_{n}"))
        zg = sb("zg", [P, NT, P])
        zn, zm = sb("zn", [P, 2, 4, P]), sb("zm", [P, 2, 4, P])
        gw, gb = sb("gw", [P, P]), sb("gb", [P, P])
        back = [sem(f"back{g}") for g in range(4)]
        var_ready, std_ready, rstd_ready = sem("var"), sem("std"), sem("rstd")
        tab_done, sum_done, bn_done, zn_ready, zm_ready, xb_done, out_ready, stored = (
            sem(n) for n in ("tab_done", "sum_done", "bn_done", "zn_ready", "zm_ready", "xb_done", "out_ready", "stored"))
        over = lambda row: row.unsqueeze(1).to_broadcast([P, 4, P])
        four = lambda t, g: t[:, ds(4 * g, 4), :]

        with nc.Block() as block:
            @block.gpsimd
            def _(pool):
                for n in range(NT):
                    pool.indirect_dma_start(out=zg[:, n, :], out_offset=None, in_=A["zs"],
                                            in_offset=bass.IndirectOffsetOnAxis(ap=pos[:, n:n + 1], axis=0))\
                        .then_inc(back[n // 16], 16)
                pool.wait_ge(tab_done, 2)

                def scale(i):
                    for s in range(2):
                        g = 2 * i + s
                        pool.wait_ge(zn_ready, 4 * g + 4)
                        wait(pool, out_ready, 2 * i)
                        pool.tensor_tensor(zm[:, s, :, :], zn[:, s, :, :], over(gw[:, :]), ALU.mult).then_inc(zm_ready, 1)
                scale(0)
                with pool.Fori(1, G // 2) as i:
                    scale(i)

            @block.vector
            def _(v):
                v.tensor_tensor(gw[:, :], K.rows[:, 2, :], K.tab[:, 2, :], ALU.mult).then_inc(tab_done, 1)
                v.tensor_tensor(gb[:, :], K.rows[:, 3, :], K.tab[:, 2, :], ALU.mult).then_inc(tab_done, 1)
                v.wait_ge(tab_done, 2)
                with v.Fori(0, G) as g:
                    v.tensor_tensor(four(K.X, g), four(K.X, g), over(gb[:, :]), ALU.add).then_inc(xb_done, 1)
                for q in range(4):
                    v.wait_ge(back[q], 16 * 16)
                    with v.Fori(4 * q, 4 * q + 4) as g:
                        v.tensor_tensor(four(K.U, g), four(K.U, g), four(zg, g), ALU.add).then_inc(sum_done, 1)
                    v.wait_ge(sum_done, 4 * q + 4)
                    with v.Fori(4 * q, 4 * q + 4) as g:
                        for j in range(4):
                            tile_stats(v, K, K.U, 4 * g + j, bn_done)
                v.wait_ge(bn_done, NT)
                finish_stats_vector(v, K, var_ready, std_ready, rstd_ready)
                v.wait_ge(xb_done, G)
                with v.Fori(0, G // 2) as i:
                    for s in range(2):
                        g = 2 * i + s
                        v.wait_ge(zm_ready, g + 1)
                        v.tensor_tensor(four(K.X, g), four(K.X, g), zm[:, s, :, :], ALU.add).then_inc(out_ready, 1)

            @block.scalar
            def _(act):
                finish_stats_scalar(act, K, var_ready, std_ready, rstd_ready)

                def normalise(g, s):
                    wait(act, zm_ready, g - 1)
                    for t in range(4):
                        act.activation(zn[:, s, t, :], K.U[:, ds(4 * g + t, 1), :].rearrange("p a f -> p (a f)"),
                                       ACT.Identity, bias=K.nmr[:, ds(4 * g + t, 1)],
                                       scale=K.rstd[:, ds(4 * g + t, 1)]).then_inc(zn_ready, 1)
                normalise(0, 0)
                normalise(1, 1)
                with act.Fori(1, G // 2) as i:
                    normalise(2 * i, 0)
                    normalise(2 * i + 1, 1)

            @block.sync
            def _(sp):
                xo = out.rearrange("b (n t) f -> t b n f", t=8)
                for q in range(4):
                    sp.wait_ge(out_ready, 4 * q + 4)
                    for t in range(8):
                        sp.dma_start(xo[t][:, 16 * q:16 * q + 16, :], K.X[16 * t:16 * t + 16, 16 * q:16 * q + 16, :])\
                          .then_inc(stored, 16)
                sp.wait_ge(stored, 32 * 16)




def constants():
    import numpy as np
    k = {}
    i = np.arange(P)
    k["k_ident"] = np.eye(P, dtype=np.float32)
    k["k_utri"] = (i[:, None] <= i[None, :]).astype(np.float32)
    k["k_ustrict"] = (i[:, None] < i[None, :]).astype(np.float32)
    k["k_centre"] = (np.eye(P) - (i[:, None] // D == i[None, :] // D) / D).astype(np.float32)
    k["k_blk"] = np.repeat((i[:, None] // D == np.arange(H)[None, :]).astype(np.float32), 9, axis=1)
    inv = (np.float32(1.0) / np.float32(10000.0) ** (np.arange(0, D, 2, dtype=np.float32) / np.float32(D))).astype(np.float32)
    freqs = (np.arange(T, dtype=np.float32)[:, None] * inv[None, :]).astype(np.float32)
    emb = np.concatenate([freqs, freqs], axis=-1)
    cos, sin = np.cos(emb).astype(np.float64), np.sin(emb).astype(np.float64)
    sin[:, :D // 2] *= -1.0
    gam = 1.0 - 2.0 ** (-5.0 - np.arange(H))
    t = np.arange(T)[:, None, None]
    up = gam[None, :, None] ** t * D ** -0.5
    down = gam[None, :, None] ** (-t)
    for name, f in (("k_rope_c", cos), ("k_rope_s", sin)):
        q = (f[:, None, :] * up).reshape(T, P)
        kk = (f[:, None, :] * down).reshape(T, P)
        k[name] = np.concatenate([q, kk], axis=1).astype(np.float32)
    g = (i[:, None] % 32) // 16 != (np.arange(32)[None, :] // 16)
    k["k_smask"] = np.where(g, NEG, 0.0).astype(np.float32)
    k["k_tie"] = np.tile((E - np.arange(E, dtype=np.float32))[None, :], (P, 1))
    k["k_iota"] = np.tile(np.arange(SLOTS, dtype=np.float32)[None, :], (P, 1))
    return k


_INS = ['L0_attn_x', 'L0_attn_w_attn', 'L0_attn_w_proj', 'L0_ffn_W_r', 'L0_ffn_W_k', 'L0_ffn_W_v', 'L0_ffn_mu_r',
        'L0_ffn_mu_k', 'L0_c', 'L0_wmod', 'L1_attn_Wq', 'L1_attn_Wk', 'L1_attn_Wv', 'L1_attn_Wg', 'L1_attn_Wo',
        'L1_attn_gn_w', 'L1_attn_gn_b', 'L1_ffn_Wqkv', 'L1_ffn_bqkv', 'L1_ffn_Wo', 'L1_ffn_bo', 'L1_ffn_g1',
        'L1_ffn_be1', 'L1_ffn_g2', 'L1_ffn_be2', 'L1_ffn_Wg', 'L1_ffn_W1', 'L1_ffn_b1', 'L1_ffn_W2', 'L1_ffn_b2',
        'L1_c', 'L1_wmod']


class Kept:
    pass


def build(nc, A, out):
    K = Kept()
    with ExitStack() as ctx:
        sb = lambda n, s, d=F32: ctx.enter_context(nc.sbuf_tensor(n, s, d))
        sem = lambda n: ctx.enter_context(nc.semaphore(n))
        K.X = sb("X", [P, NT, P])
        K.bn, K.diff, K.var, K.std = sb("bn", [P, NT, 6]), sb("diff", [P, NT]), sb("var", [P, NT]), sb("std", [P, NT])
        K.rstd, K.nmr, K.eps = sb("rstd", [P, NT]), sb("nmr", [P, NT]), sb("eps", [P, 1])
        K.ident, K.utri = sb("ident", [P, P]), sb("utri", [P, P])
        K.W = sb("W", [P, 11, P])
        K.wg8, K.cols, K.mod, K.tab = sb("wg8", [P, E]), sb("cols", [P, 7]), sb("mod", [P, 6, B]), sb("tab", [P, 3, P])
        K.bo, K.rows, K.smask = sb("bo", [P, P]), sb("rows", [P, 4, P]), sb("smask", [P, 32])
        K.w1, K.w2 = sb("w1", [P, E, DF]), sb("w2", [P, E, FC, P])
        K.x_in = [sem(f"x_in{g}") for g in range(4)]
        K.ys_zero = sem("ys_zero")
        with ExitStack() as early:
            sb2 = lambda n, s, d=F32: early.enter_context(nc.sbuf_tensor(n, s, d))
            K.wgate = sb2("wgate", [P, 3, B, P])
            K.wqkv0, K.wo1, K.cmat = sb2("wqkv0", [P, 3 * P]), sb2("wo1", [P, P]), sb2("cmat", [P, P])
            K.blk = sb2("blk", [P, H, 9])
            K.rope_c, K.rope_s = sb2("rope_c", [P, TPB, 2 * P]), sb2("rope_s", [P, TPB, 2 * P])
            prologue(nc, A, K)
            attention(nc, A, K, 0)
            token_shift_ffn(nc, A, K)
            attention(nc, A, K, 1)
        clear_semaphores(nc)
        K.U = sb("U", [P, NT, P])
        attend_batches(nc, A, K)
        clear_semaphores(nc)
        experts(nc, A, K, out)


def clear_semaphores(nc):
    released = sorted(nc.released_uncleared_semaphores)
    with nc.Block() as block:
        @block.gpsimd
        def _(pool):
            start = 0
            for i in range(1, len(released) + 1):
                if i == len(released) or released[i] != released[i - 1] + 1:
                    pool.sem_clear(range(released[start], released[i - 1] + 1))
                    start = i


def kernel(**inputs):
    import numpy as np
    import concourse.bacc as _bacc
    from concourse.bass_utils import run_bass_kernel_spmd as _run

    nc = _bacc.Bacc("TRN2", target_bir_lowering=False, num_devices=1)
    arrays, A = {}, {}
    for name in _INS:
        a = np.ascontiguousarray(inputs[name])
        arrays[f"in_{name}_dram"] = a
        A[name] = nc.dram_tensor(f"in_{name}_dram", a.shape, mybir.dt.from_np(a.dtype), kind="ExternalInput").ap()
    for name, a in constants().items():
        arrays[f"in_{name}_dram"] = a
        A[name] = nc.dram_tensor(f"in_{name}_dram", a.shape, mybir.dt.from_np(a.dtype), kind="ExternalInput").ap()
    A["xs"] = nc.dram_tensor("xs", (B * T, C), F32, kind="Internal").ap()
    A["ys"] = nc.dram_tensor("ys", (SLOTS * P, C), F32, kind="Internal").ap()
    A["zs"] = nc.dram_tensor("zs", (SLOTS * P, C), F32, kind="Internal").ap()
    out = nc.dram_tensor("out_0_dram", (B, T, C), F32, kind="ExternalOutput").ap()
    build(nc, A, out)
    r = _run(nc, [arrays], core_ids=[0])
    return r.results[0]["out_0_dram"]
```

```python
from contextlib import ExitStack

import concourse.bass as bass
from concourse import mybir

F32 = mybir.dt.float32
I32 = mybir.dt.int32
U32 = mybir.dt.uint32
ALU = mybir.AluOpType
ACT = mybir.ActivationFunctionType
AX = mybir.AxisListType

B, T, C = 16, 512, 128
P = 128
TPB = T // P
NT = B * TPB
H, D = 16, 8
EPS = 1e-5
EPS_DEN = 1e-6
GATE_MIN = 0.25
FH, FD = 4, 32
E, DF = 8, 512
FC = DF // P
SLOTS = 72
NEG = -1e30
ds = bass.ds

W_PROJT, W_RT, W_KT, W_Q1, W_K1, W_V1, W_G1, W_FQ, W_FK, W_FV, W_FO = range(11)
SA0, CA0, SB0, CB0, SA1, CA1 = range(6)
MU_R, MU_K, GN_W, GN_B, BQ, BK, BV = range(7)


def wait(e, sem, value):
    if isinstance(value, int) and value <= 0:
        return
    e.wait_ge(sem, value)


def prologue(nc, A, K):
    with ExitStack() as ctx:
        sb = lambda n, s, d=F32: ctx.enter_context(nc.sbuf_tensor(n, s, d))
        sem = lambda n: ctx.enter_context(nc.semaphore(n))
        ps = [ctx.enter_context(nc.psum_tensor(f"p0_{i}", [P, 512], F32)) for i in range(8)]
        craw = sb("craw", [32, P])
        wmod = [sb(f"wmod{l}", [P, 6 * P]) for l in range(2)]
        raw = sb("raw", [P, 12, P])
        raw8 = sb("raw8", [E, P])
        sc = sb("sc", [P, 32])
        sc_rep = sb("sc_rep", [P, 8, 16])
        gates = sb("gates", [P, 3, 16])
        bv_rep = sb("bv_rep", [P, P])
        bo_row = sb("bo_row", [P, P])
        diag = sb("diag", [P, 2, 4, P])
        ct = [sb(f"ct{i}", [P, P]) for i in range(3)]
        cg = [sb(f"cg{i}", [P, 48]) for i in range(3)]

        s_c, s_w, s_v, s_tab = sem("s_c"), sem("s_w"), sem("s_v"), sem("s_tab")
        silu_done, crep, csT = sem("silu_done"), sem("crep"), sem("csT")
        mod_ps, mod_done, gate_done = sem("mod_ps"), sem("mod_done"), sem("gate_done")
        chain, tab_ps = sem("chain0"), sem("tab_ps")
        wt_ps, wt_done = sem("wt_ps"), sem("wt_done")
        diag_vec, diag_pool, wg_ps, wg_done = sem("diag_vec"), sem("diag_pool"), sem("wg_ps"), sem("wg_done")
        bo_ps, vrep, zset, stats = sem("bo_ps"), sem("vrep"), sem("zset"), sem("stats0")
        ident_in = sem("ident_in")

        col = lambda v: v.rearrange("(p a) -> p a", a=1)
        row = lambda v: v.rearrange("(a n) -> a n", a=1)

        raws = [A["L0_attn_w_proj"], A["L0_ffn_W_r"], A["L0_ffn_W_k"], A["L1_attn_Wq"], A["L1_attn_Wk"],
                A["L1_attn_Wv"], A["L1_attn_Wg"], A["L1_ffn_Wqkv"][0:P, :], A["L1_ffn_Wqkv"][P:2 * P, :],
                A["L1_ffn_Wqkv"][2 * P:3 * P, :], A["L1_ffn_Wo"], A["L0_ffn_W_v"]]

        def diagonals(e, g, done):
            if g >= 2:
                e.wait_ge(wg_ps, g - 1)
            e.tensor_tensor(diag[:, g % 2, :, :], K.ident[:, :].unsqueeze(1).to_broadcast([P, 4, P]),
                            gates[:, g // 4, 4 * (g % 4):4 * (g % 4) + 4].unsqueeze(2).to_broadcast([P, 4, P]),
                            ALU.mult).then_inc(done, 1)

        with nc.Block() as block:
            @block.sync
            def _(sp):
                sp.dma_start(craw[0:16, :], A["L0_c"]).then_inc(s_c, 16)
                sp.dma_start(craw[16:32, :], A["L1_c"]).then_inc(s_c, 16)
                sp.dma_start(K.ident[:, :], A["k_ident"]).then_inc(ident_in, 16)
                for l in range(2):
                    sp.dma_start(wmod[l][:, :], A[f"L{l}_wmod"]).then_inc(s_c, 16)
                for g in range(4):
                    sp.dma_start(K.X[:, 16 * g:16 * g + 16, :],
                                 A["L0_attn_x"].rearrange("b (t p) f -> p (b t) f", p=P)[:, 16 * g:16 * g + 16, :])\
                      .then_inc(K.x_in[g], 16)
                for i, w in enumerate(raws[8:]):
                    sp.dma_start(raw[:, 8 + i, :], w).then_inc(s_w, 16)
                sp.dma_start(raw8[:, :], A["L1_ffn_Wg"]).then_inc(s_w, 16)
                sp.dma_start(K.wo1[:, :], A["L1_attn_Wo"]).then_inc(s_w, 16)
                sp.dma_start(K.cmat[:, :], A["k_centre"]).then_inc(s_w, 16)
                sp.dma_start(K.wqkv0[:, :], A["L0_attn_w_attn"]).then_inc(s_tab, 16)
                sp.dma_start(K.utri[:, :], A["k_utri"]).then_inc(s_tab, 16)
                sp.dma_start(K.blk[:, :, :], A["k_blk"].rearrange("p (h j) -> p h j", h=H)).then_inc(s_tab, 16)
                vecs = [A["L0_ffn_mu_r"], A["L0_ffn_mu_k"], A["L1_attn_gn_w"], A["L1_attn_gn_b"],
                        A["L1_ffn_bqkv"][0:P], A["L1_ffn_bqkv"][P:2 * P], A["L1_ffn_bqkv"][2 * P:3 * P]]
                for i, v in enumerate(vecs):
                    sp.dma_start(K.cols[:, i:i + 1], col(v)).then_inc(s_v, 16)
                sp.dma_start(bo_row[:, :], row(A["L1_ffn_bo"]).to_broadcast([P, P])).then_inc(s_v, 16)
                sp.wait_ge(s_v, 8 * 16)
                sp.wait_ge(s_tab, 3 * 16)

            @block.scalar
            def _(act):
                for i, w in enumerate(raws[0:8]):
                    act.dma_start(raw[:, i, :], w).then_inc(s_w, 16)
                act.wait_ge(csT, 1)
                act.activation(sc[:, :], ps[0][:, 0:32], ACT.Silu).then_inc(silu_done, 1)
                for g in range(3):
                    n = min(4, 11 - 4 * g)
                    act.wait_ge(wt_ps, g + 1)
                    act.activation(K.W[:, 4 * g:4 * g + n, :].rearrange("p a b -> p (a b)"), ps[2 + g][:, 0:n * P],
                                   ACT.Copy).then_inc(wt_done, 1)
                act.wait_ge(wt_ps, 4)
                act.activation(K.wg8[:, :], ps[5][:, 0:E], ACT.Copy).then_inc(wt_done, 1)
                for g in range(12):
                    act.wait_ge(wg_ps, g + 1)
                    act.activation(K.wgate[:, g // 4, 4 * (g % 4):4 * (g % 4) + 4, :].rearrange("p a b -> p (a b)"),
                                   ps[6 + g % 2][:, :], ACT.Copy).then_inc(wg_done, 1)

            @block.tensor
            def _(pe):
                pe.wait_ge(s_c, 64)
                pe.wait_ge(ident_in, 16)
                pe.transpose(ps[0][:, 0:32], craw[:, :], K.ident[0:32, 0:32]).then_inc(csT, 1)
                pe.wait_ge(silu_done, 1)
                kinds = [(0, 0), (0, 1), (0, 3), (0, 4), (1, 0), (1, 1), (0, 2), (0, 5), (1, 2)]
                for i, (l, k) in enumerate(kinds):
                    mm = pe.matmul(ps[1][:, 16 * i:16 * i + 16], wmod[l][:, k * P:(k + 1) * P],
                                   sc[:, 16 * l:16 * l + 16], start=True, stop=True)
                mm.then_inc(mod_ps, 1)
                pe.wait_ge(crep, 1)
                pe.matmul(ps[0][:, 0:3 * P], sc_rep[:, :, :].rearrange("p a b -> p (a b)"),
                          wmod[1][:, 3 * P:6 * P], start=True, stop=True).then_inc(tab_ps, 1)
                pe.wait_ge(s_w, 15 * 16)
                for i in range(11):
                    o = ps[2 + i // 4][:, (i % 4) * P:(i % 4 + 1) * P]
                    if i == W_V1:
                        mm = pe.matmul(o, raw[:, i, :], K.cmat[:, :], start=True, stop=True)
                    else:
                        mm = pe.transpose(o, raw[:, i, :], K.ident[:, :])
                    if i % 4 == 3 or i == 10:
                        mm.then_inc(wt_ps, 1)
                pe.transpose(ps[5][:, 0:E], raw8[:, :], K.ident[0:E, 0:E]).then_inc(wt_ps, 1)
                pe.wait_ge(wt_done, 4)
                lhs = [K.W[:, W_PROJT, :], raw[:, 11, :], K.wo1[:, :]]
                for g in range(12):
                    pe.wait_ge((diag_vec, diag_pool)[g % 2], g // 2 + 1)
                    if g >= 2:
                        pe.wait_ge(wg_done, g - 1)
                    for j in range(4):
                        mm = pe.matmul(ps[6 + g % 2][:, j * P:(j + 1) * P], lhs[g // 4], diag[:, g % 2, j, :],
                                       start=True, stop=True)
                    mm.then_inc(wg_ps, 1)
                pe.wait_ge(vrep, 1)
                pe.matmul(ps[5][:, P:2 * P], bv_rep[:, :], K.W[:, W_FO, :], start=True, stop=True).then_inc(bo_ps, 1)

            @block.gpsimd
            def _(pool):
                pool.memset(K.eps[:, :], EPS).then_inc(zset, 1)
                pool.wait_ge(diag_vec, 1)
                for g in range(1, 12, 2):
                    diagonals(pool, g, diag_pool)

            @block.vector
            def _(v):
                count = [0]

                def link(ins):
                    count[0] += 1
                    ins.then_inc(chain, 1)
                    v.wait_ge(chain, count[0])

                def clamp(out, x, tmp):
                    link(v.scalar_tensor_tensor(out=tmp[0], in0=x, scalar=-1.0, in1=x, op0=ALU.mult, op1=ALU.max))
                    link(v.tensor_scalar(tmp[1], x, 0.0, 2.0, ALU.is_ge, ALU.mult))
                    link(v.tensor_scalar(tmp[0], tmp[0], GATE_MIN, None, ALU.max))
                    link(v.scalar_tensor_tensor(out=out, in0=tmp[1], scalar=-1.0, in1=tmp[0],
                                                op0=ALU.add, op1=ALU.mult))

                def x_stats(n):
                    if n % 16 == 0:
                        v.wait_ge(K.x_in[n // 16], 16)
                    tile_stats(v, K, K.X, n, stats)

                for n in range(24):
                    x_stats(n)
                v.wait_ge(silu_done, 1)
                v.tensor_copy(sc_rep[:, :, :], sc[:, 16:32].unsqueeze(1).to_broadcast([P, 8, 16])).then_inc(crep, 1)
                v.wait_ge(mod_ps, 1)
                v.tensor_copy(K.mod[:, :, :].rearrange("p k b -> p (k b)"), ps[1][:, 0:96]).then_inc(mod_done, 1)
                link(v.tensor_copy(cg[2][:, :], ps[1][:, 96:144]))
                v.wait_ge(mod_done, 1)
                for k in (CA0, CB0, CA1):
                    link(v.tensor_scalar(K.mod[:, k, :], K.mod[:, k, :], 1.0, None, ALU.add))
                clamp(gates[:, :, :].rearrange("p k b -> p (k b)"), cg[2][:, :], [cg[0][:, :], cg[1][:, :]])
                for g in range(0, 12, 2):
                    diagonals(v, g, diag_vec)
                    for n in range(24 + 40 * g // 12, 24 + 40 * (g + 2) // 12):
                        x_stats(n)
                v.wait_ge(s_v, 8 * 16)
                v.tensor_copy(bv_rep[:, :], K.cols[:, BV:BV + 1].to_broadcast([P, P])).then_inc(vrep, 1)
                v.wait_ge(tab_ps, 1)
                link(v.tensor_copy(K.tab[:, 0, :], ps[0][:, 0:P]))
                link(v.tensor_scalar(K.tab[:, 1, :], ps[0][:, P:2 * P], 1.0, None, ALU.add))
                link(v.tensor_copy(ct[2][:, :], ps[0][:, 2 * P:3 * P]))
                clamp(K.tab[:, 2, :], ct[2][:, :], [ct[0][:, :], ct[1][:, :]])
                v.wait_ge(bo_ps, 1)
                link(v.tensor_tensor(K.bo[:, :], ps[5][:, P:2 * P], bo_row[:, :], ALU.add))


def finish_stats_vector(v, K, var_ready, std_ready, rstd_ready, part=0, parts=1):
    n = slice(part * NT // parts, (part + 1) * NT // parts)
    mean0, m20, mean1, m21 = (K.bn[:, n, i] for i in (1, 2, 4, 5))
    v.tensor_tensor(K.diff[:, n], mean0, mean1, ALU.subtract).then_inc(var_ready, 1)
    v.tensor_tensor(K.var[:, n], m20, m21, ALU.add).then_inc(var_ready, 1)
    v.wait_ge(var_ready, 5 * part + 2)
    v.scalar_tensor_tensor(out=K.std[:, n], in0=K.diff[:, n], scalar=P / 4.0, in1=K.diff[:, n],
                           op0=ALU.mult, op1=ALU.mult).then_inc(var_ready, 1)
    v.wait_ge(var_ready, 5 * part + 3)
    v.tensor_tensor(K.var[:, n], K.var[:, n], K.std[:, n], ALU.add).then_inc(var_ready, 1)
    v.tensor_tensor(K.diff[:, n], mean0, mean1, ALU.add).then_inc(var_ready, 1)
    v.wait_ge(std_ready, part + 1)
    v.reciprocal(K.rstd[:, n], K.std[:, n]).then_inc(rstd_ready, 1)
    v.wait_ge(rstd_ready, 2 * part + 1)
    v.wait_ge(var_ready, 5 * part + 5)
    v.scalar_tensor_tensor(out=K.nmr[:, n], in0=K.diff[:, n], scalar=-0.5, in1=K.rstd[:, n],
                           op0=ALU.mult, op1=ALU.mult).then_inc(rstd_ready, 1)


def finish_stats_scalar(act, K, var_ready, std_ready, rstd_ready, part=0, parts=1):
    n = slice(part * NT // parts, (part + 1) * NT // parts)
    act.wait_ge(var_ready, 5 * part + 4)
    act.activation(K.std[:, n], K.var[:, n], ACT.Sqrt, bias=K.eps[:, 0:1], scale=1.0 / P).then_inc(std_ready, 1)
    act.wait_ge(rstd_ready, 2 * part + 2)


def tile_stats(v, K, x, n, done):
    v.bn_stats(K.bn[:, ds(n, 1), :].rearrange("p a f -> p (a f)"), x[:, ds(n, 1), :].rearrange("p a f -> p (a f)"))\
     .then_inc(done, 1)


def attention(nc, A, K, layer):
    J = 9 if layer == 0 else 8
    SC = D * J
    heads = [(0, 6), (6, 11), (11, 16)]
    banks_halved = 3
    HH = heads[banks_halved - 1][1]
    sh, scl = (SA0, CA0) if layer == 0 else (SA1, CA1)
    with ExitStack() as ctx:
        sb = lambda n, s, d=F32: ctx.enter_context(nc.sbuf_tensor(f"a{layer}_{n}", s, d))
        sem = lambda n: ctx.enter_context(nc.semaphore(f"a{layer}_{n}"))
        pb = lambda n: ctx.enter_context(nc.psum_tensor(f"a{layer}_{n}", [P, 512], F32))
        pS = [pb(f"pS{c}") for c in range(3)]
        pR, pT, pQ, pI, pO = pb("pR"), pb("pT"), pb("pQ"), pb("pI"), pb("pO")

        xn = sb("xn", [P, TPB, P])
        hT = sb("hT", [P, TPB * P])
        qk = sb("qk", [P, TPB, 2 * P])
        vv = sb("vv", [P, TPB, H, J])
        kv = sb("kv", [P, 2, H, D, J])
        tt = sb("tt", [P, 2, H, D + 1, J])
        R = sb("R", [P, H, J])
        qT = sb("qT", [P, P])
        nd = sb("nd", [P, 2, H, J])
        rec = sb("rec", [P, H])
        y = sb("y", [P, P])
        yT = sb("yT", [P, P])
        if layer == 0:
            ea = sb("ea", [P, 2, 2 * P])
            eb = sb("eb", [P, 2, 2 * P])
            den = sb("den", [P, H])
            wqkv = K.wqkv0[:, :]
        else:
            ra = sb("ra", [P, 2, 2 * P])
            rb = sb("rb", [P, 2, 2 * P])
            gate = sb("gate", [P, 2 * T])
            sq = sb("sq", [P, P])
            vs = sb("vs", [P, H])
            sd = sb("sd", [P, H])
            yaff = sb("yaff", [P, P])
            wqkv = K.W[:, W_Q1:W_V1 + 1, :].rearrange("p a b -> p (a b)")

        var_ready, std_ready, rstd_ready = sem("var"), sem("std"), sem("rstd")
        half_done, tab_in = sem("half_done"), sem("tab_in")
        xn_ready, xn_T, hT_ready = sem("xn_ready"), sem("xn_T"), sem("hT_ready")
        qkv_ps, v_ready, e_ready, qk_ready = sem("qkv_ps"), sem("v_ready"), sem("e_ready"), sem("qk_ready")
        ones_set, relu_done = sem("ones_set"), sem("relu_done")
        gate_ps, gate_ready, rope_read, rope_b = sem("gate_ps"), sem("gate_ready"), sem("rope_read"), sem("rope_b")
        kv_ready, u_done, t_done, red_done = sem("kv_ready"), sem("u_done"), sem("t_done"), sem("red_done")
        p_done, r_ready, q_T, qT_ready = sem("p_done"), sem("r_ready"), sem("q_T"), sem("qT_ready")
        inter_ps, inter_ready = sem("inter_ps"), sem("inter_ready")
        den_done, rec_done, y_ready, y_T, yT_ready = (sem("den_done"), sem("rec_done"), sem("y_ready"),
                                                      sem("y_T"), sem("yT_ready"))
        aff_done, sq_done, var_done, sd_done = sem("aff_done"), sem("sq_done"), sem("var_done"), sem("sd_done")
        proj_ps, x_done, bn_done, x_out = sem("proj_ps"), sem("x_done"), sem("bn_done"), sem("x_out")

        YT = P + H * J
        yT_read = yT_ready if layer == 0 else aff_done
        qk_free = qk_ready if layer == 0 else rope_read

        def tile(t, n):
            return t[:, ds(n, 1), :].rearrange("p a f -> p (a f)")

        def column(t, n):
            return t[:, ds(n, 1)]

        def near(b, t, d):
            if isinstance(b, int) and not 0 <= 4 * b + t + d < NT:
                return None
            return b + (t + d) // 4, (t + d) % 4


        def act_normalise(act, b, t):
            wait(act, xn_T, 4 * b - 3 + t)
            act.activation(xn[:, t, :], tile(K.X, 4 * b + t), ACT.Identity, bias=column(K.nmr, 4 * b + t),
                           scale=column(K.rstd, 4 * b + t)).then_inc(xn_ready, 1)

        def pe_transpose_x(pe, b):
            for t in range(TPB):
                pe.wait_ge(xn_ready, 4 * b + t + 1)
                if t == 0:
                    wait(pe, hT_ready if layer == 0 else gate_ready, b)
                pe.transpose(pT[:, t * P:(t + 1) * P], xn[:, t, :], K.ident[:, :]).then_inc(xn_T, 1)

        def act_modulate(act, b):
            act.wait_ge(xn_T, 4 * b + 4)
            wait(act, qkv_ps, 4 * b)
            if layer == 1:
                wait(act, gate_ps, b)
            act.activation(hT[:, :], pT[:, :], ACT.Identity, bias=column(K.mod[:, sh, :], b),
                           scale=column(K.mod[:, scl, :], b)).then_inc(hT_ready, 1)

        def bank_of(b, t, start):
            return (pQ, pO, pI, pR)[t] if start else pQ

        def pe_qkv(pe, b, t, start=False):
            m = 4 * b + t
            pe.wait_ge(hT_ready, b + 1)
            if not start:
                wait(pe, v_ready, m)
                wait(pe, qk_free, m)
            pe.matmul(bank_of(b, t, start)[:, 0:3 * P], hT[:, t * P:(t + 1) * P], wqkv, start=True, stop=True).then_inc(qkv_ps, 1)

        def act_qkv(act, b, t, start=False):
            m = 4 * b + t
            pQ = bank_of(b, t, start)
            act.wait_ge(qkv_ps, m + 1)
            wait(act, kv_ready, m - 3)
            if t < 3:
                wait(act, p_done, 3 * b - 3 + t + 1)
            act.activation(vv[:, t, :, 0:D], pQ[:, 2 * P:3 * P].rearrange("p (h j) -> p h j", h=H),
                           ACT.Copy).then_inc(v_ready, 1)
            if layer == 0:
                wait(act, e_ready, m - 1)
                act.activation(ea[:, t % 2, :], pQ[:, 0:2 * P], ACT.Relu, scale=-1.0).then_inc(relu_done, 1)
                act.wait_ge(relu_done, m + 1)
                wait(act, qk_ready, m - 1)
                act.activation(eb[:, t % 2, :], ea[:, t % 2, :], ACT.Exp, scale=-1.0).then_inc(e_ready, 1)

        def slot_free(e, b, t):
            m = 4 * b + t
            wait(e, kv_ready, m - 3)
            wait(e, t_done, 3 * (m - 3))
            if t < 3:
                wait(e, p_done, 3 * b - 3 + t + 1)
            if t > 0:
                wait(e, q_T, 3 * b - 3 + t)

        def vec_qk(v, b, t, start=False):
            m = 4 * b + t
            pQ = bank_of(b, t, start)
            if layer == 0:
                v.wait_ge(e_ready, m + 1)
                v.wait_ge(v_ready, m + 1)
                slot_free(v, b, t)
                v.scalar_tensor_tensor(out=qk[:, t, :], in0=pQ[:, 0:2 * P], scalar=1.0, in1=eb[:, t % 2, :],
                                       op0=ALU.add, op1=ALU.max).then_inc(qk_ready, 1)
            else:
                v.wait_ge(v_ready, m + 1)
                wait(v, qk_ready, m - 1)
                v.tensor_tensor(ra[:, t % 2, :], pQ[:, 0:2 * P], K.rope_c[:, t, :], ALU.mult).then_inc(rope_b, 1)
                pv = pQ[:, 0:2 * P].rearrange("p (g u i) -> p g u i", u=2, i=D // 2)
                rv = rb[:, t % 2, :].rearrange("p (g u i) -> p g u i", u=2, i=D // 2)
                sv = K.rope_s[:, t, :].rearrange("p (g u i) -> p g u i", u=2, i=D // 2)
                v.tensor_tensor(rv[:, :, 0, :], pv[:, :, 1, :], sv[:, :, 0, :], ALU.mult).then_inc(rope_b, 1)
                v.tensor_tensor(rv[:, :, 1, :], pv[:, :, 0, :], sv[:, :, 1, :], ALU.mult).then_inc(rope_read, 1)

        def pool_rope(pool, b, t):
            m = 4 * b + t
            pool.wait_ge(rope_read, m + 1)
            pool.wait_ge(rope_b, 2 * m + 2)
            slot_free(pool, b, t)
            pool.tensor_tensor(qk[:, t, :], ra[:, t % 2, :], rb[:, t % 2, :], ALU.add).then_inc(qk_ready, 1)

        def pool_kv(pool, n, t):
            pool.wait_ge(qk_ready, n + 1)
            pool.wait_ge(v_ready, n + 1)
            wait(pool, u_done, 3 * (n - 1))
            kk = qk[:, t, P:2 * P].rearrange("p (h i) -> p h i", h=H)
            pool.tensor_tensor(kv[:, t % 2, :, :, :], kk.unsqueeze(3).to_broadcast([P, H, D, J]),
                               vv[:, t, :, :].unsqueeze(2).to_broadcast([P, H, D, J]), ALU.mult).then_inc(kv_ready, 1)

        def pe_states(pe, b, t):
            n = 4 * b + t
            pe.wait_ge(kv_ready, n + 1)
            flat = kv[:, t % 2, :, :, :].rearrange("p h i j -> p (h i j)")
            for c, (h0, h1) in enumerate(heads):
                wait(pe, t_done, 3 * (n - 1) + c + 1)
                pe.matmul(pS[c][:, 0:(h1 - h0) * SC], K.utri[:, :], flat[:, h0 * SC:h1 * SC],
                          start=True, stop=True).then_inc(u_done, 1)

        def pe_inter(pe, b, t):
            pe.wait_ge(qT_ready, 3 * b + t)
            pe.wait_ge(r_ready, 3 * b + t)
            wait(pe, yT_read, 4 * b + t - 2)
            pe.matmul(pI[:, P:P + H * J], qT[:, :], R[:, :, :].rearrange("p h j -> p (h j)"),
                      start=True, stop=True).then_inc(inter_ps, 1)

        def pe_state_sum(pe, b, t):
            wait(pe, r_ready, 3 * b + t)
            pe.wait_ge(v_ready, 4 * b + t + 1)
            pe.matmul(pR[:, 0:H * J], qk[:, t, P:2 * P], vv[:, t, :, :].rearrange("p h j -> p (h j)"),
                      start=(t == 0), stop=True, skip_group_check=True).then_inc(p_done, 1)

        def pe_transpose_q(pe, b, t):
            pe.wait_ge(qk_ready, 4 * b + t + 1)
            wait(pe, inter_ready, 3 * b + t - 1)
            pe.transpose(pI[:, 0:P], qk[:, t, 0:P], K.ident[:, :]).then_inc(q_T, 1)

        def pe_transpose_y(pe, b, t):
            m = 4 * b + t
            pe.wait_ge(y_ready, m + 1)
            if t != 2 and near(b, t, 2):
                pe.wait_ge(inter_ready, 3 * b + (2, 3, None, 4)[t])
            else:
                wait(pe, yT_read, m)
            pe.transpose(pI[:, YT:YT + P], y[:, :], K.ident[:, :]).then_inc(y_T, 1)

        def pe_project(pe, b, t):
            m = 4 * b + t
            pe.wait_ge(yT_ready, m + 1)
            wait(pe, x_done, m)
            pe.matmul(pO[:, 0:P], yT[:, :], tile(K.wgate[:, 0 if layer == 0 else 2, :, :], b),
                      start=True, stop=True).then_inc(proj_ps, 1)

        def act_inter(act, b, t):
            n = 4 * b + t
            act.wait_ge(inter_ps, 3 * b + t)
            wait(act, red_done, n - 1)
            act.activation(tt[:, t % 2, :, D, :], pI[:, P:P + H * J].rearrange("p (h j) -> p h j", h=H),
                           ACT.Copy).then_inc(inter_ready, 1)

        def act_qT(act, b, t):
            act.wait_ge(q_T, 3 * b + t)
            wait(act, inter_ps, 3 * b + t - 1)
            act.activation(qT[:, :], pI[:, 0:P], ACT.Copy).then_inc(qT_ready, 1)

        def act_yT(act, b, t):
            m = 4 * b + t
            act.wait_ge(y_T, m + 1)
            if layer == 0:
                wait(act, proj_ps, m)
                act.activation(yT[:, :], pI[:, YT:YT + P], ACT.Copy).then_inc(yT_ready, 1)
            else:
                wait(act, yT_ready, m)
                act.activation(yaff[:, :], pI[:, YT:YT + P], ACT.Identity, bias=K.cols[:, GN_B:GN_B + 1],
                               scale=K.cols[:, GN_W:GN_W + 1]).then_inc(aff_done, 1)

        def pool_gate(pool, b, t, half):
            m = 4 * b + t
            pool.wait_ge(aff_done, m + 1)
            pool.wait_ge(gate_ready, b + 1)
            wait(pool, proj_ps, m)
            pool.tensor_tensor(yT[:, :], yaff[:, :], gate[:, half * T + t * P:half * T + (t + 1) * P],
                               ALU.mult).then_inc(yT_ready, 1)

        def vec_products(v, b, t):
            n = 4 * b + t
            q = qk[:, t, 0:P].rearrange("p (h i) -> p h i", h=H)
            wait(v, red_done, n - 1)
            for c, (h0, h1) in enumerate(heads):
                v.wait_ge(u_done, 3 * n + c + 1)
                v.tensor_tensor(tt[:, t % 2, h0:h1, 0:D, :],
                                pS[c][:, 0:(h1 - h0) * SC].rearrange("p (h i j) -> p h i j", i=D, j=J),
                                q[:, h0:h1, :].unsqueeze(3).to_broadcast([P, h1 - h0, D, J]),
                                ALU.mult).then_inc(t_done, 1)

        def vec_state(v, b, t):
            v.wait_ge(p_done, 3 * b + t + 1)
            wait(v, inter_ps, 3 * b + t)
            v.tensor_tensor(R[:, :, :], pR[:, 0:H * J].rearrange("p (h j) -> p h j", h=H), K.blk[:, :, 0:J],
                            ALU.mult).then_inc(r_ready, 1)

        def pool_halve(pool, b, t):
            n = 4 * b + t
            pool.wait_ge(t_done, 3 * n + banks_halved)
            pool.tensor_tensor(tt[:, t % 2, 0:HH, D // 2:D, :], tt[:, t % 2, 0:HH, D // 2:D, :],
                               tt[:, t % 2, 0:HH, 0:D // 2, :], ALU.add).then_inc(half_done, 1)

        def vec_sum(v, b, t):
            n = 4 * b + t
            v.wait_ge(half_done, n + 1)
            v.wait_ge(t_done, 3 * n + 3)
            rows = D
            if t > 0:
                v.wait_ge(inter_ready, 3 * b + t)
                rows = D + 1
            wait(v, y_ready, n - 1)
            for h0, h1, first in ((0, HH, D // 2), (HH, H, 0)):
                if h0 < h1:
                    red = v.tensor_reduce(nd[:, t % 2, h0:h1, :], tt[:, t % 2, h0:h1, first:rows, :]
                                          .rearrange("p h i j -> p h j i"), AX.X, ALU.add)
            red.then_inc(red_done, 1)

        def vec_den(v, n, t):
            v.wait_ge(red_done, n + 1)
            wait(v, rec_done, n)
            v.tensor_scalar(den[:, :], nd[:, t % 2, :, D], EPS_DEN, None, ALU.add).then_inc(den_done, 1)

        def act_square(act, b, t):
            n = 4 * b + t
            act.wait_ge(red_done, n + 1)
            wait(act, var_done, n)
            act.activation(sq[:, :], nd[:, t % 2, :, :].rearrange("p h j -> p (h j)"), ACT.Square)\
               .then_inc(sq_done, 1)

        def act_sd(act, b, t):
            n = 4 * b + t
            act.wait_ge(var_done, n + 1)
            wait(act, rec_done, n)
            act.activation(sd[:, :], vs[:, :], ACT.Sqrt, bias=K.eps[:, 0:1], scale=1.0 / D).then_inc(sd_done, 1)

        def vec_var(v, n):
            v.wait_ge(sq_done, n + 1)
            wait(v, sd_done, n)
            v.tensor_reduce(vs[:, :], sq[:, :].rearrange("p (h j) -> p h j", h=H), AX.X, ALU.add)\
             .then_inc(var_done, 1)

        def vec_rec(v, n):
            wait(v, y_ready, n)
            if layer == 0:
                v.wait_ge(den_done, n + 1)
                v.reciprocal(rec[:, :], den[:, :]).then_inc(rec_done, 1)
            else:
                v.wait_ge(sd_done, n + 1)
                v.reciprocal(rec[:, :], sd[:, :]).then_inc(rec_done, 1)

        def vec_y(v, n, t):
            v.wait_ge(rec_done, n + 1)
            wait(v, y_T, n)
            v.tensor_tensor(y[:, :].rearrange("p (h j) -> p h j", h=H), nd[:, t % 2, :, 0:D],
                            rec[:, :].unsqueeze(2).to_broadcast([P, H, D]), ALU.mult).then_inc(y_ready, 1)

        def vec_residual(v, b, t):
            m = 4 * b + t
            v.wait_ge(proj_ps, m + 1)
            wait(v, x_done, m)
            x = tile(K.X, m)
            v.tensor_tensor(x, pO[:, 0:P], x, ALU.add).then_inc(x_done, 1)


        def act_gate(act, b, half):
            act.wait_ge(gate_ps, b + 1)
            wait(act, yT_ready, 4 * (b - 1))
            act.activation(gate[:, half * T:(half + 1) * T], pT[:, :], ACT.Silu).then_inc(gate_ready, 1)

        def pe_gate(pe, b):
            pe.wait_ge(hT_ready, b + 1)
            pe.matmul(pT[:, :], K.W[:, W_G1, :], hT[:, :], start=True, stop=True).then_inc(gate_ps, 1)

        def pe_batch(pe, b, last=False):
            for t in range(TPB):
                pe_states(pe, b, t)
                if t > 0:
                    pe_inter(pe, b, t)
                if t < 3:
                    pe_state_sum(pe, b, t)
                if not last:
                    pe_qkv(pe, b + 1, t)
                if near(b, t, -3):
                    pe_project(pe, *near(b, t, -3))
                if not last:
                    if layer == 1 and t == 1:
                        pe_gate(pe, b + 1)
                if near(b, t, -2):
                    pe_transpose_y(pe, *near(b, t, -2))
                if t < 3:
                    pe_transpose_q(pe, b, t + 1)
                if t == 3 and not last and not (isinstance(b, int) and b == B - 2):
                    pe_transpose_x(pe, b + 2)

        def act_batch(act, b, half, last=False, more=True):
            for t in range(TPB):
                if t == 0 and not last:
                    act_modulate(act, b + 1)
                if t > 0:
                    act_inter(act, b, t)
                if more:
                    act_normalise(act, b + 2, t)
                if not last:
                    act_qkv(act, b + 1, t)
                if layer == 1 and near(b, t, -1):
                    act_square(act, *near(b, t, -1))
                if t < 3:
                    act_qT(act, b, t + 1)
                if near(b, t, -2):
                    act_yT(act, *near(b, t, -2))
                if layer == 5 and t == 3 and more:
                    act_modulate(act, b + 2)
                if layer == 1:
                    if near(b, t, -1):
                        act_sd(act, *near(b, t, -1))
                    if t == 2 and not last:
                        act_gate(act, b + 1, 1 - half)

        def vec_batch(v, b, last=False):
            for t in range(TPB):
                before, out, done = near(b, t, -1), near(b, t, -3), near(b, t, -4)
                vec_products(v, b, t)
                if before:
                    vec_sum(v, *before)
                if layer == 0:
                    if t < 3:
                        vec_state(v, b, t)
                    if before:
                        vec_den(v, 4 * before[0] + before[1], before[1])
                if not last:
                    vec_qk(v, b + 1, t)
                if before:
                    if layer == 1:
                        vec_var(v, 4 * before[0] + before[1])
                    else:
                        vec_rec(v, 4 * before[0] + before[1])
                if layer == 1 and t < 3:
                    vec_state(v, b, t)
                if out:
                    vec_residual(v, *out)
                if before:
                    if layer == 1:
                        vec_rec(v, 4 * before[0] + before[1])
                    vec_y(v, 4 * before[0] + before[1], before[1])
                if layer == 0 and done:
                    tile_stats(v, K, K.X, 4 * done[0] + done[1], bn_done)

        def pool_batch(pool, b, half, last=False):
            for t in range(TPB):
                if not (last and t == 3):
                    pool_kv(pool, 4 * b + t + 1, (t + 1) % 4)
                if layer == 1:
                    if near(b, t, -3):
                        pool_gate(pool, *near(b, t, -3), half if t == 3 else 1 - half)
                    if near(b, t, 3):
                        pool_rope(pool, *near(b, t, 3))
                pool_halve(pool, b, t)

        with nc.Block() as block:
            @block.tensor
            def _(pe):
                pe_transpose_x(pe, 0)
                for t in range(TPB):
                    pe_qkv(pe, 0, t, start=True)
                if layer == 1:
                    pe_gate(pe, 0)
                pe_transpose_x(pe, 1)
                pe.wait_ge(v_ready, 4)
                pe.wait_ge(qk_free, 4)
                pe_batch(pe, 0)
                with pe.Fori(1, B - 2) as b:
                    pe_batch(pe, b)
                pe_batch(pe, B - 2)
                pe_batch(pe, B - 1, last=True)
                pe_project(pe, B - 1, 1)
                pe_transpose_y(pe, B - 1, 2)
                pe_project(pe, B - 1, 2)
                pe_transpose_y(pe, B - 1, 3)
                pe_project(pe, B - 1, 3)

            @block.scalar
            def _(act):
                finish_stats_scalar(act, K, var_ready, std_ready, rstd_ready)
                act.wait_ge(ones_set, 1)
                for t in range(TPB):
                    act_normalise(act, 0, t)
                act_modulate(act, 0)
                for t in range(TPB):
                    act_qkv(act, 0, t, start=True)
                for t in range(TPB):
                    act_normalise(act, 1, t)
                if layer == 1:
                    act_gate(act, 0, 0)
                act_batch(act, 0, 0)
                with act.Fori(0, B // 2 - 2) as i:
                    act_batch(act, 2 * i + 1, 1)
                    act_batch(act, 2 * i + 2, 0)
                act_batch(act, B - 3, 1)
                act_batch(act, B - 2, 0, more=False)
                act_batch(act, B - 1, 1, last=True, more=False)
                if layer == 1:
                    act_square(act, B - 1, 3)
                act_yT(act, B - 1, 2)
                if layer == 1:
                    act_sd(act, B - 1, 3)
                act_yT(act, B - 1, 3)

            @block.vector
            def _(v):
                v.memset(vv[:, :, :, :], 1.0).then_inc(ones_set, 1)
                finish_stats_vector(v, K, var_ready, std_ready, rstd_ready)
                for t in range(TPB):
                    vec_qk(v, 0, t, start=True)
                vec_batch(v, 0)
                with v.Fori(1, B - 1) as b:
                    vec_batch(v, b)
                vec_batch(v, B - 1, last=True)
                vec_sum(v, B - 1, 3)
                if layer == 0:
                    vec_den(v, NT - 1, 3)
                else:
                    vec_var(v, NT - 1)
                vec_rec(v, NT - 1)
                vec_y(v, NT - 1, 3)
                for t in (1, 2, 3):
                    vec_residual(v, B - 1, t)
                v.wait_ge(x_done, NT)
                if layer == 0:
                    for n in range(NT - 4, NT):
                        tile_stats(v, K, K.X, n, bn_done)

            @block.gpsimd
            def _(pool):
                if layer == 1:
                    for t in range(3):
                        pool_rope(pool, 0, t)
                pool_kv(pool, 0, 0)
                pool_batch(pool, 0, 0)
                with pool.Fori(0, B // 2 - 1) as i:
                    pool_batch(pool, 2 * i + 1, 1)
                    pool_batch(pool, 2 * i + 2, 0)
                pool_batch(pool, B - 1, 1, last=True)
                if layer == 1:
                    for t in (1, 2, 3):
                        pool_gate(pool, B - 1, t, 1)

            @block.sync
            def _(sp):
                if layer == 0:
                    row = lambda v: v.rearrange("(a n) -> a n", a=1)
                    sp.dma_start(K.rope_c[:, :, :], A["k_rope_c"].rearrange("(t p) n -> p t n", p=P)).then_inc(tab_in, 16)
                    sp.dma_start(K.rope_s[:, :, :], A["k_rope_s"].rearrange("(t p) n -> p t n", p=P)).then_inc(tab_in, 16)
                    sp.dma_start(K.smask[:, :], A["k_smask"]).then_inc(tab_in, 16)
                    for i, v in enumerate(("g1", "be1", "g2", "be2")):
                        sp.dma_start(K.rows[:, i, :], row(A["L1_ffn_" + v]).to_broadcast([P, P])).then_inc(tab_in, 16)
                    sp.dma_start(K.w1[:, :, 0:DF], A["L1_ffn_W1"].rearrange("e d f -> d e f")).then_inc(tab_in, 16)
                    sp.dma_start(K.w2[:, :, :, :], A["L1_ffn_W2"].rearrange("e (c p) f -> p e c f", p=P)).then_inc(tab_in, 16)
                    sp.wait_ge(tab_in, 9 * 16)
                if layer == 1:
                    with sp.Fori(0, B) as b:
                        sp.wait_ge(x_done, 4 * b + 4)
                        sp.dma_start(A["xs"].rearrange("(b t p) f -> b p t f", p=P, t=TPB)[ds(b, 1), :, :, :]
                                     .rearrange("o p t f -> (o p) t f"), K.X[:, ds(4 * b, 4), :]).then_inc(x_out, 16)
                    sp.wait_ge(x_out, 16 * B)


def token_shift_ffn(nc, A, K):
    with ExitStack() as ctx:
        sb = lambda n, s, d=F32: ctx.enter_context(nc.sbuf_tensor(f"f_{n}", s, d))
        sem = lambda n: ctx.enter_context(nc.semaphore(f"f_{n}"))
        pb = lambda n: [ctx.enter_context(nc.psum_tensor(f"f_{n}{i}", [P, 512], F32)) for i in range(2)]
        pT, pK, pR, pV = pb("pT"), pb("pK"), pb("pR"), pb("pV")
        xn = sb("xn", [P, TPB, P])
        h = sb("h", [P, 2, T + 1])
        d, xr, xk, kr, ka, sg, vm = (sb(n, [P, 2, T]) for n in ("d", "xr", "xk", "kr", "ka", "sg", "vm"))
        var_ready, std_ready, rstd_ready = sem("var"), sem("std"), sem("rstd")
        xn_ready, xn_T, h_ready, col_zero = sem("xn_ready"), sem("xn_T"), sem("h_ready"), sem("col_zero")
        d_ready, xr_ready, xk_ready = sem("d_ready"), sem("xr_ready"), sem("xk_ready")
        k_ps, r_ps, v_ps = sem("k_ps"), sem("r_ps"), sem("v_ps")
        kr_ready, ka_ready, sg_ready, vm_ready = sem("kr_ready"), sem("ka_ready"), sem("sg_ready"), sem("vm_ready")
        x_done, bn_done = sem("x_done"), sem("bn_done")

        def act_normalise(act, b):
            for t in range(TPB):
                wait(act, xn_T, 4 * b - 3 + t)
                act.activation(xn[:, t, :], K.X[:, ds(4 * b + t, 1), :].rearrange("p a f -> p (a f)"), ACT.Identity,
                               bias=K.nmr[:, ds(4 * b + t, 1)], scale=K.rstd[:, ds(4 * b + t, 1)]).then_inc(xn_ready, 1)

        def act_h(act, b, p):
            act.wait_ge(xn_T, 4 * b + 4)
            wait(act, xr_ready, b - 1)
            act.activation(h[:, p, 1:T + 1], pT[p][:, :], ACT.Identity, bias=K.mod[:, SB0, ds(b, 1)],
                           scale=K.mod[:, CB0, ds(b, 1)]).then_inc(h_ready, 1)

        def pe_h(pe, b, p):
            for t in range(TPB):
                pe.wait_ge(xn_ready, 4 * b + t + 1)
                if t == 0:
                    wait(pe, h_ready, b - 1)
                pe.transpose(pT[p][:, t * P:(t + 1) * P], xn[:, t, :], K.ident[:, :]).then_inc(xn_T, 1)

        def pool_diff(pool, b, p):
            pool.wait_ge(h_ready, b + 1)
            wait(pool, xr_ready, b - 1)
            pool.tensor_tensor(d[:, p, :], h[:, p, 1:T + 1], h[:, p, 0:T], ALU.subtract).then_inc(d_ready, 1)

        def vec_mix(v, b, p):
            v.wait_ge(d_ready, b + 1)
            wait(v, k_ps, b - 1)
            v.scalar_tensor_tensor(out=xk[:, p, :], in0=d[:, p, :], scalar=K.cols[:, MU_K:MU_K + 1],
                                   in1=h[:, p, 0:T], op0=ALU.mult, op1=ALU.add).then_inc(xk_ready, 1)
            wait(v, r_ps, b - 1)
            v.scalar_tensor_tensor(out=xr[:, p, :], in0=d[:, p, :], scalar=K.cols[:, MU_R:MU_R + 1],
                                   in1=h[:, p, 0:T], op0=ALU.mult, op1=ALU.add).then_inc(xr_ready, 1)

        def pe_kr(pe, b, p):
            pe.wait_ge(xk_ready, b + 1)
            wait(pe, kr_ready, b - 1)
            pe.matmul(pK[p][:, :], K.W[:, W_KT, :], xk[:, p, :], start=True, stop=True).then_inc(k_ps, 1)
            pe.wait_ge(xr_ready, b + 1)
            wait(pe, sg_ready, b - 1)
            for t in range(TPB):
                mm = pe.matmul(pR[p][:, t * P:(t + 1) * P], xr[:, p, t * P:(t + 1) * P], K.W[:, W_RT, :],
                               start=True, stop=True)
            mm.then_inc(r_ps, 1)

        def act_kr(act, b, p):
            act.wait_ge(k_ps, b + 1)
            wait(act, ka_ready, b - 1)
            act.activation(kr[:, p, :], pK[p][:, :], ACT.Relu).then_inc(kr_ready, 1)

        def act_square(act, b, p):
            act.wait_ge(kr_ready, b + 1)
            wait(act, v_ps, b - 1)
            act.activation(ka[:, p, :], kr[:, p, :], ACT.Square).then_inc(ka_ready, 1)

        def act_sigmoid(act, b, p):
            act.wait_ge(r_ps, b + 1)
            wait(act, vm_ready, b - 1)
            act.activation(sg[:, p, :], pR[p][:, :], ACT.Sigmoid).then_inc(sg_ready, 1)

        def pe_v(pe, b, p):
            pe.wait_ge(ka_ready, b + 1)
            wait(pe, vm_ready, b - 1)
            for t in range(TPB):
                mm = pe.matmul(pV[p][:, t * P:(t + 1) * P], ka[:, p, t * P:(t + 1) * P],
                               K.wgate[:, 1, ds(b, 1), :].rearrange("p a f -> p (a f)"), start=True, stop=True)
            mm.then_inc(v_ps, 1)

        def vec_gate(v, b, p):
            v.wait_ge(v_ps, b + 1)
            v.wait_ge(sg_ready, b + 1)
            wait(v, x_done, b)
            v.tensor_tensor(vm[:, p, :], pV[p][:, :], sg[:, p, :], ALU.mult).then_inc(vm_ready, 1)

        def vec_stats(v, b):
            for t in range(TPB):
                tile_stats(v, K, K.X, 4 * b + t, bn_done)

        def vec_residual(v, b, p):
            v.wait_ge(vm_ready, b + 1)
            x = K.X[:, ds(4 * b, 4), :].rearrange("p a f -> p (a f)")
            v.tensor_tensor(x, vm[:, p, :], x, ALU.add).then_inc(x_done, 1)

        def there(b):
            return not isinstance(b, int) or 0 <= b < B

        def pe_step(pe, s, p):
            if there(s - 1):
                pe_v(pe, s - 1, 1 - p)
            if there(s):
                pe_kr(pe, s, p)
            if there(s + 2):
                pe_h(pe, s + 2, p)

        def act_step(act, s, p):
            if there(s):
                act_kr(act, s, p)
                act_square(act, s, p)
                act_sigmoid(act, s, p)
            if there(s + 2):
                act_h(act, s + 2, p)
            if there(s + 3):
                act_normalise(act, s + 3)

        def vec_step(v, s, p):
            if there(s + 1):
                vec_mix(v, s + 1, 1 - p)
            if there(s - 1):
                vec_gate(v, s - 1, 1 - p)
            if there(s - 2):
                vec_stats(v, s - 2)
            if there(s - 1):
                vec_residual(v, s - 1, 1 - p)

        def pool_step(pool, s, p):
            if there(s + 1):
                pool_diff(pool, s + 1, 1 - p)

        def run(e, step):
            for s in (0, 1):
                step(e, s, s % 2)
            with e.Fori(1, B // 2 - 2) as i:
                step(e, 2 * i, 0)
                step(e, 2 * i + 1, 1)
            for s in range(B - 4, B + 1):
                step(e, s, s % 2)

        with nc.Block() as block:
            @block.tensor
            def _(pe):
                pe_h(pe, 0, 0)
                pe_h(pe, 1, 1)
                run(pe, pe_step)

            @block.scalar
            def _(act):
                finish_stats_scalar(act, K, var_ready, std_ready, rstd_ready)
                act_normalise(act, 0)
                act_h(act, 0, 0)
                act_normalise(act, 1)
                act_h(act, 1, 1)
                act_normalise(act, 2)
                run(act, act_step)

            @block.vector
            def _(v):
                v.memset(h[:, :, 0:1], 0.0).then_inc(col_zero, 1)
                finish_stats_vector(v, K, var_ready, std_ready, rstd_ready)
                vec_mix(v, 0, 0)
                run(v, vec_step)
                v.wait_ge(x_done, B)
                vec_stats(v, B - 1)

            @block.gpsimd
            def _(pool):
                pool.wait_ge(col_zero, 1)
                pool_diff(pool, 0, 0)
                run(pool, pool_step)


def attend_batches(nc, A, K):
    G = NT // 4
    with ExitStack() as ctx:
        sb = lambda n, s, d=F32: ctx.enter_context(nc.sbuf_tensor(f"m_{n}", s, d))
        sem = lambda n: ctx.enter_context(nc.semaphore(f"m_{n}"))
        pb = lambda n: ctx.enter_context(nc.psum_tensor(f"m_{n}", [P, 512], F32))
        pT, pq, pk, pv, pS, pO, pU = pb("pT"), pb("pq"), pb("pk"), pb("pv"), pb("pS"), pb("pO"), pb("pU")
        xn, h1, h = (sb(n, [P, 4, P]) for n in ("xn", "h1", "h"))
        hT, qT = sb("hT", [P, 4 * P]), sb("qT", [P, 4 * P])
        kx = sb("kx", [P, 16, FH, 32])
        v_ = sb("v", [P, 2, 4, P])
        sm, s2, ex, pn = (sb(n, [P, 16, 32]) for n in ("sm", "s2", "ex", "pn"))
        mx, sm_sum, rc = sb("mx", [P, 16]), sb("sum", [P, 16]), sb("rc", [P, 16])
        ax = sb("ax", [P, 16, 4, 32])
        oT = sb("oT", [P, 4 * P])
        x_in = [sem(f"x_in{g}") for g in range(4)]
        stats, var_ready, std_ready, rstd_ready = sem("stats"), sem("var"), sem("std"), sem("rstd")
        xn_ready, h1_ready, h_ready, h3_ready = sem("xn_ready"), sem("h1_ready"), sem("h_ready"), sem("h3_ready")
        h_T, hT_ready, q_ps, k_ps, v_ps = sem("h_T"), sem("hT_ready"), sem("q_ps"), sem("k_ps"), sem("v_ps")
        q_ready, kx_act, kx_vec, v_ready, zeroed = (sem("q_ready"), sem("kx_act"), sem("kx_vec"), sem("v_ready"),
                                                    sem("zeroed"))
        s_ps, sm_ready, mx_ready, s2_ready, ex_ready = (sem("s_ps"), sem("sm_ready"), sem("mx_ready"),
                                                        sem("s2_ready"), sem("ex_ready"))
        sum_ready, rc_ready, pn_ready, ax_ready = sem("sum_ready"), sem("rc_ready"), sem("pn_ready"), sem("ax_ready")
        o_ps, oT_ready, w_ps, u_ready, bn_done = sem("o_ps"), sem("oT_ready"), sem("w_ps"), sem("u_ready"), sem("bn_done")

        flat = lambda t: t[:, :, :].rearrange("p a b -> p (a b)")
        over = lambda row: row.unsqueeze(1).to_broadcast([P, 4, P])

        def act_xn(act, g):
            wait(act, h1_ready, g)
            for t in range(4):
                act.activation(xn[:, t, :], K.X[:, ds(4 * g + t, 1), :].rearrange("p a f -> p (a f)"), ACT.Identity,
                               bias=K.nmr[:, ds(4 * g + t, 1)], scale=K.rstd[:, ds(4 * g + t, 1)]).then_inc(xn_ready, 1)

        def pool_h(pool, g):
            pool.wait_ge(xn_ready, 4 * g + 4)
            wait(pool, h_ready, g)
            pool.tensor_tensor(h1[:, :, :], xn[:, :, :], over(K.tab[:, 1, :]), ALU.mult).then_inc(h1_ready, 1)
            pool.wait_ge(h1_ready, g + 1)
            wait(pool, h_T, g)
            wait(pool, h3_ready, g)
            pool.tensor_tensor(h[:, :, :], h1[:, :, :], over(K.tab[:, 0, :]), ALU.add).then_inc(h_ready, 1)

        def pool_h3(pool, g):
            pool.wait_ge(h_ready, g + 1)
            pool.tensor_tensor(K.U[:, ds(4 * g, 4), :], h[:, :, :], over(K.bo[:, :]), ALU.add).then_inc(h3_ready, 1)

        def pool_shift(pool, g):
            pool.wait_ge(mx_ready, g + 1)
            wait(pool, ex_ready, g)
            pool.tensor_tensor(s2[:, :, :], sm[:, :, :], mx[:, :].unsqueeze(2).to_broadcast([P, 16, 32]),
                               ALU.subtract).then_inc(s2_ready, 1)

        def pe_T(pe, g):
            pe.wait_ge(h_ready, g + 1)
            wait(pe, hT_ready, g)
            for t in range(4):
                mm = pe.transpose(pT[:, t * P:(t + 1) * P], h[:, t, :], K.ident[:, :])
            mm.then_inc(h_T, 1)

        def act_hT(act, g):
            act.wait_ge(h_T, g + 1)
            wait(act, v_ps, g)
            act.activation(hT[:, :], pT[:, :], ACT.Copy).then_inc(hT_ready, 1)

        def pe_qk(pe, g):
            pe.wait_ge(hT_ready, g + 1)
            wait(pe, q_ready, g)
            pe.matmul(pq[:, :], K.W[:, W_FQ, :], hT[:, :], start=True, stop=True).then_inc(q_ps, 1)
            wait(pe, kx_act, 2 * g)
            wait(pe, kx_vec, 2 * g)
            pe.matmul(pk[:, :], K.W[:, W_FK, :], hT[:, :], start=True, stop=True).then_inc(k_ps, 1)

        def pe_v(pe, g):
            wait(pe, v_ready, g)
            for t in range(4):
                mm = pe.matmul(pv[:, t * P:(t + 1) * P], hT[:, t * P:(t + 1) * P], K.W[:, W_FV, :],
                               start=True, stop=True)
            mm.then_inc(v_ps, 1)

        def act_q(act, g):
            act.wait_ge(q_ps, g + 1)
            wait(act, s_ps, g)
            act.activation(qT[:, :], pq[:, :], ACT.Identity, bias=K.cols[:, BQ:BQ + 1]).then_inc(q_ready, 1)

        def kx_view(hd):
            rows = slice(32 * hd, 32 * hd + 32)
            return rows, kx[rows, :, hd, :], pk[rows, :].rearrange("p (c s) -> p c s", c=16)

        def act_k(act, g):
            act.wait_ge(k_ps, g + 1)
            for hd in range(2):
                rows, o, i = kx_view(hd)
                act.activation(o, i, ACT.Identity, bias=K.cols[rows, BK:BK + 1]).then_inc(kx_act, 1)

        def vec_k(v, g):
            v.wait_ge(k_ps, g + 1)
            wait(v, s_ps, g)
            for hd in range(2, FH):
                rows, o, i = kx_view(hd)
                v.tensor_scalar(o, i, K.cols[rows, BK:BK + 1], None, ALU.add).then_inc(kx_vec, 1)

        def act_v(act, g, p):
            act.wait_ge(v_ps, g + 1)
            wait(act, o_ps, g - 1)
            act.activation(flat(v_[:, p, :, :]), pv[:, :], ACT.Copy).then_inc(v_ready, 1)

        def pe_scores(pe, g):
            pe.wait_ge(q_ready, g + 1)
            pe.wait_ge(kx_act, 2 * g + 2)
            pe.wait_ge(kx_vec, 2 * g + 2)
            wait(pe, sm_ready, g)
            for t in range(4):
                for c in range(4):
                    mm = pe.matmul(pS[32 * c:32 * c + 32, t * P:(t + 1) * P], qT[:, t * P + 32 * c:t * P + 32 * c + 32],
                                   kx[:, 4 * t + c, :, :].rearrange("p h s -> p (h s)"), start=True, stop=True,
                                   skip_group_check=True)
            mm.then_inc(s_ps, 1)

        def vec_scores(v, g):
            v.wait_ge(s_ps, g + 1)
            wait(v, s2_ready, g)
            v.scalar_tensor_tensor(out=sm[:, :, :], in0=pS[:, :].rearrange("p (a s) -> p a s", s=32),
                                   scalar=float(FD) ** -0.5, in1=K.smask[:, :].unsqueeze(1).to_broadcast([P, 16, 32]),
                                   op0=ALU.mult, op1=ALU.add).then_inc(sm_ready, 1)

        def vec_max(v, g):
            v.wait_ge(sm_ready, g + 1)
            v.tensor_reduce(mx[:, :], sm[:, :, :], AX.X, ALU.max).then_inc(mx_ready, 1)

        def act_exp(act, g):
            act.wait_ge(s2_ready, g + 1)
            wait(act, pn_ready, g)
            act.activation(flat(ex), flat(s2), ACT.Exp).then_inc(ex_ready, 1)

        def vec_total(v, g):
            v.wait_ge(ex_ready, g + 1)
            wait(v, rc_ready, g)
            v.tensor_reduce(sm_sum[:, :], ex[:, :, :], AX.X, ALU.add).then_inc(sum_ready, 1)

        def vec_reciprocal(v, g):
            v.wait_ge(sum_ready, g + 1)
            wait(v, pn_ready, g)
            v.reciprocal(rc[:, :], sm_sum[:, :]).then_inc(rc_ready, 1)

        def vec_probs(v, g):
            v.wait_ge(rc_ready, g + 1)
            wait(v, ax_ready, 4 * g)
            v.tensor_tensor(pn[:, :, :], ex[:, :, :], rc[:, :].unsqueeze(2).to_broadcast([P, 16, 32]),
                            ALU.mult).then_inc(pn_ready, 1)

        def vec_transpose(v, g):
            v.wait_ge(pn_ready, g + 1)
            wait(v, o_ps, g)
            for c in range(4):
                rows = slice(32 * c, 32 * c + 32)
                v.transpose(ax[rows, :, c, :], pn[rows, :, :]).then_inc(ax_ready, 1)

        def pe_values(pe, g, p):
            pe.wait_ge(ax_ready, 4 * g + 4)
            pe.wait_ge(v_ready, g + 1)
            wait(pe, oT_ready, g)
            for t in range(4):
                for hd in range(FH):
                    mm = pe.matmul(pO[32 * hd:32 * hd + 32, t * P:(t + 1) * P], v_[:, p, t, 32 * hd:32 * hd + 32],
                                   ax[:, 4 * t + hd, :, :].rearrange("p c s -> p (c s)"), start=True, stop=True,
                                   skip_group_check=True)
            mm.then_inc(o_ps, 1)

        def act_o(act, g):
            act.wait_ge(o_ps, g + 1)
            wait(act, w_ps, g)
            act.activation(oT[:, :], pO[:, :], ACT.Copy).then_inc(oT_ready, 1)

        def pe_out(pe, g):
            pe.wait_ge(oT_ready, g + 1)
            wait(pe, u_ready, g)
            for t in range(4):
                mm = pe.matmul(pU[:, t * P:(t + 1) * P], oT[:, t * P:(t + 1) * P], K.W[:, W_FO, :],
                               start=True, stop=True)
            mm.then_inc(w_ps, 1)

        def vec_u(v, g):
            v.wait_ge(w_ps, g + 1)
            v.wait_ge(h3_ready, g + 1)
            wait(v, u_ready, g)
            u = K.U[:, ds(4 * g, 4), :].rearrange("p a f -> p (a f)")
            v.tensor_tensor(u, pU[:, :], u, ALU.add).then_inc(u_ready, 1)

        def vec_stats(v, g):
            for t in range(4):
                tile_stats(v, K, K.U, 4 * g + t, bn_done)

        def there(g):
            return not isinstance(g, int) or 0 <= g < G

        def pe_step(pe, s, p):
            if there(s):
                pe_scores(pe, s)
            if there(s + 1):
                pe_T(pe, s + 1)
            if there(s - 2):
                pe_out(pe, s - 2)
            if there(s + 1):
                pe_qk(pe, s + 1)
                pe_v(pe, s + 1)
            if there(s - 1):
                pe_values(pe, s - 1, 1 - p)

        def act_step(act, s, p):
            if there(s - 2):
                act_o(act, s - 2)
            if there(s):
                act_v(act, s, p)
            if there(s + 1):
                act_hT(act, s + 1)
            if there(s + 2):
                act_xn(act, s + 2)
            if there(s + 1):
                act_q(act, s + 1)
            if there(s + 1):
                act_k(act, s + 1)
            if there(s):
                act_exp(act, s)

        def vec_step(v, s, p):
            if there(s - 1):
                vec_total(v, s - 1)
            if there(s):
                vec_scores(v, s)
            if there(s - 1):
                vec_reciprocal(v, s - 1)
            if there(s):
                vec_max(v, s)
            if there(s - 1):
                vec_probs(v, s - 1)
                vec_transpose(v, s - 1)
            if there(s + 1):
                vec_k(v, s + 1)
            if there(s - 2):
                vec_u(v, s - 2)
            if there(s - 3):
                vec_stats(v, s - 3)

        def pool_step(pool, s, p):
            if there(s + 2):
                pool_h(pool, s + 2)
            if there(s):
                pool_shift(pool, s)
            if there(s + 2):
                pool_h3(pool, s + 2)

        def run(e, step, before={}):
            for s in range(-2, 4):
                if s in before:
                    before[s]()
                step(e, s, s % 2)
            with e.Fori(2, G // 2 - 1) as i:
                step(e, 2 * i, 0)
                step(e, 2 * i + 1, 1)
            for s in range(G - 2, G + 2):
                step(e, s, s % 2)

        with nc.Block() as block:
            @block.sync
            def _(sp):
                xs = A["xs"].rearrange("(b n t) f -> t b n f", n=NT, t=8)
                for g in range(4):
                    for t in range(8):
                        sp.dma_start(K.X[16 * t:16 * t + 16, 16 * g:16 * g + 16, :], xs[t][:, 16 * g:16 * g + 16, :])\
                          .then_inc(x_in[g], 16)

            @block.tensor
            def _(pe):
                pe.wait_ge(zeroed, 2)
                run(pe, pe_step)

            @block.scalar
            def _(act):
                stats_scalar = lambda q: finish_stats_scalar(act, K, var_ready, std_ready, rstd_ready, q, 4)
                act.wait_ge(zeroed, 2)
                stats_scalar(0)
                run(act, act_step, before={0: lambda: stats_scalar(1), 1: lambda: [stats_scalar(2), stats_scalar(3)]})

            @block.vector
            def _(v):
                def quarter(q):
                    v.wait_ge(x_in[q], 8 * 16)
                    for n in range(16 * q, 16 * q + 16):
                        tile_stats(v, K, K.X, n, stats)
                    v.wait_ge(stats, 16 * q + 16)
                    finish_stats_vector(v, K, var_ready, std_ready, rstd_ready, q, 4)
                quarter(0)
                v.wait_ge(zeroed, 2)
                run(v, vec_step, before={0: lambda: quarter(1), 1: lambda: [quarter(2), quarter(3)]})
                v.wait_ge(u_ready, G)
                vec_stats(v, G - 1)

            @block.gpsimd
            def _(pool):
                pool.memset(kx[:, :, :, :], 0.0).then_inc(zeroed, 1)
                pool.memset(ax[:, :, :, :], 0.0).then_inc(zeroed, 1)
                run(pool, pool_step)


def route(nc, A, K, row, row_z, expert):
    G = NT // 4
    with ExitStack() as ctx:
        sb = lambda n, s, d=F32: ctx.enter_context(nc.sbuf_tensor(f"r_{n}", s, d))
        sem = lambda n: ctx.enter_context(nc.semaphore(f"r_{n}"))
        pb = lambda n: ctx.enter_context(nc.psum_tensor(f"r_{n}", [P, 512], F32))
        pT, pL, pR, pC = [pb("pT0"), pb("pT1")], [pb("pL0"), pb("pL1")], pb("pR"), pb("pC")
        yn, y1, yb = (sb(n, [P, 2, 4, P]) for n in ("yn", "y1", "yb"))
        yT = sb("yT", [P, 2, 4 * P])
        logits = sb("logits", [P, NT, E])
        ustrict, tie, iota, ones = sb("ustrict", [P, P]), sb("tie", [P, E]), sb("iota", [P, P]), sb("ones", [P, P])
        best, first = sb("best", [P, NT]), sb("first", [P, NT])
        hot, work = sb("hot", [P, NT, E]), sb("work", [P, NT, E])
        total, upto = sb("total", [P, E, NT]), sb("upto", [P, E, NT])
        tiles, ends, base = sb("tiles", [P, E]), sb("ends", [P, E]), sb("base", [P, E])
        after = sb("after", [P, SLOTS, E])
        posf, expf = sb("posf", [P, NT]), sb("expf", [P, SLOTS])
        place, place_a, place_b = (sb(n, [P, NT], I32) for n in ("place", "place_a", "place_b"))
        a_of, b_of, ids = sb("a_of", [P, NT]), sb("b_of", [P, NT]), sb("ids", [P, NT])
        at_a, at_b = sb("at_a", [P, NT, SLOTS]), sb("at_b", [P, 2, 8, P])
        zero_row, rowf, spare = sb("zero_row", [1, P]), sb("rowf", [P, SLOTS]), sb("spare", [P, SLOTS])
        gb, gate_done, xb_done = sb("gb", [P, P]), sem("gate_done"), sem("xb_done")
        ab_ready, at_a_done, at_b_done, row_ps, ab_ints, zero_set, y_out = (
            sem(n) for n in ("ab_ready", "at_a_done", "at_b_done", "row_ps", "ab_ints", "zero_set", "y_out"))
        var_ready, std_ready, rstd_ready = sem("var"), sem("std"), sem("rstd")
        tab_in, yn_ready, y1_ready, yb_ready, y_ready = (sem("tab_in"), sem("yn_ready"), sem("y1_ready"),
                                                         sem("yb_ready"), sem("y_ready"))
        y_T, yT_ready, l_ps, l_ready, chain, hot_ready, c_ps = (sem("y_T"), sem("yT_ready"), sem("l_ps"), sem("l_ready"),
                                                                sem("chain"), sem("hot_ready"), sem("c_ps"))
        over = lambda row: row.unsqueeze(1).to_broadcast([P, 4, P])

        def act_normalise(act, g, s):
            wait(act, y1_ready, g - 1)
            for t in range(4):
                act.activation(yn[:, s, t, :], K.U[:, ds(4 * g + t, 1), :].rearrange("p a f -> p (a f)"), ACT.Identity,
                               bias=K.nmr[:, ds(4 * g + t, 1)], scale=K.rstd[:, ds(4 * g + t, 1)]).then_inc(yn_ready, 1)

        def act_yT(act, g, s):
            act.wait_ge(y_T, g + 1)
            wait(act, l_ps, g - 1)
            act.activation(yT[:, s, :], pT[s][:, :], ACT.Copy).then_inc(yT_ready, 1)

        def pe_T(pe, g, s):
            pe.wait_ge(yb_ready, g + 1)
            wait(pe, yT_ready, g - 1)
            for t in range(4):
                mm = pe.transpose(pT[s][:, t * P:(t + 1) * P], yb[:, s, t, :], K.ident[:, :])
            mm.then_inc(y_T, 1)

        def pe_logits(pe, g, s):
            pe.wait_ge(yT_ready, g + 1)
            wait(pe, l_ready, g - 1)
            for t in range(4):
                mm = pe.matmul(pL[s][:, t * E:(t + 1) * E], yT[:, s, t * P:(t + 1) * P], K.wg8[:, :],
                               start=True, stop=True)
            mm.then_inc(l_ps, 1)

        def vec_y(v, g, s):
            v.wait_ge(yn_ready, 4 * g + 4)
            wait(v, yb_ready, g - 1)
            wait(v, y_ready, g - 1)
            v.tensor_tensor(y1[:, s, :, :], yn[:, s, :, :], over(K.rows[:, 0, :]), ALU.mult).then_inc(y1_ready, 1)
            v.wait_ge(y1_ready, g + 1)
            wait(v, y_T, g - 1)
            v.tensor_tensor(yb[:, s, :, :], y1[:, s, :, :], over(K.rows[:, 1, :]), ALU.add).then_inc(yb_ready, 1)

        def vec_logits(v, g, s):
            v.wait_ge(l_ps, g + 1)
            v.tensor_copy(logits[:, ds(4 * g, 4), :], pL[s][:, 0:4 * E].rearrange("p (a e) -> p a e", e=E))\
             .then_inc(l_ready, 1)

        def pool_y(pool, g, s):
            pool.wait_ge(y1_ready, g + 1)
            pool.tensor_tensor(K.U[:, ds(4 * g, 4), :], y1[:, s, :, :], over(K.rows[:, 1, :]), ALU.add)\
                .then_inc(y_ready, 1)

        def there(g):
            return not isinstance(g, int) or 0 <= g < G

        def act_step(act, k, s):
            if there(k):
                act_yT(act, k, s)
            if there(k + 2):
                act_normalise(act, k + 2, s)

        def vec_step(v, k, s):
            if there(k + 1):
                vec_y(v, k + 1, 1 - s)
            if there(k - 1):
                vec_logits(v, k - 1, 1 - s)

        def pe_step(pe, k, s):
            if there(k):
                pe_T(pe, k, s)
            if there(k - 1):
                pe_logits(pe, k - 1, 1 - s)

        def run(e, step):
            for k in range(4):
                step(e, k, k % 2)
            with e.Fori(2, G // 2 - 1) as i:
                step(e, 2 * i, 0)
                step(e, 2 * i + 1, 1)
            for k in range(G - 2, G + 1):
                step(e, k, k % 2)

        with nc.Block() as block:
            @block.sync
            def _(sp):
                sp.dma_start(ustrict[:, :], A["k_ustrict"]).then_inc(tab_in, 16)
                sp.dma_start(tie[:, :], A["k_tie"]).then_inc(tab_in, 16)
                sp.dma_start(iota[:, :], A["k_iota"]).then_inc(tab_in, 16)
                sp.dma_start(K.w1[:, :, DF + FC:], A["L1_ffn_b2"].rearrange("(a e) f -> a e f", a=1)
                             .to_broadcast([P, E, P])).then_inc(tab_in, 16)
                sp.dma_start(ids[:, :], A["k_ids"]).then_inc(tab_in, 16)
                sp.dma_start(spare[:, :], A["k_spare"]).then_inc(tab_in, 16)
                sp.wait_ge(zero_set, 1)
                sp.dma_start(A["ys"][0:1, :], zero_row[:, :]).then_inc(y_out, 16)
                rows = A["ys"][1:1 + B * T, :].rearrange("(g n p) f -> g p n f", p=P, n=4)
                with sp.Fori(0, G) as g:
                    sp.wait_ge(y_ready, g + 1)
                    sp.dma_start(rows[ds(g, 1), :, :, :].rearrange("o p n f -> (o p) n f"), K.U[:, ds(4 * g, 4), :])\
                      .then_inc(y_out, 16)
                sp.wait_ge(y_out, 16 * (G + 1))
                sp.wait_ge(tab_in, 6 * 16)

            @block.scalar
            def _(act):
                finish_stats_scalar(act, K, var_ready, std_ready, rstd_ready)
                act_normalise(act, 0, 0)
                act_normalise(act, 1, 1)
                run(act, act_step)

            @block.tensor
            def _(pe):
                run(pe, pe_step)
                pe.wait_ge(hot_ready, 1)
                pe.wait_ge(tab_in, 6 * 16)
                h = hot[:, :, :].rearrange("p n e -> p (n e)")
                pe.matmul(pR[:, :], ustrict[:, :], h, start=True, stop=True).then_inc(c_ps, 1)
                pe.matmul(pC[:, :], ones[:, :], h, start=True, stop=True).then_inc(c_ps, 1)
                for q in range(8):
                    pe.wait_ge(at_b_done, q + 1)
                    for n in range(8 * q, 8 * q + 8):
                        pe.wait_ge(at_a_done, n + 1)
                        mm = pe.matmul(pT[0][:, 0:SLOTS], at_b[:, q % 2, n % 8, :], at_a[:, n, :],
                                       start=(n == 0), stop=(n == NT - 1))
                    mm.then_inc(row_ps, 1)

            @block.gpsimd
            def _(pool):
                pool.memset(zero_row[:, :], 0.0).then_inc(zero_set, 1)
                with pool.Fori(0, G // 2) as i:
                    for s in range(2):
                        pool_y(pool, 2 * i + s, s)
                pool.tensor_tensor(K.gw[:, :], K.rows[:, 2, :], K.tab[:, 2, :], ALU.mult).then_inc(gate_done, 1)
                pool.tensor_tensor(gb[:, :], K.rows[:, 3, :], K.tab[:, 2, :], ALU.mult).then_inc(gate_done, 1)
                pool.wait_ge(gate_done, 2)
                with pool.Fori(0, G) as g:
                    x = K.X[:, ds(4 * g, 4), :]
                    pool.tensor_tensor(x, x, over(gb[:, :]), ALU.add).then_inc(xb_done, 1)

            @block.vector
            def _(v):
                count = [0]

                def link(ins):
                    count[0] += 1
                    ins.then_inc(chain, 1)
                    v.wait_ge(chain, count[0])

                link(v.memset(ones[:, :], 1.0))
                finish_stats_vector(v, K, var_ready, std_ready, rstd_ready)
                v.wait_ge(rstd_ready, 2)
                vec_y(v, 0, 0)
                run(v, vec_step)
                v.wait_ge(l_ready, G)
                v.wait_ge(tab_in, 6 * 16)
                by_e = lambda t: t.unsqueeze(2).to_broadcast([P, NT, E])
                by_n = lambda t: t.unsqueeze(1).to_broadcast([P, NT, E])
                link(v.tensor_reduce(best[:, :], logits[:, :, :], AX.X, ALU.max))
                link(v.tensor_tensor(work[:, :, :], logits[:, :, :], by_e(best[:, :]), ALU.is_ge))
                link(v.tensor_tensor(hot[:, :, :], work[:, :, :], by_n(tie[:, :]), ALU.mult))
                link(v.tensor_reduce(first[:, :], hot[:, :, :], AX.X, ALU.max))
                link(v.tensor_tensor(work[:, :, :], by_n(tie[:, :]), by_e(first[:, :]), ALU.is_equal))
                v.tensor_copy(hot[:, :, :], work[:, :, :]).then_inc(hot_ready, 1)
                v.wait_ge(c_ps, 2)
                link(v.tensor_copy(total[:, :, :], pC[:, :].rearrange("p (n e) -> p e n", e=E)))
                for e in range(E):
                    link(v.tensor_tensor_scan(upto[:, e, :], ones[:, 0:NT], total[:, e, :], 0.0, ALU.mult, ALU.add))
                w = work[:, :, :].rearrange("p n e -> p (n e)").rearrange("p (e n) -> p e n", e=E)
                link(v.tensor_scalar(expf[:, 0:NT], iota[:, 0:NT], float(P), None, ALU.mult))
                link(v.tensor_tensor(w, upto[:, :, NT - 1:NT].to_broadcast([P, E, NT]),
                                     expf[:, 0:NT].unsqueeze(1).to_broadcast([P, E, NT]), ALU.is_gt))
                link(v.tensor_reduce(tiles[:, :], w, AX.X, ALU.add))
                link(v.tensor_tensor_scan(ends[:, :], ones[:, 0:E], tiles[:, :], 0.0, ALU.mult, ALU.add))
                link(v.tensor_tensor(base[:, :], ends[:, :], tiles[:, :], ALU.subtract))
                link(v.tensor_scalar(base[:, :], base[:, :], float(P), None, ALU.mult))
                link(v.tensor_tensor(total[:, :, :], upto[:, :, :], total[:, :, :], ALU.subtract))
                link(v.tensor_tensor(total[:, :, :], total[:, :, :], base[:, :].unsqueeze(2).to_broadcast([P, E, NT]),
                                     ALU.add))
                link(v.tensor_tensor(work[:, :, :], pR[:, :].rearrange("p (n e) -> p n e", e=E),
                                     total[:, :, :].rearrange("p e n -> p n e"), ALU.add))
                link(v.tensor_tensor(work[:, :, :], work[:, :, :], hot[:, :, :], ALU.mult))
                link(v.tensor_reduce(posf[:, :], work[:, :, :], AX.X, ALU.add))
                link(v.tensor_copy(place[:, :], posf[:, :]))
                v.tensor_scalar(place_a[:, :], place[:, :], P.bit_length() - 1, None, ALU.logical_shift_right)\
                 .then_inc(ab_ints, 1)
                v.tensor_scalar(place_b[:, :], place[:, :], P - 1, None, ALU.bitwise_and).then_inc(ab_ints, 1)
                v.wait_ge(ab_ints, 2)
                v.tensor_copy(a_of[:, :], place_a[:, :]).then_inc(ab_ready, 1)
                v.tensor_copy(b_of[:, :], place_b[:, :]).then_inc(ab_ready, 1)
                v.wait_ge(ab_ready, 2)
                for q in range(8):
                    wait(v, row_ps, q - 1)
                    v.tensor_tensor(at_b[:, q % 2, :, :], b_of[:, 8 * q:8 * q + 8].unsqueeze(2).to_broadcast([P, 8, P]),
                                    iota[:, :].unsqueeze(1).to_broadcast([P, 8, P]), ALU.is_equal).then_inc(at_b_done, 1)
                    for n in range(8 * q, 8 * q + 8):
                        v.tensor_scalar(at_a[:, n, :], iota[:, 0:SLOTS], a_of[:, n:n + 1], ids[:, n:n + 1],
                                        ALU.is_equal, ALU.mult).then_inc(at_a_done, 1)
                link(v.tensor_tensor(after[:, :, :], ends[:, :].unsqueeze(1).to_broadcast([P, SLOTS, E]),
                                     iota[:, 0:SLOTS].unsqueeze(2).to_broadcast([P, SLOTS, E]), ALU.is_le))
                link(v.tensor_reduce(expf[:, :], after[:, :, :], AX.X, ALU.add))
                link(v.tensor_scalar(expf[:, :], expf[:, :], float(E - 1), None, ALU.min))
                link(v.tensor_copy(expert[:, :], expf[:, :]))
                v.wait_ge(row_ps, 8)
                link(v.tensor_copy(rowf[:, :], pT[0][:, 0:SLOTS]))
                link(v.tensor_copy(row[:, :], rowf[:, :]))
                link(v.scalar_tensor_tensor(out=expf[:, :], in0=rowf[:, :], scalar=0.0, in1=spare[:, :],
                                            op0=ALU.is_equal, op1=ALU.mult))
                link(v.tensor_tensor(rowf[:, :], rowf[:, :], expf[:, :], ALU.add))
                link(v.tensor_copy(row_z[:, :], rowf[:, :]))


def experts(nc, A, K, out):
    with ExitStack() as ctx:
        sb = lambda n, s, d=F32: ctx.enter_context(nc.sbuf_tensor(f"e_{n}", s, d))
        row, row_z, expert = sb("row", [P, SLOTS], U32), sb("row_z", [P, SLOTS], U32), sb("expert", [P, SLOTS], I32)
        K.gw = sb("gw", [P, P])
        route(nc, A, K, row, row_z, expert)
        run_experts(nc, A, K, row, row_z, expert)
        finish(nc, A, K, out)


def run_experts(nc, A, K, row, row_z, expert):
    with ExitStack() as ctx:
        sb = lambda n, s, d=F32: ctx.enter_context(nc.sbuf_tensor(f"x_{n}", s, d))
        sem = lambda n: ctx.enter_context(nc.semaphore(f"x_{n}"))
        pb = lambda n: ctx.enter_context(nc.psum_tensor(f"x_{n}", [P, 512], F32))
        pT, pA, pB, pZ = ([pb(f"{n}{i}") for i in range(2)] for n in ("pT", "pA", "pB", "pZ"))
        yl, z = sb("yl", [P, 4, P]), sb("z", [P, 4, P])
        yT, w1, hT = sb("yT", [P, 2, P]), sb("w1", [P, 4, DF + FC + P]), sb("hT", [P, 2, DF])
        b1_raw = sb("b1_raw", [E * FC, P])
        b1_in, b1_T, b1_ready = sem("b1_in"), sem("b1_T"), sem("b1_ready")
        y_in, z_out = [sem(f"y_in{s}") for s in range(4)], [sem(f"z_out{s}") for s in range(4)]
        y_T, yT_ready, w1_ready, h_ps, h_act, h_vec, z_ps, z_ready = (
            sem(n) for n in ("y_T", "yT_ready", "w1_ready", "h_ps", "h_act", "h_vec", "z_ps", "z_ready"))
        rounds = SLOTS // 4
        half = FC // 2 * P

        def load_expert(e, j):
            return e.value_load(expert[0:1, ds(j, 1)], min_val=0, max_val=E - 1)

        def pe_T(pe, i, s):
            j = 4 * i + s
            pe.wait_ge(y_in[s], 16 * i + 16)
            wait(pe, yT_ready, j - 1)
            pe.transpose(pT[s % 2][:, 0:P], yl[:, s, :], K.ident[:, :]).then_inc(y_T, 1)

        def act_yT(act, i, s):
            j = 4 * i + s
            act.wait_ge(y_T, j + 1)
            wait(act, h_ps, j - 1)
            act.activation(yT[:, s % 2, :], pT[s % 2][:, 0:P], ACT.Copy).then_inc(yT_ready, 1)

        def vec_w1(v, i, s):
            j = 4 * i + s
            e = load_expert(v, j)
            wait(v, z_ready, j - 3)
            v.tensor_copy(w1[:, s, :], K.w1[:, ds(e, 1), :].rearrange("p a f -> p (a f)")).then_inc(w1_ready, 1)

        def pe_h(pe, i, s):
            j = 4 * i + s
            pe.wait_ge(yT_ready, j + 1)
            pe.wait_ge(w1_ready, j + 1)
            wait(pe, h_act, j - 1)
            wait(pe, h_vec, j - 1)
            for c in range(FC):
                o = (pA, pB)[c // 2][s % 2][:, (c % 2) * P:(c % 2 + 1) * P]
                mm = pe.matmul(o, w1[:, s, c * P:(c + 1) * P], yT[:, s % 2, :], start=True, stop=True)
            mm.then_inc(h_ps, 1)

        def act_h(act, i, s):
            j = 4 * i + s
            act.wait_ge(h_ps, j + 1)
            wait(act, z_ps, j - 1)
            for c in range(2):
                a = act.activation(hT[:, s % 2, c * P:(c + 1) * P], pA[s % 2][:, c * P:(c + 1) * P], ACT.Relu,
                                   bias=w1[:, s, DF + c:DF + c + 1])
            a.then_inc(h_act, 1)

        def vec_h(v, i, s):
            j = 4 * i + s
            v.wait_ge(h_ps, j + 1)
            wait(v, z_ps, j - 1)
            for c in range(2):
                a = v.tensor_scalar(hT[:, s % 2, half + c * P:half + (c + 1) * P], pB[s % 2][:, c * P:(c + 1) * P],
                                    w1[:, s, DF + 2 + c:DF + 3 + c], 0.0, ALU.add, ALU.max)
            a.then_inc(h_vec, 1)

        def pe_z(pe, i, s, e):
            j = 4 * i + s
            pe.wait_ge(h_act, j + 1)
            pe.wait_ge(h_vec, j + 1)
            wait(pe, z_ready, j - 1)
            for c in range(FC):
                mm = pe.matmul(pZ[s % 2][:, 0:P], hT[:, s % 2, c * P:(c + 1) * P],
                               K.w2[:, ds(e, 1), c, :].rearrange("p a f -> p (a f)"), start=(c == 0), stop=(c == FC - 1))
            mm.then_inc(z_ps, 1)

        def vec_z(v, i, s):
            j = 4 * i + s
            v.wait_ge(z_ps, j + 1)
            wait(v, z_out[s], 16 * i)
            v.tensor_tensor(z[:, s, :], pZ[s % 2][:, 0:P], w1[:, s, DF + FC:], ALU.add).then_inc(z_ready, 1)

        def ahead(i, s, d):
            if isinstance(i, int) and 4 * i + s + d >= SLOTS:
                return None
            return i + (s + d) // 4, (s + d) % 4

        def pe_step(pe, i, s):
            e = load_expert(pe, 4 * i + s)
            if ahead(i, s, 2):
                pe_T(pe, *ahead(i, s, 2))
            if ahead(i, s, 1):
                pe_h(pe, *ahead(i, s, 1))
            pe_z(pe, i, s, e)

        def act_step(act, i, s):
            if ahead(i, s, 2):
                act_yT(act, *ahead(i, s, 2))
            if ahead(i, s, 1):
                act_h(act, *ahead(i, s, 1))

        def vec_step(v, i, s):
            if ahead(i, s, 2):
                vec_w1(v, *ahead(i, s, 2))
            if ahead(i, s, 1):
                vec_h(v, *ahead(i, s, 1))
            vec_z(v, i, s)

        def run(e, step):
            for s in range(4):
                step(e, 0, s)
            with e.Fori(1, rounds - 1) as i:
                for s in range(4):
                    step(e, i, s)
            for s in range(4):
                step(e, rounds - 1, s)

        with nc.Block() as block:
            @block.sync
            def _(sp):
                sp.dma_start(b1_raw[:, :], A["L1_ffn_b1"].rearrange("e (c p) -> (e c) p", p=P)).then_inc(b1_in, 16)
                sp.wait_ge(b1_in, 16)

            @block.gpsimd
            def _(pool):
                def gather(j):
                    wait(pool, y_T, j - 3)
                    pool.indirect_dma_start(out=yl[:, j % 4, :], out_offset=None, in_=A["ys"],
                                            in_offset=bass.IndirectOffsetOnAxis(ap=row[:, j:j + 1], axis=0))\
                        .then_inc(y_in[j % 4], 16)

                def scatter(j):
                    pool.wait_ge(z_ready, j + 1)
                    pool.indirect_dma_start(out=A["zs"], out_offset=bass.IndirectOffsetOnAxis(ap=row_z[:, j:j + 1], axis=0),
                                            in_=z[:, j % 4, :], in_offset=None).then_inc(z_out[j % 4], 16)
                for j in range(6):
                    gather(j)
                for j in range(SLOTS):
                    scatter(j)
                    if j + 6 < SLOTS:
                        gather(j + 6)
                for s in range(4):
                    pool.wait_ge(z_out[s], 16 * rounds)

            @block.tensor
            def _(pe):
                pe.wait_ge(b1_in, 16)
                pe.transpose(pZ[0][:, 0:E * FC], b1_raw[:, :], K.ident[0:E * FC, 0:E * FC]).then_inc(b1_T, 1)
                pe_T(pe, 0, 0)
                pe_T(pe, 0, 1)
                pe_h(pe, 0, 0)
                pe.wait_ge(b1_ready, 1)
                run(pe, pe_step)

            @block.scalar
            def _(act):
                act.wait_ge(b1_T, 1)
                act.activation(K.w1[:, :, DF:DF + FC], pZ[0][:, 0:E * FC].rearrange("p (e c) -> p e c", c=FC), ACT.Copy)\
                   .then_inc(b1_ready, 1)
                act_yT(act, 0, 0)
                act_yT(act, 0, 1)
                act_h(act, 0, 0)
                run(act, act_step)

            @block.vector
            def _(v):
                v.wait_ge(b1_ready, 1)
                vec_w1(v, 0, 0)
                vec_w1(v, 0, 1)
                vec_h(v, 0, 0)
                run(v, vec_step)


def finish(nc, A, K, out):
    PARTS = 8
    TP = NT // PARTS
    with ExitStack() as ctx:
        sb = lambda n, s, d=F32: ctx.enter_context(nc.sbuf_tensor(f"o_{n}", s, d))
        sem = lambda n: ctx.enter_context(nc.semaphore(f"o_{n}"))
        zg = sb("zg", [P, NT, P])
        zn, zm = sb("zn", [P, 2, TP, P]), sb("zm", [P, 2, TP, P])
        back = [sem(f"back{q}") for q in range(PARTS)]
        var_ready, std_ready, rstd_ready = sem("var"), sem("std"), sem("rstd")
        sum_done, bn_done, zn_ready, zm_ready, out_ready, stored = (
            sem(n) for n in ("sum_done", "bn_done", "zn_ready", "zm_ready", "out_ready", "stored"))
        over = lambda row: row.unsqueeze(1).to_broadcast([P, TP, P])
        part = lambda t, q: t[:, TP * q:TP * (q + 1), :]

        def vec_sum(v, q):
            v.wait_ge(back[q], 16)
            v.tensor_tensor(part(K.U, q), part(K.U, q), part(zg, q), ALU.add).then_inc(sum_done, 1)
            v.wait_ge(sum_done, q + 1)
            for n in range(TP * q, TP * (q + 1)):
                tile_stats(v, K, K.U, n, bn_done)
            v.wait_ge(bn_done, TP * (q + 1))
            finish_stats_vector(v, K, var_ready, std_ready, rstd_ready, q, PARTS)

        def act_normalise(act, q):
            finish_stats_scalar(act, K, var_ready, std_ready, rstd_ready, q, PARTS)
            wait(act, zm_ready, q - 1)
            for n in range(TP):
                m = TP * q + n
                act.activation(zn[:, q % 2, n, :], K.U[:, m, :], ACT.Identity, bias=K.nmr[:, m:m + 1],
                               scale=K.rstd[:, m:m + 1]).then_inc(zn_ready, 1)

        def pool_scale(pool, q):
            pool.wait_ge(zn_ready, TP * (q + 1))
            wait(pool, out_ready, q - 1)
            pool.tensor_tensor(zm[:, q % 2, :, :], zn[:, q % 2, :, :], over(K.gw[:, :]), ALU.mult).then_inc(zm_ready, 1)

        def vec_out(v, q):
            v.wait_ge(zm_ready, q + 1)
            v.tensor_tensor(part(K.X, q), part(K.X, q), zm[:, q % 2, :, :], ALU.add).then_inc(out_ready, 1)

        with nc.Block() as block:
            @block.gpsimd
            def _(pool):
                for q in range(PARTS):
                    pool_scale(pool, q)

            @block.vector
            def _(v):
                for q in range(PARTS + 2):
                    if q < PARTS:
                        vec_sum(v, q)
                    if q >= 2:
                        vec_out(v, q - 2)

            @block.scalar
            def _(act):
                for q in range(PARTS):
                    act_normalise(act, q)

            @block.sync
            def _(sp):
                rows = A["zs"][1:1 + B * T, :].rearrange("(n p) f -> p n f", p=P)
                for q in range(PARTS):
                    sp.dma_start(part(zg, q), part(rows, q)).then_inc(back[q], 16)
                xo = out.rearrange("b (n t) f -> t b n f", t=8)
                for q in range(PARTS):
                    sp.wait_ge(out_ready, q + 1)
                    for t in range(8):
                        sp.dma_start(xo[t][:, TP * q:TP * (q + 1), :], part(K.X, q)[16 * t:16 * t + 16, :, :])\
                          .then_inc(stored, 16)
                sp.wait_ge(stored, PARTS * 8 * 16)


def constants():
    import numpy as np
    k = {}
    i = np.arange(P)
    k["k_ident"] = np.eye(P, dtype=np.float32)
    k["k_utri"] = (i[:, None] <= i[None, :]).astype(np.float32)
    k["k_ustrict"] = (i[:, None] < i[None, :]).astype(np.float32)
    k["k_centre"] = (np.eye(P) - (i[:, None] // D == i[None, :] // D) / D).astype(np.float32)
    k["k_blk"] = np.repeat((i[:, None] // D == np.arange(H)[None, :]).astype(np.float32), 9, axis=1)
    inv = (np.float32(1.0) / np.float32(10000.0) ** (np.arange(0, D, 2, dtype=np.float32) / np.float32(D))).astype(np.float32)
    freqs = (np.arange(T, dtype=np.float32)[:, None] * inv[None, :]).astype(np.float32)
    emb = np.concatenate([freqs, freqs], axis=-1)
    cos, sin = np.cos(emb).astype(np.float64), np.sin(emb).astype(np.float64)
    sin[:, :D // 2] *= -1.0
    gam = 1.0 - 2.0 ** (-5.0 - np.arange(H))
    t = np.arange(T)[:, None, None]
    up = gam[None, :, None] ** t * D ** -0.5
    down = gam[None, :, None] ** (-t)
    for name, f in (("k_rope_c", cos), ("k_rope_s", sin)):
        q = (f[:, None, :] * up).reshape(T, P)
        kk = (f[:, None, :] * down).reshape(T, P)
        k[name] = np.concatenate([q, kk], axis=1).astype(np.float32)
    g = (i[:, None] % 32) // 16 != (np.arange(32)[None, :] // 16)
    k["k_smask"] = np.where(g, NEG, 0.0).astype(np.float32)
    k["k_tie"] = np.tile((E - np.arange(E, dtype=np.float32))[None, :], (P, 1))
    k["k_iota"] = np.tile(np.arange(P, dtype=np.float32)[None, :], (P, 1))
    k["k_spare"] = (1 + B * T + P * np.arange(SLOTS)[None, :] + i[:, None]).astype(np.float32)
    k["k_ids"] = (1 + P * np.arange(NT)[None, :] + i[:, None]).astype(np.float32)
    return k


_INS = ['L0_attn_x', 'L0_attn_w_attn', 'L0_attn_w_proj', 'L0_ffn_W_r', 'L0_ffn_W_k', 'L0_ffn_W_v', 'L0_ffn_mu_r',
        'L0_ffn_mu_k', 'L0_c', 'L0_wmod', 'L1_attn_Wq', 'L1_attn_Wk', 'L1_attn_Wv', 'L1_attn_Wg', 'L1_attn_Wo',
        'L1_attn_gn_w', 'L1_attn_gn_b', 'L1_ffn_Wqkv', 'L1_ffn_bqkv', 'L1_ffn_Wo', 'L1_ffn_bo', 'L1_ffn_g1',
        'L1_ffn_be1', 'L1_ffn_g2', 'L1_ffn_be2', 'L1_ffn_Wg', 'L1_ffn_W1', 'L1_ffn_b1', 'L1_ffn_W2', 'L1_ffn_b2',
        'L1_c', 'L1_wmod']


class Kept:
    pass


def build(nc, A, out):
    K = Kept()
    with ExitStack() as ctx:
        sb = lambda n, s, d=F32: ctx.enter_context(nc.sbuf_tensor(n, s, d))
        sem = lambda n: ctx.enter_context(nc.semaphore(n))
        K.X = sb("X", [P, NT, P])
        K.bn, K.diff, K.var, K.std = sb("bn", [P, NT, 6]), sb("diff", [P, NT]), sb("var", [P, NT]), sb("std", [P, NT])
        K.rstd, K.nmr, K.eps = sb("rstd", [P, NT]), sb("nmr", [P, NT]), sb("eps", [P, 1])
        K.ident, K.utri = sb("ident", [P, P]), sb("utri", [P, P])
        K.W = sb("W", [P, 11, P])
        K.wg8, K.cols, K.mod, K.tab = sb("wg8", [P, E]), sb("cols", [P, 7]), sb("mod", [P, 6, B]), sb("tab", [P, 3, P])
        K.bo, K.rows, K.smask = sb("bo", [P, P]), sb("rows", [P, 4, P]), sb("smask", [P, 32])
        K.w1, K.w2 = sb("w1", [P, E, DF + FC + P]), sb("w2", [P, E, FC, P])
        K.x_in = [sem(f"x_in{g}") for g in range(4)]
        with ExitStack() as early:
            sb2 = lambda n, s, d=F32: early.enter_context(nc.sbuf_tensor(n, s, d))
            K.wgate = sb2("wgate", [P, 3, B, P])
            K.wqkv0, K.wo1, K.cmat = sb2("wqkv0", [P, 3 * P]), sb2("wo1", [P, P]), sb2("cmat", [P, P])
            K.blk = sb2("blk", [P, H, 9])
            K.rope_c, K.rope_s = sb2("rope_c", [P, TPB, 2 * P]), sb2("rope_s", [P, TPB, 2 * P])
            prologue(nc, A, K)
            attention(nc, A, K, 0)
            token_shift_ffn(nc, A, K)
            attention(nc, A, K, 1)
        clear_semaphores(nc)
        K.U = sb("U", [P, NT, P])
        attend_batches(nc, A, K)
        clear_semaphores(nc)
        experts(nc, A, K, out)


def clear_semaphores(nc):
    released = sorted(nc.released_uncleared_semaphores)
    with nc.Block() as block:
        @block.gpsimd
        def _(pool):
            start = 0
            for i in range(1, len(released) + 1):
                if i == len(released) or released[i] != released[i - 1] + 1:
                    pool.sem_clear(range(released[start], released[i - 1] + 1))
                    start = i


def kernel(**inputs):
    import numpy as np
    import concourse.bacc as _bacc
    from concourse.bass_utils import run_bass_kernel_spmd as _run

    nc = _bacc.Bacc("TRN2", target_bir_lowering=False, num_devices=1)
    arrays, A = {}, {}
    for name in _INS:
        a = np.ascontiguousarray(inputs[name])
        arrays[f"in_{name}_dram"] = a
        A[name] = nc.dram_tensor(f"in_{name}_dram", a.shape, mybir.dt.from_np(a.dtype), kind="ExternalInput").ap()
    for name, a in constants().items():
        arrays[f"in_{name}_dram"] = a
        A[name] = nc.dram_tensor(f"in_{name}_dram", a.shape, mybir.dt.from_np(a.dtype), kind="ExternalInput").ap()
    A["xs"] = nc.dram_tensor("xs", (B * T, C), F32, kind="Internal").ap()
    A["ys"] = nc.dram_tensor("ys", (B * T + 1, C), F32, kind="Internal").ap()
    A["zs"] = nc.dram_tensor("zs", (B * T + 1 + SLOTS * P, C), F32, kind="Internal").ap()
    out = nc.dram_tensor("out_0_dram", (B, T, C), F32, kind="ExternalOutput").ap()
    build(nc, A, out)
    r = _run(nc, [arrays], core_ids=[0])
    return r.results[0]["out_0_dram"]
```
